# Optimizing a Trainium2 kernel written in Bass

```python
import numpy as np
import jax
import jax.numpy as jnp

def _softmax(x, axis=-1):
    return jax.nn.softmax(x, axis=axis)
def _gelu(x):
    return jax.nn.gelu(x, approximate=True)
def _silu(x):
    return jax.nn.silu(x)
def _sigmoid(x):
    return jax.nn.sigmoid(x)
def _layernorm(x, axis=-1, eps=1e-5):
    m = jnp.mean(x, axis=axis, keepdims=True)
    v = jnp.var(x, axis=axis, keepdims=True)
    return (x - m) / jnp.sqrt(v + eps)
def _scatter_add(tgt, idx, src, axis=0):
    return tgt.at[idx].add(src)
def _segment_sum(src, seg, n):
    return jax.ops.segment_sum(src, seg, n)

kernel_name = 'mk_vit_tower_d1_tok_img512_c6f067'

def setup_inputs(seed: int = 0):
    np.random.seed(seed)
    _w = jnp.asarray
    def _rec_inputs():
        import jax
        import jax.numpy as jnp
        _rk = jax.random.key(seed)
        x = (-0.000356955 + 1 * jax.random.normal(jax.random.fold_in(_rk, 1), (32, 3, 384, 384), jnp.float32))
        return x
    x = _rec_inputs()
    def _L0_tok_setup():
        import jax, jax.numpy as jnp
        import numpy as np
        key = jax.random.key(seed)
        k1, k2, k3 = jax.random.split(key, 3)
        B, C, H, W = (128, 3, 224, 224)
        E, p = (512, 16)
        K = C * p * p
        img = jax.random.normal(k1, (B, C, H, W), dtype=jnp.float32)
        w = jax.random.normal(k2, (E, K), dtype=jnp.float32) * (1.0 / np.sqrt(K))
        b = jax.random.normal(k3, (E,), dtype=jnp.float32)
        return {'img': img, 'w': w, 'b': b, 'patch_size': p}
    _L0_tok_all = _L0_tok_setup()
    _L0_tok_in = {k: v for k, v in _L0_tok_all.items() if k in ('w', 'b', )}
    del _L0_tok_all

    def _L0_attn_setup():
        import jax, jax.numpy as jnp
        import numpy as np
        N_HEAD = 8
        D_MODEL = 512
        D_HEAD = D_MODEL // N_HEAD
        QLEN = 2048
        BSZ = 4
        LN_EPS = 1e-05

        def _layer_norm(x, gamma, beta):
            mu = jnp.mean(x, axis=-1, keepdims=True)
            var = jnp.mean(jnp.square(x - mu), axis=-1, keepdims=True)
            return (x - mu) * jax.lax.rsqrt(var + LN_EPS) * gamma + beta

        def _pos_emb(qlen, d_model, dtype):
            pos_seq = jnp.arange(qlen - 1, -1, -1, dtype=dtype)
            inv_freq = 1.0 / 10000.0 ** (jnp.arange(0, d_model, 2, dtype=dtype) / d_model)
            sinusoid = pos_seq[:, None] * inv_freq[None, :]
            return jnp.concatenate([jnp.sin(sinusoid), jnp.cos(sinusoid)], axis=-1)

        def _rel_shift(x):
            q, r, b, n = x.shape
            x_padded = jnp.pad(x, ((0, 0), (1, 0), (0, 0), (0, 0)))
            x_padded = x_padded.reshape(r + 1, q, b, n)
            return x_padded[1:].reshape(q, r, b, n)
        key = jax.random.key(seed)
        ks = jax.random.split(key, 6)
        s = 0.02
        return {'w': jax.random.normal(ks[0], (QLEN, BSZ, D_MODEL), dtype=jnp.float32), 'Wqkv': jax.random.normal(ks[1], (3 * D_MODEL, D_MODEL), dtype=jnp.float32) * s, 'Wr': jax.random.normal(ks[2], (D_MODEL, D_MODEL), dtype=jnp.float32) * s, 'Wo': jax.random.normal(ks[3], (D_MODEL, D_MODEL), dtype=jnp.float32) * s, 'ln_gamma': jnp.ones((D_MODEL,), dtype=jnp.float32), 'ln_beta': jnp.zeros((D_MODEL,), dtype=jnp.float32), 'r_w_bias': jax.random.normal(ks[4], (N_HEAD, D_HEAD), dtype=jnp.float32) * s, 'r_r_bias': jax.random.normal(ks[5], (N_HEAD, D_HEAD), dtype=jnp.float32) * s}
    _L0_attn_all = _L0_attn_setup()
    _L0_attn_in = {k: v for k, v in _L0_attn_all.items() if k in ('Wqkv', 'Wr', 'Wo', 'ln_gamma', 'ln_beta', 'r_w_bias', 'r_r_bias', )}
    del _L0_attn_all

    def _L0_ffn_setup():
        import jax, jax.numpy as jnp
        import numpy as np
        CAPACITY_FACTOR = 1.2
        key = jax.random.key(seed)
        k1, k2, k3 = jax.random.split(key, 3)
        B, S, D, E = (8, 4096, 512, 16)
        x = jax.random.normal(k1, (B, S, D), dtype=jnp.float32)
        switch_w = jax.random.normal(k2, (E, D), dtype=jnp.float32) * 0.02
        switch_b = jnp.zeros((E,), dtype=jnp.float32)
        expert_w = jax.random.normal(k3, (E, D, D), dtype=jnp.float32) * 0.02
        expert_b = jnp.zeros((E, D), dtype=jnp.float32)
        return {'x': x, 'switch_w': switch_w, 'switch_b': switch_b, 'expert_w': expert_w, 'expert_b': expert_b}
    _L0_ffn_all = _L0_ffn_setup()
    _L0_ffn_in = {k: v for k, v in _L0_ffn_all.items() if k in ('switch_w', 'switch_b', 'expert_w', 'expert_b', )}
    del _L0_ffn_all

    return {
        "x": x,
        "L0_tok_w": _L0_tok_in["w"],
        "L0_tok_b": _L0_tok_in["b"],
        "L0_attn_Wqkv": _L0_attn_in["Wqkv"],
        "L0_attn_Wr": _L0_attn_in["Wr"],
        "L0_attn_Wo": _L0_attn_in["Wo"],
        "L0_attn_ln_gamma": _L0_attn_in["ln_gamma"],
        "L0_attn_ln_beta": _L0_attn_in["ln_beta"],
        "L0_attn_r_w_bias": _L0_attn_in["r_w_bias"],
        "L0_attn_r_r_bias": _L0_attn_in["r_r_bias"],
        "L0_ffn_switch_w": _L0_ffn_in["switch_w"],
        "L0_ffn_switch_b": _L0_ffn_in["switch_b"],
        "L0_ffn_expert_w": _L0_ffn_in["expert_w"],
        "L0_ffn_expert_b": _L0_ffn_in["expert_b"],
    }

def reference(x, L0_tok_w, L0_tok_b, L0_attn_Wqkv, L0_attn_Wr, L0_attn_Wo, L0_attn_ln_gamma, L0_attn_ln_beta, L0_attn_r_w_bias, L0_attn_r_r_bias, L0_ffn_switch_w, L0_ffn_switch_b, L0_ffn_expert_w, L0_ffn_expert_b):
    import jax
    import jax.numpy as jnp
    def _L0_tok_ref(img, w, b, patch_size):
        import jax, jax.numpy as jnp
        import numpy as np
        B, C, H, W = img.shape
        p = patch_size
        Hp, Wp = (H // p, W // p)
        S = Hp * Wp
        patches = img.reshape(B, C, Hp, p, Wp, p)
        patches = patches.transpose(0, 2, 4, 1, 3, 5).reshape(B, S, C * p * p)
        out = jnp.einsum('bsk,ek->bse', patches, w) + b
        return out

    def _L0_attn_ref(w, Wqkv, Wr, Wo, ln_gamma, ln_beta, r_w_bias, r_r_bias):
        import jax, jax.numpy as jnp
        import numpy as np
        N_HEAD = 8
        D_MODEL = 512
        D_HEAD = D_MODEL // N_HEAD
        QLEN = 2048
        BSZ = 4
        LN_EPS = 1e-05

        def _layer_norm(x, gamma, beta):
            mu = jnp.mean(x, axis=-1, keepdims=True)
            var = jnp.mean(jnp.square(x - mu), axis=-1, keepdims=True)
            return (x - mu) * jax.lax.rsqrt(var + LN_EPS) * gamma + beta

        def _pos_emb(qlen, d_model, dtype):
            pos_seq = jnp.arange(qlen - 1, -1, -1, dtype=dtype)
            inv_freq = 1.0 / 10000.0 ** (jnp.arange(0, d_model, 2, dtype=dtype) / d_model)
            sinusoid = pos_seq[:, None] * inv_freq[None, :]
            return jnp.concatenate([jnp.sin(sinusoid), jnp.cos(sinusoid)], axis=-1)

        def _rel_shift(x):
            q, r, b, n = x.shape
            x_padded = jnp.pad(x, ((0, 0), (1, 0), (0, 0), (0, 0)))
            x_padded = x_padded.reshape(r + 1, q, b, n)
            return x_padded[1:].reshape(q, r, b, n)
        qlen, bsz, d_model = w.shape
        scale = 1.0 / D_HEAD ** 0.5
        r = _pos_emb(qlen, d_model, w.dtype)
        wn = _layer_norm(w, ln_gamma, ln_beta)
        heads = jnp.einsum('ibd,ed->ibe', wn, Wqkv)
        q_h, k_h, v_h = jnp.split(heads, 3, axis=-1)
        q_h = q_h.reshape(qlen, bsz, N_HEAD, D_HEAD)
        k_h = k_h.reshape(qlen, bsz, N_HEAD, D_HEAD)
        v_h = v_h.reshape(qlen, bsz, N_HEAD, D_HEAD)
        r_k = jnp.einsum('rd,ed->re', r, Wr).reshape(qlen, N_HEAD, D_HEAD)
        AC = jnp.einsum('ibnd,jbnd->ijbn', q_h + r_w_bias, k_h)
        BD = _rel_shift(jnp.einsum('ibnd,jnd->ijbn', q_h + r_r_bias, r_k))
        attn_score = (AC + BD) * scale
        attn_prob = jax.nn.softmax(attn_score, axis=1)
        attn_vec = jnp.einsum('ijbn,jbnd->ibnd', attn_prob, v_h)
        attn_vec = attn_vec.reshape(qlen, bsz, N_HEAD * D_HEAD)
        attn_out = jnp.einsum('ibe,de->ibd', attn_vec, Wo)
        return w + attn_out

    def _L0_ffn_ref(x, switch_w, switch_b, expert_w, expert_b):
        import jax, jax.numpy as jnp
        import numpy as np
        CAPACITY_FACTOR = 1.2
        B, S, D = x.shape
        E = switch_w.shape[0]
        N = B * S
        xf = x.reshape(N, D)
        logits = xf @ switch_w.T + switch_b
        probs = jax.nn.softmax(logits, axis=-1)
        route_probs = jnp.max(probs, axis=-1)
        routes = jnp.argmax(probs, axis=-1)
        oh = jax.nn.one_hot(routes, E, dtype=jnp.int32)
        pos = jnp.take_along_axis(jnp.cumsum(oh, axis=0), routes[:, None], axis=1)[:, 0] - 1
        capacity = int(CAPACITY_FACTOR * N / E)
        keep = pos < capacity
        buf = jnp.zeros((E, capacity, D), dtype=xf.dtype).at[routes, pos].set(xf)
        y = jnp.einsum('ecd,efd->ecf', buf, expert_w) + expert_b[:, None, :]
        gathered = y[routes, jnp.minimum(pos, capacity - 1)]
        out = jnp.where(keep[:, None], gathered, xf) * route_probs[:, None]
        return out.reshape(B, S, D)

    h = _L0_tok_ref(x, L0_tok_w, L0_tok_b, 16)
    h = h + _L0_attn_ref(_layernorm(h, axis=-1), L0_attn_Wqkv, L0_attn_Wr, L0_attn_Wo, L0_attn_ln_gamma, L0_attn_ln_beta, L0_attn_r_w_bias, L0_attn_r_r_bias)
    h = h + _L0_ffn_ref(_layernorm(h, axis=-1), L0_ffn_switch_w, L0_ffn_switch_b, L0_ffn_expert_w, L0_ffn_expert_b)
    return h


_drawn_inputs = setup_inputs


def setup_inputs(seed=0):
    import zlib

    import numpy as np

    out = dict(_drawn_inputs(seed))
    spreads = {'L0_attn_ln_gamma': (1.0, 0.6),
     'L0_attn_ln_beta': (0.0, 0.8),
     'L0_ffn_switch_b': (0.0, 0.356),
     'L0_ffn_expert_b': (0.0, 2.0)}
    factors = {'L0_attn_Wr': 22.696,
     'L0_attn_r_w_bias': 64.0,
     'L0_attn_r_r_bias': 64.0,
     'L0_ffn_expert_w': 3.467}
    for name, (base, spread) in spreads.items():
        noise = np.random.default_rng([zlib.crc32(name.encode()), seed]).standard_normal(out[name].shape)
        drawn = base * np.exp(spread * noise) if base else spread * noise
        out[name] = jnp.asarray(drawn.astype(out[name].dtype))
    for name, factor in factors.items():
        out[name] = (out[name] * factor).astype(out[name].dtype)
    return out
```

```python
from contextlib import ExitStack

import numpy as np

import concourse.bass as bass
from concourse import mybir

P = 128
IMAGES, CHANNELS, SIDE, PATCH = 32, 3, 384, 16
POSITIONS = (SIDE // PATCH) ** 2
QUADS = P // IMAGES
TILES = POSITIONS // QUADS
TPG = 3
GROUPS = TILES // TPG
GTOK = TPG * P
D = 512
DC = D // P
KC = CHANNELS * PATCH * PATCH // P
HEADS, DH = 8, 64
PAIRS = HEADS // 2
BLOCKS = 2 * TPG * PAIRS
EXPERTS = 16
TOKENS = IMAGES * POSITIONS
CAPACITY = int(1.2 * TOKENS / EXPERTS)
TPE = -(-CAPACITY // P)
SLOT_TILES = EXPERTS * TPE
DUMP = TOKENS
XROW = D + 4
ROW = XROW + D
EPS = 1e-5
PADDED = IMAGES + 1
BLOCK_STRIDE = P * PADDED

F32, F32R, BF16, I32 = mybir.dt.float32, mybir.dt.float32r, mybir.dt.bfloat16, mybir.dt.int32
ALU, ACT, AX = mybir.AluOpType, mybir.ActivationFunctionType, mybir.AxisListType


def wait(eng, sem, value):
    if not isinstance(value, int) or value > 0:
        eng.wait_ge(sem, value)


def hold_until(eng, waits, passed):
    for sem, value in waits:
        if not isinstance(value, int) or value > 0:
            eng.wait_ge(sem, value)
            eng.sem_inc(passed, 1)


def prepare(nc, io, sb):
    ctx = ExitStack()
    with ctx:
        def buf(name, shape, dt=F32):
            return ctx.enter_context(nc.sbuf_tensor(name, shape, dt))

        def sem(name):
            return ctx.enter_context(nc.semaphore(name))

        tok_raw = buf("tok_raw", [P, KC, D])
        qkv_raw = buf("qkv_raw", [P, DC, 3 * D])
        qkv_scaled = buf("qkv_scaled", [P, DC, 3 * D])
        out_raw = buf("out_raw", [P, DC, D])
        wr_raw = buf("wr_raw", [P, DC, D])
        sinusoid = buf("sinusoid", [P, DC, IMAGES])
        gamma = buf("gamma", [P, DC])
        beta = buf("beta", [P, DC])
        w_bias = buf("w_bias", [P, PAIRS])
        r_bias = buf("r_bias", [P, PAIRS])
        bias_gap = buf("bias_gap", [P, PAIRS])
        gap_cols = buf("gap_cols", [P, PAIRS, P])
        zeros = buf("zeros", [P, ROW])
        proj_ps = ctx.enter_context(nc.psum_tensor("proj_ps", [P, 2, D], F32))
        gap_ps = ctx.enter_context(nc.psum_tensor("gap_ps", [P, 2, D], F32))
        tok_in, qkv_in, out_in, small_in, wr_in = (sem(f"{n}_in") for n in ("tok", "qkv", "out", "small", "wr"))
        zeros_set, zeros_out, scaled, his, los = (sem(n) for n in ("zeros_set", "zeros_out", "scaled", "his", "los"))
        projected, rk_ready, gap_ready, gap_mm, prep_done, pt_zero = (
            sem(n) for n in ("projected", "rk_ready", "gap_ready", "gap_mm", "prep_done", "pt_zero"))
        block = ctx.enter_context(nc.Block())

        @block.sync
        def _(sp):
            sp.dma_start(tok_raw[:], io["tok_wT"]).then_inc(tok_in, 16)
            sp.dma_start(qkv_raw[:], io["qkv_wT"]).then_inc(qkv_in, 16)
            sp.dma_start(out_raw[:], io["out_wT"]).then_inc(out_in, 16)
            sp.dma_start(wr_raw[:], io["wr_wT"]).then_inc(wr_in, 16)
            sp.wait_ge(zeros_set, 1)
            sp.dma_start(io["shift"].rearrange("(p n) -> p n", p=P),
                         zeros[:, 0:BLOCKS * BLOCK_STRIDE // P]).then_inc(zeros_out, 16)
            sp.dma_start(io["rows"][DUMP:DUMP + P, :], zeros[:]).then_inc(zeros_out, 16)
            sp.wait_ge(zeros_out, 32)

        @block.scalar
        def _(act):
            for dst, src in ((gamma, "gamma"), (beta, "beta"), (w_bias, "r_w_bias"), (r_bias, "r_r_bias"),
                             (sinusoid, "sinusoid"), (sb["ident"], "ident"), (sb["tok_b"], "tok_b"),
                             (sb["gate_wT"], "gate_wT"), (sb["gate_b"], "gate_b"), (sb["expert_ids"], "expert_ids")):
                act.dma_start(dst[:], io[src]).then_inc(small_in, 16)
            act.wait_ge(tok_in, 16)
            for c in range(KC):
                act.activation(sb["tok_hi"][:, c, :], tok_raw[:, c, :], ACT.Copy).then_inc(his, 1)
            for c in range(DC):
                act.wait_ge(scaled, c + 1)
                act.activation(sb["qkv_hi"][:, c, :], qkv_scaled[:, c, :], ACT.Copy).then_inc(his, 1)
            act.wait_ge(out_in, 16)
            for c in range(DC):
                act.activation(sb["out_hi"][:, c, :], out_raw[:, c, :], ACT.Copy).then_inc(his, 1)

        @block.vector
        def _(dve):
            dve.memset(zeros[:], 0.0).then_inc(zeros_set, 1)
            dve.wait_ge(small_in, 160)
            dve.tensor_sub(bias_gap[:], r_bias[:], w_bias[:]).then_inc(prep_done, 1)
            dve.wait_ge(prep_done, 1)
            dve.tensor_copy(gap_cols[:], bias_gap[:].unsqueeze(2).broadcast_to([P, PAIRS, P])).then_inc(gap_ready, 1)
            for c in range(KC):
                dve.wait_ge(his, c + 1)
                dve.tensor_sub(sb["tok_lo"][:, c, :], tok_raw[:, c, :], sb["tok_hi"][:, c, :].bitcast(F32)).then_inc(los, 1)
            dve.wait_ge(projected, 2)
            dve.tensor_copy(sb["rk"][:], proj_ps[:, 1, 0:DC * IMAGES].rearrange("p (c r) -> p c r", c=DC)).then_inc(rk_ready, 1)
            dve.tensor_add(sb["qkv_b"][:, 0:DC], proj_ps[:, 0, 0:DC], w_bias[:]).then_inc(prep_done, 1)
            dve.tensor_copy(sb["qkv_b"][:, DC:3 * DC], proj_ps[:, 0, DC:3 * DC]).then_inc(prep_done, 1)
            dve.wait_ge(gap_mm, 1)
            dve.tensor_copy(sb["bd_const"][:], gap_ps[:, :, 0:PAIRS * IMAGES].rearrange("p a (c r) -> p a c r", c=PAIRS)).then_inc(prep_done, 1)
            for c in range(DC):
                dve.wait_ge(his, KC + c + 1)
                dve.tensor_sub(sb["qkv_lo"][:, c, :], qkv_scaled[:, c, :], sb["qkv_hi"][:, c, :].bitcast(F32)).then_inc(los, 1)
            for c in range(DC):
                dve.wait_ge(his, KC + DC + c + 1)
                dve.tensor_sub(sb["out_lo"][:, c, :], out_raw[:, c, :], sb["out_hi"][:, c, :].bitcast(F32)).then_inc(los, 1)

        @block.gpsimd
        def _(pool):
            pool.memset(sb["half"][:], -0.5).then_inc(pt_zero, 1)
            pool.memset(sb["probsT"][:], 0.0).then_inc(pt_zero, 1)
            pool.wait_ge(qkv_in, 16)
            pool.wait_ge(small_in, 160)
            for c in range(DC):
                pool.tensor_scalar(qkv_scaled[:, c, :], qkv_raw[:, c, :], gamma[:, c:c + 1], None, ALU.mult).then_inc(scaled, 1)

        @block.tensor
        def _(pe):
            pe.wait_ge(small_in, 160)
            pe.wait_ge(qkv_in, 16)
            for e in range(3 * DC):
                for c in range(DC):
                    last = pe.matmul(proj_ps[:, 0, e:e + 1], qkv_raw[:, c, e * P:(e + 1) * P], beta[:, c:c + 1],
                                     start=c == 0, stop=c == DC - 1)
            last.then_inc(projected, 1)
            pe.wait_ge(wr_in, 16)
            for e in range(DC):
                for c in range(DC):
                    last = pe.matmul(proj_ps[:, 1, e * IMAGES:(e + 1) * IMAGES], wr_raw[:, c, e * P:(e + 1) * P],
                                     sinusoid[:, c, :], start=c == 0, stop=c == DC - 1)
            last.then_inc(projected, 1)
            pe.wait_ge(gap_ready, 1)
            pe.wait_ge(rk_ready, 1)
            for par in range(2):
                rows = slice(par * DH, (par + 1) * DH)
                for n in range(PAIRS):
                    last = pe.matmul(gap_ps[:, par, n * IMAGES:(n + 1) * IMAGES], gap_cols[rows, n, :],
                                     sb["rk"][rows, n, :], start=True, stop=True)
            last.then_inc(gap_mm, 1)


def tower(nc, io, sb):
    ctx = ExitStack()
    with ctx:
        def buf(name, shape, dt=F32):
            return ctx.enter_context(nc.sbuf_tensor(name, shape, dt))

        def sem(name):
            return ctx.enter_context(nc.semaphore(name))

        x_raw = buf("x_raw", [P, TPG, KC * P])
        x_hi = buf("x_hi", [P, TPG, KC * P], F32R)
        x_lo = buf("x_lo", [P, TPG, KC * P], F32R)
        h = buf("h", [P, TPG, D])
        normed = buf("normed", [P, TPG * D])
        u = normed[:, :].rearrange("p (t d) -> p t d", t=TPG)
        xfT = normed[:, :].rearrange("p (c n) -> p c n", c=DC)
        resid = buf("resid", [P, TPG, D])
        xf = buf("xf", [P, TPG, XROW])
        wT_hi = buf("wT_hi", [P, DC, GTOK], F32R)
        wT_lo = buf("wT_lo", [P, DC, GTOK], F32R)
        qT = buf("qT", [P, PAIRS, GTOK])
        kT = buf("kT", [P, PAIRS, GTOK])
        v = buf("v", [P, TPG, D])
        bd = buf("bd", [P, 2, TPG, PAIRS, IMAGES])
        scores = buf("scores", [P, BLOCKS, IMAGES])
        scores5 = scores[:, :, :].rearrange("p (a t n) j -> p a (t n j)", a=2, t=TPG)
        row_max = buf("row_max", [P, BLOCKS])
        row_sum = buf("row_sum", [P, BLOCKS])
        row_inv = buf("row_inv", [P, BLOCKS])
        probsT = sb["probsT"]
        attnT_hi = buf("attnT_hi", [P, DC, GTOK], F32R)
        attnT_lo = buf("attnT_lo", [P, DC, GTOK], F32R)
        stats = buf("stats", [P, TPG, 6])
        mv = buf("mv", [P, TPG, 2])
        stats2 = buf("stats2", [P, TPG, 6])
        mv2 = buf("mv2", [P, TPG, 2])
        work = buf("work", [P, 8, TPG])
        coef = buf("coef", [P, 4, TPG])
        coef2 = buf("coef2", [P, 2, TPG])
        work2 = buf("work2", [P, 2, TPG])
        logits = buf("logits", [P, TPG, EXPERTS])
        gate_exp = buf("gate_exp", [P, TPG, EXPERTS])
        cand = buf("cand", [P, TPG, EXPERTS])
        gate_max = buf("gate_max", [P, TPG])
        gate_sum = buf("gate_sum", [P, TPG])
        wide_ps = ctx.enter_context(nc.psum_tensor("wide_ps", [P, 2, D], F32))
        turn_ps = ctx.enter_context(nc.psum_tensor("turn_ps", [P, 2, D], F32))
        ac_ps = ctx.enter_context(nc.psum_tensor("ac_ps", [P, 2, D], F32))
        bd_ps = ctx.enter_context(nc.psum_tensor("bd_ps", [P, 2, D], F32))

        x_loaded = [sem(f"x_loaded{t}") for t in range(TPG)]
        names = """x_his x_los tok_mm h_ready stats_ready coef_work coef_ready u_ready resid_ready uT_mm w_his w_los
            qk_mm qk_ready bd_mm bd_ready bd_stored bd_shifted v_mm v_ready ac_mm sum_ready max_ready centred exped
            rowsum_ready inv_ready probs_ready probsT_ready pv_mm attn_his attn_los out_mm h2_ready stats2_ready
            coef2_work coef2_ready xf_ready xf_stored xfT_mm xfT_ready gate_mm logits_read gate_maxed gate_centred
            gate_exped gate_summed gate_p cand_a cand_b outd_ready outd_stored""".split()
        s = {n: sem(n) for n in names}
        pe_passed, dve_passed, pool_passed, sp_passed = (sem(f"{n}_passed") for n in ("pe", "dve", "pool", "sp"))
        block = ctx.enter_context(nc.Block())
        ident = sb["ident"]

        @block.tensor
        def _(pe):
            def three(out, a_hi, a_lo, b_hi, b_lo, first, last):
                pe.matmul(out, a_hi, b_hi, start=first, stop=False)
                pe.matmul(out, a_hi, b_lo, start=False, stop=False)
                return pe.matmul(out, a_lo, b_hi, start=False, stop=last)

            def tokenize(g, first):
                for t in range(TPG):
                    pe.wait_ge(s["x_los"], TPG * g + t + 1)
                    if t == 2:
                        pe.wait_ge(s["h_ready"], TPG * g + 1)
                    elif not first:
                        pe.wait_ge(s["v_ready"], TPG * g + t - 1)
                    for c in range(KC):
                        cols = slice(c * P, (c + 1) * P)
                        last = three(wide_ps[:, (t + 1) % 2, :], x_hi[:, t, cols], x_lo[:, t, cols],
                                     sb["tok_hi"][:, c, :], sb["tok_lo"][:, c, :], c == 0, c == KC - 1)
                    last.then_inc(s["tok_mm"], 1)

            def turn_u(g, first):
                for c in range(DC):
                    if c == 0:
                        pe.wait_ge(s["u_ready"], TPG * g + TPG)
                    if c >= 2:
                        pe.wait_ge(s["w_los"], DC * g + c - 1)
                    elif not first:
                        pe.wait_ge(s["attn_los"], DC * g + c - 1)
                    for t in range(TPG):
                        last = pe.transpose(turn_ps[:, c % 2, t * P:(t + 1) * P], u[:, t, c * P:(c + 1) * P], ident[:])
                    last.then_inc(s["uT_mm"], 1)

            def queries_keys(g):
                pe.wait_ge(s["w_los"], DC * g + DC)
                for e in range(2 * DC):
                    if e >= 2:
                        pe.wait_ge(s["qk_ready"], 2 * DC * g + e - 1)
                    for c in range(DC):
                        cols = slice(e * P, (e + 1) * P)
                        last = three(turn_ps[:, e % 2, 0:GTOK], sb["qkv_hi"][:, c, cols], sb["qkv_lo"][:, c, cols],
                                     wT_hi[:, c, :], wT_lo[:, c, :], c == 0, c == DC - 1)
                    last.then_inc(s["qk_mm"], 1)

            def gate(g, last_group):
                for c in range(DC):
                    if c == 0:
                        pe.wait_ge(s["xf_ready"], TPG * g + TPG)
                    if c >= 2:
                        pe.wait_ge(s["xfT_ready"], DC * g + c - 1)
                    elif last_group:
                        pe.wait_ge(s["attn_los"], DC * g + c + 3)
                    else:
                        pe.wait_ge(s["qk_ready"], 2 * DC * g + 2 * DC + c + 7)
                    for t in range(TPG):
                        last = pe.transpose(turn_ps[:, c % 2, t * P:(t + 1) * P], xf[:, t, c * P:(c + 1) * P], ident[:])
                    last.then_inc(s["xfT_mm"], 1)
                pe.wait_ge(s["xfT_ready"], DC * g + DC)
                pe.wait_ge(s["h2_ready"], TPG * g + TPG)
                for t in range(TPG):
                    for c in range(DC):
                        last = pe.matmul(wide_ps[:, 1, t * EXPERTS:(t + 1) * EXPERTS], xfT[:, c, t * P:(t + 1) * P],
                                         sb["gate_wT"][:, c, :], start=c == 0, stop=c == DC - 1)
                last.then_inc(s["gate_mm"], 1)

            def position_scores(g):
                pe.wait_ge(s["qk_ready"], 2 * DC * g + DC)
                wait(pe, s["bd_ready"], g)
                for par in range(2):
                    rows = slice(par * DH, (par + 1) * DH)
                    for t in range(TPG):
                        for n in range(PAIRS):
                            at = (t * PAIRS + n) * IMAGES
                            last = pe.matmul(bd_ps[:, par, at:at + IMAGES], qT[rows, n, t * P:(t + 1) * P],
                                             sb["rk"][rows, n, :], start=True, stop=True)
                last.then_inc(s["bd_mm"], 1)

            def values(g):
                for t in range(TPG):
                    if t == 0:
                        wait(pe, s["h2_ready"], TPG * g)
                    elif t == 1:
                        wait(pe, s["logits_read"], g)
                    else:
                        pe.wait_ge(s["v_ready"], TPG * g + 1)
                    for c in range(DC):
                        cols = slice(t * P, (t + 1) * P)
                        last = three(wide_ps[:, t % 2, :], wT_hi[:, c, cols], wT_lo[:, c, cols],
                                     sb["qkv_hi"][:, c, 2 * D:], sb["qkv_lo"][:, c, 2 * D:], c == 0, c == DC - 1)
                    last.then_inc(s["v_mm"], 1)

            def content_scores(g):
                hold_until(pe, [(s["qk_ready"], 2 * DC * g + 2 * DC), (s["sum_ready"], g)], pe_passed)
                for par in range(2):
                    rows = slice(par * DH, (par + 1) * DH)
                    for t in range(TPG):
                        for n in range(PAIRS):
                            at = (t * PAIRS + n) * IMAGES
                            for q in range(QUADS):
                                toks = slice(t * P + q * IMAGES, t * P + (q + 1) * IMAGES)
                                last = pe.matmul(ac_ps[q * IMAGES:(q + 1) * IMAGES, par, at:at + IMAGES],
                                                 qT[rows, n, toks], kT[rows, n, toks], start=True, stop=True)
                last.then_inc(s["ac_mm"], 1)

            def attend(g, first):
                pe.wait_ge(s["v_ready"], TPG * g + TPG)
                pe.wait_ge(s["probsT_ready"], QUADS * g + QUADS)
                for c in range(DC):
                    if c >= 2:
                        pe.wait_ge(s["attn_los"], DC * g + c - 1)
                    elif first:
                        pe.wait_ge(s["qk_ready"], 2 * DC * g + c + 7)
                    else:
                        pe.wait_ge(s["xfT_ready"], DC * g + c - 1)
                    for par in range(2):
                        head = 2 * c + par
                        for t in range(TPG):
                            blk = (par * TPG + t) * PAIRS + c
                            last = pe.matmul(turn_ps[par * DH:(par + 1) * DH, c % 2, t * P:(t + 1) * P],
                                             v[:, t, head * DH:(head + 1) * DH], probsT[:, blk, :], start=True, stop=True)
                    last.then_inc(s["pv_mm"], 1)

            def project(g, last_group):
                pe.wait_ge(s["attn_los"], DC * g + DC)
                for t in range(TPG):
                    if t == 2:
                        pe.wait_ge(s["h2_ready"], TPG * g + 1)
                    elif last_group:
                        pe.wait_ge(s["v_ready"], TPG * g + TPG)
                    else:
                        pe.wait_ge(s["h_ready"], TPG * g + TPG + t + 2)
                    for c in range(DC):
                        cols = slice(t * P, (t + 1) * P)
                        last = three(wide_ps[:, t % 2, :], attnT_hi[:, c, cols], attnT_lo[:, c, cols],
                                     sb["out_hi"][:, c, :], sb["out_lo"][:, c, :], c == 0, c == DC - 1)
                    last.then_inc(s["out_mm"], 1)

            def step(i, first, last):
                queries_keys(i)
                if not first:
                    gate(i - 1, False)
                position_scores(i)
                values(i)
                content_scores(i)
                if not last:
                    tokenize(i + 1, False)
                attend(i, first)
                if not last:
                    turn_u(i + 1, False)
                project(i, last)

            tokenize(0, True)
            turn_u(0, True)
            step(0, True, False)
            with pe.Fori(1, GROUPS - 1) as i:
                step(i, False, False)
            step(GROUPS - 1, False, True)
            gate(GROUPS - 1, True)

        @block.scalar
        def _(act):
            def patches_hi(g, t):
                act.wait_ge(x_loaded[t], 16 * g + 16)
                wait(act, s["tok_mm"], TPG * g - TPG + t + 1)
                act.activation(x_hi[:, t, :], x_raw[:, t, :], ACT.Copy).then_inc(s["x_his"], 1)

            def scale_u(g, first):
                act.wait_ge(s["coef_ready"], g + 1)
                if not first:
                    wait(act, s["gate_mm"], g - 1)
                for t in range(TPG):
                    act.activation(u[:, t, :], h[:, t, :], ACT.Identity, bias=coef[:, 3, t:t + 1],
                                   scale=coef[:, 2, t:t + 1]).then_inc(s["u_ready"], 1)

            def activations_hi(g):
                for c in range(DC):
                    act.wait_ge(s["uT_mm"], DC * g + c + 1)
                    act.activation(wT_hi[:, c, :], turn_ps[:, c % 2, 0:GTOK], ACT.Copy).then_inc(s["w_his"], 1)

            def query_key(g, e):
                act.wait_ge(s["qk_mm"], 2 * DC * g + e + 1)
                act.activation((qT if e < DC else kT)[:, e % DC, :], turn_ps[:, e % 2, 0:GTOK], ACT.Identity,
                               bias=sb["qkv_b"][:, e:e + 1]).then_inc(s["qk_ready"], 1)

            def normalise(g, t):
                if t == 0:
                    act.wait_ge(s["coef2_ready"], g + 1)
                    wait(act, s["xf_stored"], 16 * g)
                    wait(act, s["outd_ready"], TPG * g)
                act.activation(xf[:, t, 0:D], resid[:, t, :], ACT.Identity, bias=coef2[:, 1, t:t + 1],
                               scale=coef2[:, 0, t:t + 1]).then_inc(s["xf_ready"], 1)

            def xf_turned(g):
                for c in range(DC):
                    act.wait_ge(s["xfT_mm"], DC * g + c + 1)
                    act.activation(xfT[:, c, :], turn_ps[:, c % 2, 0:GTOK], ACT.Copy).then_inc(s["xfT_ready"], 1)
                act.wait_ge(s["gate_centred"], g + 1)
                act.activation(gate_exp[:], logits[:], ACT.Exp).then_inc(s["gate_exped"], 1)

            def values(g):
                for t in range(TPG):
                    act.wait_ge(s["v_mm"], TPG * g + t + 1)
                    act.activation(v[:, t, :], wide_ps[:, t % 2, :], ACT.Copy).then_inc(s["v_ready"], 1)

            def exponentials(g):
                act.wait_ge(s["centred"], g + 1)
                act.activation(scores[:], scores[:], ACT.Exp, scale=DH ** -0.5).then_inc(s["exped"], 1)

            def attention_hi(g, c):
                act.wait_ge(s["pv_mm"], DC * g + c + 1)
                act.activation(attnT_hi[:, c, :], turn_ps[:, c % 2, 0:GTOK], ACT.Identity,
                               bias=sb["qkv_b"][:, 2 * DC + c:2 * DC + c + 1]).then_inc(s["attn_his"], 1)

            def step(i, first, last):
                for e in range(DC):
                    query_key(i, e)
                    if not first and e < TPG:
                        normalise(i - 1, e)
                for e in range(DC, 2 * DC):
                    if not last and e < DC + TPG:
                        patches_hi(i + 1, e - DC)
                    query_key(i, e)
                if not first:
                    xf_turned(i - 1)
                values(i)
                exponentials(i)
                attention_hi(i, 0)
                attention_hi(i, 1)
                if not last:
                    scale_u(i + 1, False)
                attention_hi(i, 2)
                attention_hi(i, 3)
                if not last:
                    activations_hi(i + 1)

            for t in range(TPG):
                patches_hi(0, t)
            scale_u(0, True)
            activations_hi(0)
            step(0, True, False)
            with act.Fori(1, GROUPS - 1) as i:
                step(i, False, False)
            step(GROUPS - 1, False, True)
            for t in range(TPG):
                normalise(GROUPS - 1, t)
            xf_turned(GROUPS - 1)

        @block.vector
        def _(dve):
            def patches_lo(g, t):
                dve.wait_ge(s["x_his"], TPG * g + t + 1)
                dve.tensor_sub(x_lo[:, t, :], x_raw[:, t, :], x_hi[:, t, :].bitcast(F32)).then_inc(s["x_los"], 1)

            def tokens(g, t):
                dve.wait_ge(s["tok_mm"], TPG * g + t + 1)
                if t == 0:
                    wait(dve, s["u_ready"], TPG * g)
                    wait(dve, s["resid_ready"], TPG * g)
                dve.tensor_add(h[:, t, :], wide_ps[:, (t + 1) % 2, :], sb["tok_b"][:]).then_inc(s["h_ready"], 1)
                dve.wait_ge(s["h_ready"], TPG * g + t + 1)
                dve.bn_stats(stats[:, t, :], h[:, t, :]).then_inc(s["stats_ready"], 1)
                if t == TPG - 1:
                    hold_until(dve, [(s["stats_ready"], 2 * TPG * g + TPG)], dve_passed)
                    for k in range(TPG):
                        dve.bn_aggr(mv[:, k, :], stats[:, k, :]).then_inc(s["stats_ready"], 1)

            def activations_lo(g):
                for c in range(DC):
                    dve.wait_ge(s["w_his"], DC * g + c + 1)
                    dve.tensor_sub(wT_lo[:, c, :], turn_ps[:, c % 2, 0:GTOK], wT_hi[:, c, :].bitcast(F32)).then_inc(s["w_los"], 1)

            def gate_logits(g):
                dve.wait_ge(s["gate_mm"], g + 1)
                dve.tensor_add(logits[:], wide_ps[:, 1, 0:TPG * EXPERTS].rearrange("p (t e) -> p t e", t=TPG),
                               sb["gate_b"][:].unsqueeze(1).broadcast_to([P, TPG, EXPERTS])).then_inc(s["logits_read"], 1)
                dve.wait_ge(s["logits_read"], g + 1)
                dve.reduce_max(gate_max[:], logits[:], AX.X).then_inc(s["gate_maxed"], 1)
                dve.wait_ge(s["gate_maxed"], g + 1)
                dve.tensor_sub(logits[:], logits[:], gate_max[:].unsqueeze(2).broadcast_to([P, TPG, EXPERTS])).then_inc(s["gate_centred"], 1)

            def gate_choice(g):
                dve.wait_ge(s["gate_centred"], g + 1)
                dve.tensor_scalar(cand[:], logits[:], 0.0, float(EXPERTS), ALU.is_lt, ALU.mult).then_inc(s["cand_a"], 1)
                dve.wait_ge(s["cand_a"], g + 1)
                dve.tensor_add(cand[:], cand[:], sb["expert_ids"][:].unsqueeze(1).broadcast_to([P, TPG, EXPERTS])).then_inc(s["cand_b"], 1)
                dve.wait_ge(s["gate_exped"], g + 1)
                dve.reduce_sum(gate_sum[:], gate_exp[:], AX.X).then_inc(s["gate_summed"], 1)
                dve.wait_ge(s["cand_b"], g + 1)
                dve.tensor_reduce(sb["route"][:, bass.ds(TPG * g, TPG)], cand[:], axis=AX.X, op=ALU.min)
                dve.wait_ge(s["gate_summed"], g + 1)
                dve.reciprocal(xf[:, :, D:XROW], gate_sum[:].unsqueeze(2).broadcast_to([P, TPG, XROW - D])).then_inc(s["gate_p"], 1)
                dve.wait_ge(s["gate_p"], g + 1)
                for t in range(TPG):
                    dve.scalar_tensor_tensor(out=resid[:, t, :], in0=xf[:, t, 0:D], scalar=xf[:, t, D:D + 1],
                                             in1=resid[:, t, :], op0=ALU.mult, op1=ALU.add).then_inc(s["outd_ready"], 1)

            def position_scores(g):
                dve.wait_ge(s["bd_mm"], g + 1)
                wait(dve, s["bd_stored"], 16 * g)
                for par in range(2):
                    ins = dve.tensor_add(bd[:, par, :, :, :].rearrange("p t n r -> p t (n r)"),
                                         bd_ps[:, par, 0:GTOK].rearrange("p (t m) -> p t m", t=TPG),
                                         sb["bd_const"][:, par, :, :].rearrange("p n r -> p (n r)").unsqueeze(1)
                                         .broadcast_to([P, TPG, PAIRS * IMAGES]))
                ins.then_inc(s["bd_ready"], 1)

            def scores_max(g):
                dve.wait_ge(s["ac_mm"], g + 1)
                dve.wait_ge(s["bd_shifted"], 16 * QUADS * g + 16 * QUADS)
                dve.tensor_add(scores5, ac_ps[:, :, 0:GTOK], scores5).then_inc(s["sum_ready"], 1)
                dve.wait_ge(s["sum_ready"], g + 1)
                dve.reduce_max(row_max[:], scores[:], AX.X).then_inc(s["max_ready"], 1)

            def scores_sum(g):
                dve.wait_ge(s["exped"], g + 1)
                dve.reduce_sum(row_sum[:], scores[:], AX.X).then_inc(s["rowsum_ready"], 1)
                dve.wait_ge(s["rowsum_ready"], g + 1)
                dve.reciprocal(row_inv[:], row_sum[:]).then_inc(s["inv_ready"], 1)

            def turn_probs(g):
                dve.wait_ge(s["probs_ready"], g + 1)
                wait(dve, s["pv_mm"], DC * g)
                for q in range(QUADS):
                    rows = slice(q * IMAGES, (q + 1) * IMAGES)
                    dve.transpose(probsT[rows, :, rows], scores[rows, :, :]).then_inc(s["probsT_ready"], 1)

            def attention_lo(g):
                for c in range(DC):
                    dve.wait_ge(s["attn_his"], DC * g + c + 1)
                    dve.scalar_tensor_tensor(out=attnT_lo[:, c, :], in0=turn_ps[:, c % 2, 0:GTOK],
                                             scalar=sb["qkv_b"][:, 2 * DC + c:2 * DC + c + 1],
                                             in1=attnT_hi[:, c, :].bitcast(F32), op0=ALU.add, op1=ALU.subtract
                                             ).then_inc(s["attn_los"], 1)

            def residual(g):
                for t in range(TPG):
                    dve.wait_ge(s["out_mm"], TPG * g + t + 1)
                    if t == 0:
                        dve.wait_ge(s["resid_ready"], TPG * g + TPG)
                    dve.tensor_add(resid[:, t, :], wide_ps[:, t % 2, :], resid[:, t, :]).then_inc(s["h2_ready"], 1)
                    dve.wait_ge(s["h2_ready"], TPG * g + t + 1)
                    dve.bn_stats(stats2[:, t, :], resid[:, t, :]).then_inc(s["stats2_ready"], 1)
                hold_until(dve, [(s["stats2_ready"], 2 * TPG * g + TPG)], dve_passed)
                for t in range(TPG):
                    dve.bn_aggr(mv2[:, t, :], stats2[:, t, :]).then_inc(s["stats2_ready"], 1)

            def step(i, first, last):
                if not last:
                    for t in range(TPG):
                        patches_lo(i + 1, t)
                if not first:
                    gate_logits(i - 1)
                position_scores(i)
                if not first:
                    gate_choice(i - 1)
                scores_max(i)
                if not last:
                    tokens(i + 1, 0)
                scores_sum(i)
                if not last:
                    tokens(i + 1, 1)
                turn_probs(i)
                if not last:
                    tokens(i + 1, 2)
                attention_lo(i)
                if not last:
                    activations_lo(i + 1)
                residual(i)

            for t in range(TPG):
                patches_lo(0, t)
            for t in range(TPG):
                tokens(0, t)
            activations_lo(0)
            step(0, True, False)
            with dve.Fori(1, GROUPS - 1) as i:
                step(i, False, False)
            step(GROUPS - 1, False, True)
            gate_logits(GROUPS - 1)
            gate_choice(GROUPS - 1)

        @block.gpsimd
        def _(pool):
            def coefficients(g):
                var, mean = mv[:, :, 1], mv[:, :, 0]
                steps = [
                    lambda: pool.tensor_scalar(work[:, 0, :], var, EPS, None, ALU.add),
                    lambda: pool.tensor_tensor(work[:, 1, :], work[:, 0, :], sb["half"][:], ALU.pow),
                    lambda: pool.tensor_tensor(work[:, 2, :], var, work[:, 1, :], ALU.mult),
                    lambda: pool.tensor_tensor(work[:, 3, :], work[:, 2, :], work[:, 1, :], ALU.mult),
                    lambda: pool.tensor_scalar(work[:, 4, :], work[:, 3, :], EPS, None, ALU.add),
                    lambda: pool.tensor_tensor(work[:, 5, :], work[:, 4, :], sb["half"][:], ALU.pow),
                    lambda: pool.tensor_tensor(coef[:, 2, :], work[:, 1, :], work[:, 5, :], ALU.mult),
                    lambda: pool.tensor_scalar(work[:, 6, :], mean, -1.0, None, ALU.mult),
                    lambda: pool.tensor_tensor(coef[:, 3, :], work[:, 6, :], coef[:, 2, :], ALU.mult),
                    lambda: pool.tensor_tensor(coef[:, 1, :], work[:, 6, :], work[:, 1, :], ALU.mult),
                ]
                hold_until(pool, [(s["stats_ready"], 2 * TPG * g + 2 * TPG)], pool_passed)
                for n, op in enumerate(steps):
                    if n:
                        hold_until(pool, [(s["coef_work"], len(steps) * g + n)], pool_passed)
                    op().then_inc(s["coef_work"], 1)
                pool.tensor_scalar(coef[:, 0, :], work[:, 1, :], 1.0, None, ALU.add).then_inc(s["coef_ready"], 1)

            def coefficients2(g):
                hold_until(pool, [(s["stats2_ready"], 2 * TPG * g + 2 * TPG)], pool_passed)
                pool.tensor_scalar(work2[:, 0, :], mv2[:, :, 1], EPS, None, ALU.add).then_inc(s["coef2_work"], 1)
                pool.tensor_scalar(work2[:, 1, :], mv2[:, :, 0], -1.0, None, ALU.mult).then_inc(s["coef2_work"], 1)
                pool.wait_ge(s["coef2_work"], 3 * g + 2)
                pool.tensor_tensor(coef2[:, 0, :], work2[:, 0, :], sb["half"][:], ALU.pow).then_inc(s["coef2_work"], 1)
                pool.wait_ge(s["coef2_work"], 3 * g + 3)
                pool.tensor_tensor(coef2[:, 1, :], work2[:, 1, :], coef2[:, 0, :], ALU.mult).then_inc(s["coef2_ready"], 1)

            def residual(g):
                hold_until(pool, [(s["coef_ready"], g + 1), (s["outd_stored"], 32 * g)], pool_passed)
                for t in range(TPG):
                    pool.tensor_scalar(resid[:, t, :], h[:, t, :], coef[:, 0, t:t + 1], coef[:, 1, t:t + 1],
                                       ALU.mult, ALU.add).then_inc(s["resid_ready"], 1)

            def centre(g):
                pool.wait_ge(s["max_ready"], g + 1)
                pool.tensor_sub(scores[:], scores[:], row_max[:].unsqueeze(2).broadcast_to([P, BLOCKS, IMAGES])).then_inc(s["centred"], 1)

            def probabilities(g):
                pool.wait_ge(s["inv_ready"], g + 1)
                pool.tensor_mul(scores[:], scores[:], row_inv[:].unsqueeze(2).broadcast_to([P, BLOCKS, IMAGES])).then_inc(s["probs_ready"], 1)

            def step(i, first, last):
                if not first:
                    coefficients2(i - 1)
                residual(i)
                centre(i)
                probabilities(i)
                if not last:
                    coefficients(i + 1)

            coefficients(0)
            step(0, True, False)
            with pool.Fori(1, GROUPS - 1) as i:
                step(i, False, False)
            step(GROUPS - 1, False, True)
            coefficients2(GROUPS - 1)

        @block.sync
        def _(sp):
            shift_in = io["shift"].rearrange("(k p r) -> p k r", k=BLOCKS, r=PADDED)[:, :, 1:PADDED]

            def load_patches(g, t):
                if not isinstance(g, int) or g > 0:
                    hold_until(sp, [(s["x_los"], TPG * g - TPG + t + 1)], sp_passed)
                sp.dma_start(x_raw[:, t, :], io["patches"][bass.ds(TPG * g + t, 1), :, :].rearrange("a p n -> p (a n)")
                             ).then_inc(x_loaded[t], 16)

            def store_normed(g):
                hold_until(sp, [(s["gate_p"], g + 1)], sp_passed)
                sp.dma_start(io["rows"][bass.ds(GTOK * g, GTOK), 0:XROW].rearrange("(t p) n -> p t n", p=P),
                             xf[:]).then_inc(s["xf_stored"], 16)

            def store_unrouted(g):
                hold_until(sp, [(s["outd_ready"], TPG * g + TPG)], sp_passed)
                sp.dma_start(io["out"][bass.ds(GTOK * g, GTOK), :].rearrange("(t p) n -> p t n", p=P),
                             resid[:]).then_inc(s["outd_stored"], 16)
                sp.dma_start(io["rows"][bass.ds(GTOK * g, GTOK), XROW:ROW].rearrange("(t p) n -> p t n", p=P),
                             resid[:]).then_inc(s["outd_stored"], 16)

            def shift(g):
                hold_until(sp, [(s["bd_ready"], g + 1)], sp_passed)
                sp.dma_start(shift_in, bd[:].rearrange("p a t n r -> p (a t n) r")).then_inc(s["bd_stored"], 16)
                hold_until(sp, [(s["bd_stored"], 16 * g + 16)], sp_passed)
                for q in range(QUADS):
                    src = io["shift"].rearrange("(k q m) -> k q m", k=BLOCKS, q=QUADS)[:, q, IMAGES:]
                    sp.dma_start(scores[q * IMAGES:(q + 1) * IMAGES, :, :],
                                 src.rearrange("k (i j) -> i k j", j=IMAGES)).then_inc(s["bd_shifted"], 16)

            def step(i, first, load):
                if load:
                    for t in range(TPG):
                        load_patches(i + 2, t)
                shift(i)
                if not first:
                    store_normed(i - 1)
                    store_unrouted(i - 1)

            for g in range(2):
                for t in range(TPG):
                    load_patches(g, t)
            step(0, True, True)
            with sp.Fori(1, GROUPS - 2) as i:
                step(i, False, True)
            step(GROUPS - 2, False, False)
            step(GROUPS - 1, False, False)
            store_normed(GROUPS - 1)
            store_unrouted(GROUPS - 1)
            sp.wait_ge(s["xf_stored"], 16 * GROUPS)
            sp.wait_ge(s["outd_stored"], 32 * GROUPS)


def place(nc, io, sb):
    ctx = ExitStack()
    with ctx:
        def buf(name, shape, dt=F32):
            return ctx.enter_context(nc.sbuf_tensor(name, shape, dt))

        def sem(name):
            return ctx.enter_context(nc.semaphore(name))

        chosen = buf("chosen", [P, EXPERTS, TILES])
        resets = buf("resets", [P, EXPERTS, TILES])
        counts = buf("counts", [P, EXPERTS, TILES])
        totals = buf("totals", [P, EXPERTS])
        before = buf("before", [P, EXPERTS])
        earlier = buf("earlier", [P, P])
        slot_ids_f = buf("slot_ids_f", [P, SLOT_TILES])
        lane_ids_f = buf("lane_ids_f", [P, P])
        slot_ids = buf("slot_ids", [P, SLOT_TILES], BF16)
        lane_ids = buf("lane_ids", [P, P], BF16)
        tile_no = buf("tile_no", [P, TILES])
        lane_no = buf("lane_no", [P, 1])
        pos = buf("pos", [P, TILES])
        pos_i = buf("pos_i", [P, TILES], I32)
        hi_i = buf("hi_i", [P, TILES], I32)
        lane_i = buf("lane_i", [P, TILES], I32)
        over = buf("over", [P, TILES])
        slot_tile = buf("slot_tile", [P, TILES])
        slot_lane = buf("slot_lane", [P, TILES])
        RING = 4
        lane_hot = buf("lane_hot", [P, RING, P], BF16)
        slot_hot = buf("slot_hot", [P, RING, 2, SLOT_TILES], BF16)
        empty = buf("empty", [P, SLOT_TILES])
        index_f = buf("index_f", [P, SLOT_TILES])
        base_ps = ctx.enter_context(nc.psum_tensor("base_ps", [P, D], F32))
        table_ps = ctx.enter_context(nc.psum_tensor("table_ps", [P, D], F32))
        consts_in, chain, total_ready, base_mm, hot, table_mm = (
            sem(n) for n in ("consts_in", "chain", "total_ready", "base_mm", "hot", "table_mm"))
        block = ctx.enter_context(nc.Block())

        @block.sync
        def _(sp):
            for dst, src in ((earlier, "earlier"), (slot_ids_f, "slot_ids"), (lane_ids_f, "lane_ids"),
                             (tile_no, "tile_no"), (lane_no, "lane_no")):
                sp.dma_start(dst[:], io[src]).then_inc(consts_in, 16)

        @block.tensor
        def _(pe):
            pe.wait_ge(total_ready, 1)
            pe.wait_ge(consts_in, 80)
            pe.matmul(base_ps[:, 0:EXPERTS], earlier[:], totals[:], start=True, stop=True).then_inc(base_mm, 1)

            def add(tile, ring, first, last):
                pe.wait_ge(hot, tile + 1)
                pe.matmul(table_ps[:, 0:2 * SLOT_TILES], lane_hot[:, ring, :],
                          slot_hot[:, ring, :, :].rearrange("p a n -> p (a n)"), start=first, stop=last
                          ).then_inc(table_mm, 1)

            for r in range(RING):
                add(r, r, r == 0, False)
            with pe.Fori(1, TILES // RING - 1) as i:
                for r in range(RING):
                    add(RING * i + r, r, False, False)
            for r in range(RING):
                add(TILES - RING + r, r, False, r == RING - 1)

        @block.vector
        def _(dve):
            done = [0]

            def link(ins):
                done[0] += 1
                ins.then_inc(chain, 1)
                dve.wait_ge(chain, done[0])

            link(dve.tensor_tensor(chosen[:], sb["route"][:].unsqueeze(1).broadcast_to([P, EXPERTS, TILES]),
                                   sb["expert_ids"][:].unsqueeze(2).broadcast_to([P, EXPERTS, TILES]), ALU.is_equal))
            link(dve.memset(resets[:], 1.0))
            link(dve.memset(resets[:, :, 0:1], 0.0))
            link(dve.tensor_tensor_scan(counts[:].rearrange("p e t -> p (e t)"), resets[:].rearrange("p e t -> p (e t)"),
                                        chosen[:].rearrange("p e t -> p (e t)"), 0.0, ALU.mult, ALU.add))
            dve.tensor_copy(totals[:].unsqueeze(2), counts[:, :, TILES - 1:TILES]).then_inc(total_ready, 1)
            dve.wait_ge(base_mm, 1)
            link(dve.tensor_copy(before[:], base_ps[:, 0:EXPERTS]))
            link(dve.tensor_add(counts[:], counts[:], before[:].unsqueeze(2).broadcast_to([P, EXPERTS, TILES])))
            link(dve.tensor_mul(counts[:], counts[:], chosen[:]))
            link(dve.reduce_sum(pos[:], counts[:].rearrange("p e t -> p t e"), AX.X))
            link(dve.tensor_scalar(pos[:], pos[:], -1.0, None, ALU.add))
            link(dve.tensor_copy(pos_i[:], pos[:]))
            link(dve.tensor_scalar(hi_i[:], pos_i[:], 7, None, ALU.arith_shift_right))
            link(dve.tensor_scalar(lane_i[:], pos_i[:], P - 1, None, ALU.bitwise_and))
            link(dve.tensor_copy(slot_tile[:], hi_i[:]))
            link(dve.tensor_copy(slot_lane[:], lane_i[:]))
            link(dve.scalar_tensor_tensor(out=slot_tile[:], in0=sb["route"][:], scalar=float(TPE), in1=slot_tile[:],
                                          op0=ALU.mult, op1=ALU.add))
            link(dve.tensor_scalar(over[:], pos[:], float(CAPACITY), 4096.0, ALU.is_ge, ALU.mult))
            link(dve.tensor_add(slot_tile[:], slot_tile[:], over[:]))
            dve.wait_ge(consts_in, 80)
            link(dve.tensor_copy(slot_ids[:], slot_ids_f[:]))
            link(dve.tensor_copy(lane_ids[:], lane_ids_f[:]))

            def one_hot(tile, ring, first):
                if not first:
                    dve.wait_ge(table_mm, tile - RING + 1)
                col = bass.ds(tile, 1)
                dve.tensor_scalar(lane_hot[:, ring, :], lane_ids[:], slot_lane[:, col], None, ALU.is_equal)
                dve.tensor_scalar(slot_hot[:, ring, 0, :], slot_ids[:], slot_tile[:, col], tile_no[:, col],
                                  ALU.is_equal, ALU.mult)
                dve.tensor_scalar(slot_hot[:, ring, 1, :], slot_ids[:], slot_tile[:, col], lane_no[:],
                                  ALU.is_equal, ALU.mult).then_inc(hot, 1)

            for r in range(RING):
                one_hot(r, r, True)
            with dve.Fori(1, TILES // RING) as i:
                for r in range(RING):
                    one_hot(RING * i + r, r, False)
            dve.wait_ge(table_mm, TILES)
            link(dve.tensor_scalar(empty[:], table_ps[:, 0:SLOT_TILES], 0.0, float(DUMP + P), ALU.is_equal, ALU.mult))
            link(dve.tensor_scalar(index_f[:], table_ps[:, 0:SLOT_TILES], float(P), float(-P), ALU.mult, ALU.add))
            link(dve.tensor_add(index_f[:], index_f[:], table_ps[:, SLOT_TILES:2 * SLOT_TILES]))
            link(dve.tensor_add(index_f[:], index_f[:], empty[:]))
            link(dve.tensor_scalar(empty[:], table_ps[:, 0:SLOT_TILES], 0.0, lane_no[:], ALU.is_equal, ALU.mult))
            link(dve.tensor_add(index_f[:], index_f[:], empty[:]))
            link(dve.tensor_copy(sb["index"][:], index_f[:]))


def experts(nc, io, sb):
    ctx = ExitStack()
    with ctx:
        def buf(name, shape, dt=F32):
            return ctx.enter_context(nc.sbuf_tensor(name, shape, dt))

        def sem(name):
            return ctx.enter_context(nc.semaphore(name))

        RING = TPE
        AHEAD = RING // 2
        PAIR = 2 * TPE
        STEPS = EXPERTS // 2
        w_raw = buf("w_raw", [P, 2, DC, D])
        w_hi = buf("ew_hi", [P, 2, DC, D], F32R)
        w_lo = buf("ew_lo", [P, 2, DC, D], F32R)
        bias = buf("ebias", [P, 2, D])
        rows = buf("rows_sb", [P, RING, ROW])
        now = buf("now", [P, RING], I32)
        xT_hi = buf("xT_hi", [P, 2, DC * P], F32R)
        xT_lo = buf("xT_lo", [P, 2, DC * P], F32R)
        turn = ctx.enter_context(nc.psum_tensor("turn", [P, 2, D], F32))
        prod = ctx.enter_context(nc.psum_tensor("prod", [P, 2, D], F32))
        w_in = [sem(f"w_in{r}") for r in range(2)]
        sp_passed = sem("sp_passed2")
        gathered = [sem(f"gathered{r}") for r in range(RING)]
        scattered = [sem(f"scattered{r}") for r in range(RING)]
        index_now, passed, w_his, w_los, xT_mm, xT_his, xT_los, y_mm, y_biased, y_gap, result_ready = (
            sem(n) for n in "index_now pool_passed2 ew_his ew_los xT_mm xT_his xT_los y_mm y_biased y_gap result_ready".split())
        block = ctx.enter_context(nc.Block())
        ident = sb["ident"]

        @block.sync
        def _(sp):
            def load(i, half):
                if not isinstance(i, int) or i > 0:
                    hold_until(sp, [(w_los, DC * (2 * i + half - 1))], sp_passed)
                sp.dma_start(w_raw[:, half, :, :], io["expert_wT"][bass.ds(2 * i + half, 1), :, :, :]
                             .rearrange("a p c n -> p (a c) n")).then_inc(w_in[half], 16)
                if not isinstance(i, int) or i > 0:
                    hold_until(sp, [(y_biased, PAIR * i - PAIR + TPE * (half + 1))], sp_passed)
                sp.dma_start(bias[:, half, :], io["expert_b"][bass.ds(2 * i + half, 1), :].broadcast_to([P, D])
                             ).then_inc(w_in[half], 16)

            load(0, 0)
            load(0, 1)
            with sp.Fori(1, STEPS) as i:
                load(i, 0)
                load(i, 1)

        @block.scalar
        def _(act):
            def split(i, half, c):
                if c == 0:
                    act.wait_ge(w_in[half], 32 * i + 32)
                    wait(act, y_mm, PAIR * i - PAIR + TPE * (half + 1))
                act.activation(w_hi[:, half, c, :], w_raw[:, half, c, :], ACT.Copy).then_inc(w_his, 1)

            def rows_hi(i, k):
                act.wait_ge(xT_mm, PAIR * i + k + 1)
                act.activation(xT_hi[:, k % 2, :], turn[:, k % 2, :], ACT.Copy).then_inc(xT_his, 1)

            def step(i, last):
                for k in range(PAIR):
                    rows_hi(i, k)
                    if 2 <= k < 2 + DC:
                        split(i, 1, k - 2)
                    elif TPE + 2 <= k < TPE + 2 + DC and not last:
                        split(i + 1, 0, k - TPE - 2)

            for c in range(DC):
                split(0, 0, c)
            step(0, False)
            with act.Fori(1, STEPS - 1) as i:
                step(i, False)
            step(STEPS - 1, True)

        @block.vector
        def _(dve):
            def split(i, half, c):
                dve.wait_ge(w_his, DC * (2 * i + half) + c + 1)
                dve.tensor_sub(w_lo[:, half, c, :], w_raw[:, half, c, :], w_hi[:, half, c, :].bitcast(F32)).then_inc(w_los, 1)

            def rows_lo(i, k):
                dve.wait_ge(xT_his, PAIR * i + k + 1)
                dve.tensor_sub(xT_lo[:, k % 2, :], turn[:, k % 2, :], xT_hi[:, k % 2, :].bitcast(F32)).then_inc(xT_los, 1)

            def finish(i, k):
                n, row = PAIR * i + k, rows[:, k % RING, :]
                dve.wait_ge(y_mm, n + 1)
                gap = prod[:, k % 2, :]
                dve.tensor_sub(row[:, 0:D], bias[:, k // TPE, :], row[:, 0:D]).then_inc(y_gap, 1)
                dve.wait_ge(y_gap, n + 1)
                dve.tensor_add(row[:, 0:D], gap, row[:, 0:D]).then_inc(y_biased, 1)
                dve.wait_ge(y_biased, n + 1)
                dve.scalar_tensor_tensor(out=row[:, XROW:ROW], in0=row[:, 0:D], scalar=row[:, D:D + 1],
                                         in1=row[:, XROW:ROW], op0=ALU.mult, op1=ALU.add).then_inc(result_ready, 1)

            def step(i, last):
                for k in range(PAIR):
                    if k + 1 < PAIR:
                        rows_lo(i, k + 1)
                    elif not last:
                        rows_lo(i + 1, 0)
                    finish(i, k)
                    if 2 <= k < 2 + DC:
                        split(i, 1, k - 2)
                    elif TPE + 2 <= k < TPE + 2 + DC and not last:
                        split(i + 1, 0, k - TPE - 2)

            for c in range(DC):
                split(0, 0, c)
            rows_lo(0, 0)
            step(0, False)
            with dve.Fori(1, STEPS - 1) as i:
                step(i, False)
            step(STEPS - 1, True)

        @block.tensor
        def _(pe):
            def turn_rows(i, k):
                pe.wait_ge(gathered[k % RING], 16 * (2 * i + k // RING) + 16)
                wait(pe, xT_los, PAIR * i + k - 1)
                for c in range(DC):
                    last = pe.transpose(turn[:, k % 2, c * P:(c + 1) * P], rows[:, k % RING, c * P:(c + 1) * P], ident[:])
                last.then_inc(xT_mm, 1)

            def multiply(i, k):
                half = k // TPE
                if k % TPE == 0:
                    pe.wait_ge(w_los, DC * (2 * i + half) + DC)
                pe.wait_ge(xT_los, PAIR * i + k + 1)
                wait(pe, y_biased, PAIR * i + k - 1)
                for c in range(DC):
                    hi, lo = (x[:, k % 2, c * P:(c + 1) * P] for x in (xT_hi, xT_lo))
                    pe.matmul(prod[:, k % 2, :], hi, w_hi[:, half, c, :], start=c == 0, stop=False)
                    pe.matmul(prod[:, k % 2, :], hi, w_lo[:, half, c, :], start=False, stop=False)
                    last = pe.matmul(prod[:, k % 2, :], lo, w_hi[:, half, c, :], start=False, stop=c == DC - 1)
                last.then_inc(y_mm, 1)

            def step(i, last):
                for k in range(PAIR):
                    if k + 1 < PAIR:
                        turn_rows(i, k + 1)
                    elif not last:
                        turn_rows(i + 1, 0)
                    multiply(i, k)

            turn_rows(0, 0)
            step(0, False)
            with pe.Fori(1, STEPS - 1) as i:
                step(i, False)
            step(STEPS - 1, True)

        @block.gpsimd
        def _(pool):
            def gather(i, k):
                slot = k % RING
                hold_until(pool, [(scattered[slot], 16 * (2 * i + k // RING))], passed)
                pool.tensor_copy(now[:, slot:slot + 1], sb["index"][:, bass.ds(PAIR * i + k, 1)]).then_inc(index_now, 1)
                hold_until(pool, [(index_now, PAIR * i + k + 1)], passed)
                pool.indirect_dma_start(rows[:, slot, :], None, io["rows"],
                                        bass.IndirectOffsetOnAxis(ap=now[:, slot:slot + 1], axis=0)).then_inc(gathered[slot], 16)

            def scatter(i, k):
                slot = k % RING
                hold_until(pool, [(result_ready, PAIR * i + k + 1)], passed)
                pool.indirect_dma_start(io["out"], bass.IndirectOffsetOnAxis(ap=now[:, slot:slot + 1], axis=0),
                                        rows[:, slot, XROW:ROW], None, bounds_check=TOKENS - 1, oob_is_err=False
                                        ).then_inc(scattered[slot], 16)

            def step(i, last):
                for k in range(PAIR):
                    if k + AHEAD < PAIR or not last:
                        gather(i, k + AHEAD)
                    scatter(i, k)

            for k in range(AHEAD):
                gather(0, k)
            step(0, False)
            with pool.Fori(1, STEPS - 1) as i:
                step(i, False)
            step(STEPS - 1, True)
            for slot in range(RING):
                pool.wait_ge(scattered[slot], 16 * 2 * STEPS)


def build(nc, io):
    with ExitStack() as whole:
        sb = {}

        def hold(ctx, name, shape, dt=F32):
            sb[name] = ctx.enter_context(nc.sbuf_tensor(f"{name}_sb", shape, dt))

        hold(whole, "ident", [P, P])
        hold(whole, "expert_ids", [P, EXPERTS])
        hold(whole, "route", [P, TILES])
        hold(whole, "index", [P, SLOT_TILES], I32)
        with ExitStack() as first:
            for name, cols in (("tok", D * KC), ("qkv", 3 * D * DC), ("out", D * DC)):
                chunks = KC if name == "tok" else DC
                hold(first, f"{name}_hi", [P, chunks, cols // chunks], F32R)
                hold(first, f"{name}_lo", [P, chunks, cols // chunks], F32R)
            hold(first, "rk", [P, PAIRS, IMAGES])
            hold(first, "bd_const", [P, 2, PAIRS, IMAGES])
            hold(first, "qkv_b", [P, 3 * DC])
            hold(first, "tok_b", [P, D])
            hold(first, "gate_wT", [P, DC, EXPERTS])
            hold(first, "gate_b", [P, EXPERTS])
            hold(first, "half", [P, TPG])
            hold(first, "probsT", [P, BLOCKS, P])
            prepare(nc, io, sb)
            tower(nc, io, sb)
        place(nc, io, sb)
        experts(nc, io, sb)


def constants():
    f32 = np.float32
    lane = np.arange(P)
    image, quad = lane % IMAGES, lane // IMAGES
    order = image * QUADS + quad
    place_in = np.arange(IMAGES - 1, -1, -1, dtype=f32)
    inv = (1.0 / np.power(f32(10000.0), np.arange(0, D, 2, dtype=f32) / f32(D))).astype(f32)
    angle = place_in[:, None] * inv[None, :]
    sinusoid = np.concatenate([np.sin(angle), np.cos(angle)], axis=-1).astype(f32)
    spread = lambda row, dt: np.ascontiguousarray(np.broadcast_to(row, (P, len(row)))).astype(dt)
    return {
        "ident": np.eye(P, dtype=f32),
        "sinusoid": np.ascontiguousarray(sinusoid.T.reshape(DC, P, IMAGES).transpose(1, 0, 2)),
        "expert_ids": spread(np.arange(EXPERTS), f32),
        "earlier": (order[:, None] < order[None, :]).astype(f32),
        "slot_ids": spread(np.arange(SLOT_TILES), f32),
        "lane_ids": spread(lane, f32),
        "tile_no": spread(np.arange(1, TILES + 1), f32),
        "lane_no": lane.astype(f32)[:, None],
    }


def kernel(**inputs):
    import concourse.bacc as bacc
    from concourse.bass_utils import run_bass_kernel_spmd

    a = {k: np.asarray(v) for k, v in inputs.items()}
    n = SIDE // PATCH
    x = a["x"].reshape(IMAGES, CHANNELS, n, PATCH, n, PATCH).transpose(2, 4, 1, 3, 5, 0)
    x = x.reshape(QUADS, TILES, KC, P, IMAGES).transpose(1, 3, 2, 0, 4).reshape(TILES, P, KC * P)

    def chunked(w):
        out, inn = w.shape
        return np.ascontiguousarray(w.T.reshape(inn // P, P, out).transpose(1, 0, 2))

    def spread(row):
        return np.ascontiguousarray(np.broadcast_to(row, (P, row.size)))

    def columns(row):
        return np.ascontiguousarray(row.reshape(-1, P).T)

    arrays = {
        "patches": np.ascontiguousarray(x),
        "tok_wT": chunked(a["L0_tok_w"]),
        "tok_b": spread(a["L0_tok_b"]),
        "qkv_wT": chunked(a["L0_attn_Wqkv"]),
        "wr_wT": chunked(a["L0_attn_Wr"]),
        "out_wT": chunked(a["L0_attn_Wo"]),
        "gamma": columns(a["L0_attn_ln_gamma"]),
        "beta": columns(a["L0_attn_ln_beta"]),
        "r_w_bias": columns(a["L0_attn_r_w_bias"]),
        "r_r_bias": columns(a["L0_attn_r_r_bias"]),
        "gate_wT": chunked(a["L0_ffn_switch_w"]),
        "gate_b": spread(a["L0_ffn_switch_b"]),
        "expert_wT": np.ascontiguousarray(a["L0_ffn_expert_w"].transpose(0, 2, 1).reshape(EXPERTS, DC, P, D).transpose(0, 2, 1, 3)),
        "expert_b": a["L0_ffn_expert_b"],
        **constants(),
    }
    nc = bacc.Bacc("TRN2", target_bir_lowering=False, num_devices=1)
    io = {k: nc.dram_tensor(f"in_{k}", v.shape, mybir.dt.from_np(v.dtype), kind="ExternalInput").ap() for k, v in arrays.items()}
    io["out"] = nc.dram_tensor("out_rows", (TOKENS, D), F32, kind="ExternalOutput").ap()
    io["rows"] = nc.dram_tensor("token_rows", (TOKENS + P, ROW), F32, kind="Internal").ap()
    io["shift"] = nc.dram_tensor("shift_scratch", (BLOCKS * BLOCK_STRIDE,), F32, kind="Internal").ap()
    build(nc, io)
    done = run_bass_kernel_spmd(nc, [{f"in_{k}": v for k, v in arrays.items()}], core_ids=[0])
    out = np.asarray(done.results[0]["out_rows"])
    return out.reshape(TILES, QUADS, IMAGES, D).transpose(2, 1, 0, 3).reshape(IMAGES, POSITIONS, D)
```

```python
from contextlib import ExitStack

import numpy as np

import concourse.bass as bass
from concourse import mybir

P = 128
IMAGES, CHANNELS, SIDE, PATCH = 32, 3, 384, 16
POSITIONS = (SIDE // PATCH) ** 2
QUADS = P // IMAGES
TILES = POSITIONS // QUADS
TPG = 3
GROUPS = TILES // TPG
GTOK = TPG * P
D = 512
DC = D // P
KC = CHANNELS * PATCH * PATCH // P
HEADS, DH = 8, 64
PAIRS = HEADS // 2
BLOCKS = 2 * TPG * PAIRS
EXPERTS = 16
TOKENS = IMAGES * POSITIONS
CAPACITY = int(1.2 * TOKENS / EXPERTS)
TPE = -(-CAPACITY // P)
SLOT_TILES = EXPERTS * TPE
DUMP = TOKENS
XROW = D + 4
ROW = XROW + D
EPS = 1e-5
PADDED = IMAGES + 1
BLOCK_STRIDE = P * PADDED

F32, F32R, BF16, I32 = mybir.dt.float32, mybir.dt.float32r, mybir.dt.bfloat16, mybir.dt.int32
ALU, ACT, AX = mybir.AluOpType, mybir.ActivationFunctionType, mybir.AxisListType


def wait(eng, sem, value):
    if not isinstance(value, int) or value > 0:
        eng.wait_ge(sem, value)


def hold_until(eng, waits, passed):
    for sem, value in waits:
        if not isinstance(value, int) or value > 0:
            eng.wait_ge(sem, value)
            eng.sem_inc(passed, 1)


def prepare(nc, io, sb):
    ctx = ExitStack()
    with ctx:
        def buf(name, shape, dt=F32):
            return ctx.enter_context(nc.sbuf_tensor(name, shape, dt))

        def sem(name):
            return ctx.enter_context(nc.semaphore(name))

        tok_raw = buf("tok_raw", [P, KC, D])
        qkv_raw = buf("qkv_raw", [P, DC, 3 * D])
        qkv_scaled = buf("qkv_scaled", [P, DC, 3 * D])
        out_raw = buf("out_raw", [P, DC, D])
        wr_raw = buf("wr_raw", [P, DC, D])
        gate_raw = buf("gate_raw", [P, DC, EXPERTS])
        sinusoid = buf("sinusoid", [P, DC, IMAGES])
        gamma = buf("gamma", [P, DC])
        beta = buf("beta", [P, DC])
        w_bias = buf("w_bias", [P, PAIRS])
        r_bias = buf("r_bias", [P, PAIRS])
        bias_gap = buf("bias_gap", [P, PAIRS])
        gap_cols = buf("gap_cols", [P, PAIRS, P])
        zeros = buf("zeros", [P, ROW])
        proj_ps = ctx.enter_context(nc.psum_tensor("proj_ps", [P, 2, D], F32))
        gap_ps = ctx.enter_context(nc.psum_tensor("gap_ps", [P, 2, D], F32))
        tok_in, qkv_in, out_in, small_in, wr_in = (sem(f"{n}_in") for n in ("tok", "qkv", "out", "small", "wr"))
        zeros_set, zeros_out, scaled, his, los = (sem(n) for n in ("zeros_set", "zeros_out", "scaled", "his", "los"))
        projected, rk_ready, gap_ready, gap_mm, prep_done, pt_zero = (
            sem(n) for n in ("projected", "rk_ready", "gap_ready", "gap_mm", "prep_done", "pt_zero"))
        block = ctx.enter_context(nc.Block())

        @block.sync
        def _(sp):
            sp.dma_start(tok_raw[:], io["tok_wT"]).then_inc(tok_in, 16)
            sp.dma_start(qkv_raw[:], io["qkv_wT"]).then_inc(qkv_in, 16)
            sp.dma_start(out_raw[:], io["out_wT"]).then_inc(out_in, 16)
            sp.dma_start(wr_raw[:], io["wr_wT"]).then_inc(wr_in, 16)
            sp.wait_ge(zeros_set, 1)
            sp.dma_start(io["shift"].rearrange("(p n) -> p n", p=P),
                         zeros[:, 0:BLOCKS * BLOCK_STRIDE // P]).then_inc(zeros_out, 16)
            sp.dma_start(io["rows"][DUMP:DUMP + P, :], zeros[:]).then_inc(zeros_out, 16)
            sp.wait_ge(zeros_out, 32)

        @block.scalar
        def _(act):
            for dst, src in ((gamma, "gamma"), (beta, "beta"), (w_bias, "r_w_bias"), (r_bias, "r_r_bias"),
                             (sinusoid, "sinusoid"), (sb["ident"], "ident"), (sb["tok_b"], "tok_b"),
                             (gate_raw, "gate_wT"), (sb["gate_b"], "gate_b"), (sb["expert_ids"], "expert_ids")):
                act.dma_start(dst[:], io[src]).then_inc(small_in, 16)
            act.wait_ge(tok_in, 16)
            for c in range(KC):
                act.activation(sb["tok_hi"][:, c, :], tok_raw[:, c, :], ACT.Copy).then_inc(his, 1)
            for c in range(DC):
                act.wait_ge(scaled, c + 1)
                act.activation(sb["qkv_hi"][:, c, :], qkv_scaled[:, c, :], ACT.Copy).then_inc(his, 1)
            act.wait_ge(out_in, 16)
            for c in range(DC):
                act.activation(sb["out_hi"][:, c, :], out_raw[:, c, :], ACT.Copy).then_inc(his, 1)

        @block.vector
        def _(dve):
            dve.memset(zeros[:], 0.0).then_inc(zeros_set, 1)
            dve.wait_ge(small_in, 160)
            dve.tensor_sub(bias_gap[:], r_bias[:], w_bias[:]).then_inc(prep_done, 1)
            dve.tensor_copy(sb["gate_w"][:, :, 0, :], gate_raw[:]).then_inc(prep_done, 1)
            dve.wait_ge(prep_done, 2)
            dve.tensor_sub(sb["gate_w"][:, :, 1, :], gate_raw[:], sb["gate_w"][:, :, 0, :].bitcast(F32)).then_inc(prep_done, 1)
            dve.tensor_copy(gap_cols[:], bias_gap[:].unsqueeze(2).broadcast_to([P, PAIRS, P])).then_inc(gap_ready, 1)
            for c in range(KC):
                dve.wait_ge(his, c + 1)
                dve.tensor_sub(sb["tok_lo"][:, c, :], tok_raw[:, c, :], sb["tok_hi"][:, c, :].bitcast(F32)).then_inc(los, 1)
            dve.wait_ge(projected, 2)
            dve.tensor_copy(sb["rk"][:], proj_ps[:, 1, 0:DC * IMAGES].rearrange("p (c r) -> p c r", c=DC)).then_inc(rk_ready, 1)
            dve.tensor_add(sb["qkv_b"][:, 0:DC], proj_ps[:, 0, 0:DC], w_bias[:]).then_inc(prep_done, 1)
            dve.tensor_copy(sb["qkv_b"][:, DC:3 * DC], proj_ps[:, 0, DC:3 * DC]).then_inc(prep_done, 1)
            dve.wait_ge(gap_mm, 1)
            dve.tensor_copy(sb["bd_const"][:], gap_ps[:, :, 0:PAIRS * IMAGES].rearrange("p a (c r) -> p a c r", c=PAIRS)).then_inc(prep_done, 1)
            for c in range(DC):
                dve.wait_ge(his, KC + c + 1)
                dve.tensor_sub(sb["qkv_lo"][:, c, :], qkv_scaled[:, c, :], sb["qkv_hi"][:, c, :].bitcast(F32)).then_inc(los, 1)
            for c in range(DC):
                dve.wait_ge(his, KC + DC + c + 1)
                dve.tensor_sub(sb["out_lo"][:, c, :], out_raw[:, c, :], sb["out_hi"][:, c, :].bitcast(F32)).then_inc(los, 1)

        @block.gpsimd
        def _(pool):
            pool.memset(sb["half"][:], -0.5).then_inc(pt_zero, 1)
            pool.memset(sb["probsT"][:], 0.0).then_inc(pt_zero, 1)
            pool.wait_ge(qkv_in, 16)
            pool.wait_ge(small_in, 160)
            for c in range(DC):
                pool.tensor_scalar(qkv_scaled[:, c, :], qkv_raw[:, c, :], gamma[:, c:c + 1], None, ALU.mult).then_inc(scaled, 1)

        @block.tensor
        def _(pe):
            pe.wait_ge(small_in, 160)
            pe.wait_ge(qkv_in, 16)
            for e in range(3 * DC):
                for c in range(DC):
                    last = pe.matmul(proj_ps[:, 0, e:e + 1], qkv_raw[:, c, e * P:(e + 1) * P], beta[:, c:c + 1],
                                     start=c == 0, stop=c == DC - 1)
            last.then_inc(projected, 1)
            pe.wait_ge(wr_in, 16)
            for e in range(DC):
                for c in range(DC):
                    last = pe.matmul(proj_ps[:, 1, e * IMAGES:(e + 1) * IMAGES], wr_raw[:, c, e * P:(e + 1) * P],
                                     sinusoid[:, c, :], start=c == 0, stop=c == DC - 1)
            last.then_inc(projected, 1)
            pe.wait_ge(gap_ready, 1)
            pe.wait_ge(rk_ready, 1)
            for par in range(2):
                rows = slice(par * DH, (par + 1) * DH)
                for n in range(PAIRS):
                    last = pe.matmul(gap_ps[:, par, n * IMAGES:(n + 1) * IMAGES], gap_cols[rows, n, :],
                                     sb["rk"][rows, n, :], start=True, stop=True)
            last.then_inc(gap_mm, 1)


def tower(nc, io, sb):
    ctx = ExitStack()
    with ctx:
        def buf(name, shape, dt=F32):
            return ctx.enter_context(nc.sbuf_tensor(name, shape, dt))

        def sem(name):
            return ctx.enter_context(nc.semaphore(name))

        x_raw = buf("x_raw", [P, TPG, KC * P])
        x_hi = buf("x_hi", [P, TPG, KC * P], F32R)
        x_lo = buf("x_lo", [P, TPG, KC * P], F32R)
        h = buf("h", [P, TPG, D])
        u = buf("u", [P, TPG, D])
        resid = buf("resid", [P, TPG, D])
        xf = buf("xf", [P, TPG, XROW])
        wT_hi = buf("wT_hi", [P, DC, GTOK], F32R)
        wT_lo = buf("wT_lo", [P, DC, GTOK], F32R)
        qT = buf("qT", [P, PAIRS, GTOK])
        kT = buf("kT", [P, PAIRS, GTOK])
        v = buf("v", [P, TPG, D])
        bd = buf("bd", [P, 2, TPG, PAIRS, IMAGES])
        scores = buf("scores", [P, BLOCKS, IMAGES])
        scores5 = scores[:, :, :].rearrange("p (a t n) j -> p a (t n j)", a=2, t=TPG)
        row_max = buf("row_max", [P, BLOCKS])
        row_sum = buf("row_sum", [P, BLOCKS])
        row_inv = buf("row_inv", [P, BLOCKS])
        probsT = sb["probsT"]
        attnT_hi = buf("attnT_hi", [P, DC, GTOK], F32R)
        attnT_lo = buf("attnT_lo", [P, DC, GTOK], F32R)
        stats = buf("stats", [P, TPG, 6])
        mv = buf("mv", [P, TPG, 2])
        stats2 = buf("stats2", [P, TPG, 6])
        mv2 = buf("mv2", [P, TPG, 2])
        work = buf("work", [P, 2, TPG])
        minus_mean = buf("minus_mean", [P, TPG])
        scale = buf("scale", [P, 2, TPG])
        shift = buf("shift", [P, 2, TPG])
        scale_sum = buf("scale_sum", [P, TPG])
        coef2 = buf("coef2", [P, 2, TPG])
        work2 = buf("work2", [P, 2, TPG])
        halves = buf("halves", [P, TPG * 2 * EXPERTS])
        logits = buf("logits", [P, TPG, EXPERTS])
        gate_exp = buf("gate_exp", [P, TPG, EXPERTS])
        cand = buf("cand", [P, TPG, EXPERTS])
        gate_max = buf("gate_max", [P, TPG])
        gate_sum = buf("gate_sum", [P, TPG])
        wide_ps = ctx.enter_context(nc.psum_tensor("wide_ps", [P, 2, D], F32))
        turn_ps = ctx.enter_context(nc.psum_tensor("turn_ps", [P, 2, D], F32))
        ac_ps = ctx.enter_context(nc.psum_tensor("ac_ps", [P, 2, D], F32))
        bd_ps = ctx.enter_context(nc.psum_tensor("bd_ps", [P, 2, D], F32))

        x_loaded = [sem(f"x_loaded{t}") for t in range(TPG)]
        names = """x_his x_los tok_mm h_ready stats_ready coef_work coef_ready u_ready resid_ready uT_mm w_his w_los
            qk_mm qk_ready bd_mm bd_ready bd_stored bd_shifted v_mm v_ready ac_mm sum_ready max_ready centred exped
            rowsum_ready inv_ready probs_ready probsT_ready pv_mm attn_his attn_los out_mm h2_ready stats2_ready
            coef2_work coef2_ready xf_ready xf_stored xfT_mm xfT_ready xfT_los gate_mm logits_added logits_read gate_maxed gate_centred
            gate_exped gate_summed gate_p cand_a cand_b outd_ready outd_stored""".split()
        s = {n: sem(n) for n in names}
        pe_passed, dve_passed, pool_passed, sp_passed = (sem(f"{n}_passed") for n in ("pe", "dve", "pool", "sp"))
        block = ctx.enter_context(nc.Block())
        ident = sb["ident"]

        def u_bank(c):
            return (turn_ps if c < 2 else ac_ps)[:, c % 2, 0:GTOK]

        def attn_bank(c):
            return (bd_ps if c < 2 else turn_ps)[:, c % 2, 0:GTOK]

        @block.tensor
        def _(pe):
            def three(out, a_hi, a_lo, b_hi, b_lo, first, last):
                pe.matmul(out, a_hi, b_hi, start=first, stop=False)
                pe.matmul(out, a_hi, b_lo, start=False, stop=False)
                return pe.matmul(out, a_lo, b_hi, start=False, stop=last)

            def tokenize(g, first, tiles):
                for t in tiles:
                    pe.wait_ge(s["x_los"], TPG * g + t + 1)
                    if t == 2:
                        pe.wait_ge(s["h_ready"], TPG * g + 1)
                    elif not first:
                        pe.wait_ge(s["v_ready"], TPG * g + t - 1)
                    for c in range(KC):
                        cols = slice(c * P, (c + 1) * P)
                        last = three(wide_ps[:, (t + 1) % 2, :], x_hi[:, t, cols], x_lo[:, t, cols],
                                     sb["tok_hi"][:, c, :], sb["tok_lo"][:, c, :], c == 0, c == KC - 1)
                    last.then_inc(s["tok_mm"], 1)

            def turn_u(g, first):
                for c in range(DC):
                    if c == 0:
                        pe.wait_ge(s["u_ready"], TPG * g + TPG)
                    if c < 2 and not first:
                        pe.wait_ge(s["attn_los"], DC * (g - 1) + c + 3)
                    elif not first:
                        pe.wait_ge(s["sum_ready"], g)
                    for t in range(TPG):
                        last = pe.transpose(u_bank(c)[:, t * P:(t + 1) * P], u[:, t, c * P:(c + 1) * P], ident[:])
                    last.then_inc(s["uT_mm"], 1)

            def query_key(g, e):
                if e == 0:
                    pe.wait_ge(s["w_los"], DC * g + DC)
                if e >= 2:
                    pe.wait_ge(s["qk_ready"], 2 * DC * g + e - 1)
                for c in range(DC):
                    cols = slice(e * P, (e + 1) * P)
                    last = three(turn_ps[:, e % 2, 0:GTOK], sb["qkv_hi"][:, c, cols], sb["qkv_lo"][:, c, cols],
                                 wT_hi[:, c, :], wT_lo[:, c, :], c == 0, c == DC - 1)
                last.then_inc(s["qk_mm"], 1)

            def turn_xf(g, last_group):
                for c in range(DC):
                    if c == 0:
                        pe.wait_ge(s["xf_ready"], TPG * g + TPG)
                    if last_group:
                        pe.wait_ge(s["attn_los"], DC * g + c + 1)
                    elif c < 2:
                        pe.wait_ge(s["bd_ready"], g + 2)
                    else:
                        pe.wait_ge(s["qk_ready"], 2 * DC * (g + 1) + c + 5)
                    for t in range(TPG):
                        last = pe.transpose(attn_bank(c)[:, t * P:(t + 1) * P], xf[:, t, c * P:(c + 1) * P], ident[:])
                    last.then_inc(s["xfT_mm"], 1)

            def gate(g):
                pe.wait_ge(s["xfT_los"], DC * g + DC)
                pe.wait_ge(s["h2_ready"], TPG * g + TPG)
                for c in range(DC):
                    for half in (attnT_hi, attnT_lo):
                        last = pe.matmul(wide_ps[0:2 * EXPERTS, 1, 0:GTOK], sb["gate_w"][:, c, :, :].rearrange("p a e -> p (a e)"),
                                         half[:, c, :], start=c == 0 and half is attnT_hi, stop=c == DC - 1 and half is attnT_lo)
                last.then_inc(s["gate_mm"], 1)

            def position_scores(g):
                hold_until(pe, [(s["qk_ready"], 2 * DC * g + DC),
                                (s["attn_los"], DC * g)], pe_passed)
                for par in range(2):
                    rows = slice(par * DH, (par + 1) * DH)
                    for t in range(TPG):
                        for n in range(PAIRS):
                            at = (t * PAIRS + n) * IMAGES
                            for q in range(QUADS):
                                toks = slice(t * P + q * IMAGES, t * P + (q + 1) * IMAGES)
                                last = pe.matmul(bd_ps[q * IMAGES:(q + 1) * IMAGES, par, at:at + IMAGES],
                                                 qT[rows, n, toks], sb["rk"][rows, n, :], start=True, stop=True)
                last.then_inc(s["bd_mm"], 1)

            def values(g, tiles):
                for t in tiles:
                    if t == 0:
                        wait(pe, s["h2_ready"], TPG * g)
                    elif t == 1:
                        wait(pe, s["logits_read"], g)
                    else:
                        pe.wait_ge(s["v_ready"], TPG * g + 1)
                    for c in range(DC):
                        cols = slice(t * P, (t + 1) * P)
                        last = three(wide_ps[:, t % 2, :], wT_hi[:, c, cols], wT_lo[:, c, cols],
                                     sb["qkv_hi"][:, c, 2 * D:], sb["qkv_lo"][:, c, 2 * D:], c == 0, c == DC - 1)
                    last.then_inc(s["v_mm"], 1)

            def content_scores(g):
                hold_until(pe, [(s["qk_ready"], 2 * DC * g + 2 * DC),
                                (s["w_los"], DC * g + DC)], pe_passed)
                for par in range(2):
                    rows = slice(par * DH, (par + 1) * DH)
                    for t in range(TPG):
                        for n in range(PAIRS):
                            at = (t * PAIRS + n) * IMAGES
                            for q in range(QUADS):
                                toks = slice(t * P + q * IMAGES, t * P + (q + 1) * IMAGES)
                                last = pe.matmul(ac_ps[q * IMAGES:(q + 1) * IMAGES, par, at:at + IMAGES],
                                                 qT[rows, n, toks], kT[rows, n, toks], start=True, stop=True)
                last.then_inc(s["ac_mm"], 1)

            def attend(g, first):
                pe.wait_ge(s["v_ready"], TPG * g + TPG)
                pe.wait_ge(s["probsT_ready"], QUADS * g + QUADS)
                for c in range(DC):
                    if not first:
                        pe.wait_ge(s["xfT_los"], DC * (g - 1) + c + 1)
                    elif c < 2:
                        pe.wait_ge(s["bd_ready"], g + 1)
                    else:
                        pe.wait_ge(s["qk_ready"], 2 * DC * g + c + 5)
                    for par in range(2):
                        head = 2 * c + par
                        for t in range(TPG):
                            blk = (par * TPG + t) * PAIRS + c
                            last = pe.matmul(attn_bank(c)[par * DH:(par + 1) * DH, t * P:(t + 1) * P],
                                             v[:, t, head * DH:(head + 1) * DH], probsT[:, blk, :], start=True, stop=True)
                    last.then_inc(s["pv_mm"], 1)

            def project(g, last_group, tiles):
                if tiles[0] == 0:
                    pe.wait_ge(s["attn_los"], DC * g + DC)
                for t in tiles:
                    if t == 2:
                        pe.wait_ge(s["h2_ready"], TPG * g + 1)
                    elif last_group:
                        pe.wait_ge(s["v_ready"], TPG * g + TPG)
                    else:
                        pe.wait_ge(s["h_ready"], TPG * g + TPG + t + 2)
                    for c in range(DC):
                        cols = slice(t * P, (t + 1) * P)
                        last = three(wide_ps[:, t % 2, :], attnT_hi[:, c, cols], attnT_lo[:, c, cols],
                                     sb["out_hi"][:, c, :], sb["out_lo"][:, c, :], c == 0, c == DC - 1)
                    last.then_inc(s["out_mm"], 1)

            def step(i, first, last):
                for e in range(DC + 1):
                    query_key(i, e)
                position_scores(i)
                for e in range(DC + 1, 2 * DC):
                    query_key(i, e)
                if not first:
                    turn_xf(i - 1, False)
                values(i, (0,))
                if not first:
                    gate(i - 1)
                content_scores(i)
                values(i, (1, 2))
                if not last:
                    tokenize(i + 1, False, (0, 1))
                attend(i, first)
                if not last:
                    tokenize(i + 1, False, (2,))
                project(i, last, (0, 1))
                if not last:
                    turn_u(i + 1, False)
                project(i, last, (2,))

            tokenize(0, True, (0, 1, 2))
            turn_u(0, True)
            step(0, True, False)
            with pe.Fori(1, GROUPS - 1) as i:
                step(i, False, False)
            step(GROUPS - 1, False, True)
            turn_xf(GROUPS - 1, True)
            gate(GROUPS - 1)

        @block.scalar
        def _(act):
            def patches_hi(g, t):
                act.wait_ge(x_loaded[t], 16 * g + 16)
                wait(act, s["tok_mm"], TPG * g - TPG + t + 1)
                act.activation(x_hi[:, t, :], x_raw[:, t, :], ACT.Copy).then_inc(s["x_his"], 1)

            def scale_u(g):
                for t in range(TPG):
                    if t != 1:
                        act.wait_ge(s["coef_ready"], 2 * g + (1 if t == 0 else 2))
                    act.activation(u[:, t, :], h[:, t, :], ACT.Identity, bias=shift[:, 1, t:t + 1],
                                   scale=scale[:, 1, t:t + 1]).then_inc(s["u_ready"], 1)

            def activations_hi(g):
                for c in range(DC):
                    act.wait_ge(s["uT_mm"], DC * g + c + 1)
                    act.activation(wT_hi[:, c, :], u_bank(c), ACT.Copy).then_inc(s["w_his"], 1)

            def query_key(g, e):
                act.wait_ge(s["qk_mm"], 2 * DC * g + e + 1)
                act.activation((qT if e < DC else kT)[:, e % DC, :], turn_ps[:, e % 2, 0:GTOK], ACT.Identity,
                               bias=sb["qkv_b"][:, e:e + 1]).then_inc(s["qk_ready"], 1)

            def normalise(g, t):
                if t == 0:
                    act.wait_ge(s["coef2_ready"], g + 1)
                    wait(act, s["xf_stored"], 16 * g)
                    wait(act, s["outd_ready"], TPG * g)
                act.activation(xf[:, t, 0:D], resid[:, t, :], ACT.Identity, bias=coef2[:, 1, t:t + 1],
                               scale=coef2[:, 0, t:t + 1]).then_inc(s["xf_ready"], 1)

            def xf_turned(g):
                for c in range(DC):
                    act.wait_ge(s["xfT_mm"], DC * g + c + 1)
                    act.activation(attnT_hi[:, c, :], attn_bank(c), ACT.Copy).then_inc(s["xfT_ready"], 1)

            def gate_exponentials(g):
                act.wait_ge(s["gate_centred"], g + 1)
                act.activation(gate_exp[:], logits[:], ACT.Exp).then_inc(s["gate_exped"], 1)

            def values(g, tiles):
                for t in tiles:
                    act.wait_ge(s["v_mm"], TPG * g + t + 1)
                    act.activation(v[:, t, :], wide_ps[:, t % 2, :], ACT.Copy).then_inc(s["v_ready"], 1)

            def exponentials(g):
                act.wait_ge(s["centred"], g + 1)
                act.activation(scores[:], scores[:], ACT.Exp, scale=DH ** -0.5).then_inc(s["exped"], 1)

            def attention_hi(g, c):
                act.wait_ge(s["pv_mm"], DC * g + c + 1)
                act.activation(attnT_hi[:, c, :], attn_bank(c), ACT.Identity,
                               bias=sb["qkv_b"][:, 2 * DC + c:2 * DC + c + 1]).then_inc(s["attn_his"], 1)

            def step(i, first, last):
                for e in range(DC):
                    query_key(i, e)
                    if not first and e < TPG:
                        normalise(i - 1, e)
                for e in range(DC, 2 * DC):
                    if not last and e < DC + TPG:
                        patches_hi(i + 1, e - DC)
                    query_key(i, e)
                if not first:
                    xf_turned(i - 1)
                values(i, (0,))
                if not first:
                    gate_exponentials(i - 1)
                values(i, (1,))
                exponentials(i)
                values(i, (2,))
                for c in range(DC):
                    attention_hi(i, c)
                if not last:
                    scale_u(i + 1)
                    activations_hi(i + 1)

            for t in range(TPG):
                patches_hi(0, t)
            scale_u(0)
            activations_hi(0)
            step(0, True, False)
            with act.Fori(1, GROUPS - 1) as i:
                step(i, False, False)
            step(GROUPS - 1, False, True)
            for t in range(TPG):
                normalise(GROUPS - 1, t)
            xf_turned(GROUPS - 1)
            gate_exponentials(GROUPS - 1)

        @block.vector
        def _(dve):
            def patches_lo(g, t):
                dve.wait_ge(s["x_his"], TPG * g + t + 1)
                dve.tensor_sub(x_lo[:, t, :], x_raw[:, t, :], x_hi[:, t, :].bitcast(F32)).then_inc(s["x_los"], 1)

            def tokens(g, t):
                dve.wait_ge(s["tok_mm"], TPG * g + t + 1)
                if t == 0:
                    wait(dve, s["u_ready"], TPG * g)
                    wait(dve, s["resid_ready"], TPG * g)
                dve.tensor_add(h[:, t, :], wide_ps[:, (t + 1) % 2, :], sb["tok_b"][:]).then_inc(s["h_ready"], 1)
                dve.wait_ge(s["h_ready"], TPG * g + t + 1)
                dve.bn_stats(stats[:, t, :], h[:, t, :]).then_inc(s["stats_ready"], 1)
                if t >= 1:
                    hold_until(dve, [(s["stats_ready"], 2 * TPG * g + (2 if t == 1 else 5))], dve_passed)
                    for k in ((0, 1) if t == 1 else (2,)):
                        dve.bn_aggr(mv[:, k, :], stats[:, k, :]).then_inc(s["stats_ready"], 1)

            def activations_lo(g):
                for c in range(DC):
                    dve.wait_ge(s["w_his"], DC * g + c + 1)
                    dve.tensor_sub(wT_lo[:, c, :], u_bank(c), wT_hi[:, c, :].bitcast(F32)).then_inc(s["w_los"], 1)

            def xf_lo(g):
                for c in range(DC):
                    dve.wait_ge(s["xfT_ready"], DC * g + c + 1)
                    dve.tensor_sub(attnT_lo[:, c, :], attn_bank(c), attnT_hi[:, c, :].bitcast(F32)).then_inc(s["xfT_los"], 1)

            def gate_logits(g):
                dve.wait_ge(s["gate_mm"], g + 1)
                for q in range(QUADS):
                    rows = slice(q * IMAGES, (q + 1) * IMAGES)
                    ins = dve.transpose(halves[rows, :].rearrange("p (t b) -> p t b", t=TPG),
                                        wide_ps[0:2 * EXPERTS, 1, 0:GTOK].rearrange("p (t b) -> p t b", t=TPG)[:, :, rows])
                ins.then_inc(s["logits_read"], 1)
                dve.wait_ge(s["logits_read"], g + 1)
                sums = halves[:].rearrange("p (t a e) -> p t a e", t=TPG, a=2)
                dve.tensor_add(logits[:], sums[:, :, 0, :], sums[:, :, 1, :]).then_inc(s["logits_added"], 1)
                dve.wait_ge(s["logits_added"], 2 * g + 1)
                dve.tensor_add(logits[:], logits[:],
                               sb["gate_b"][:].unsqueeze(1).broadcast_to([P, TPG, EXPERTS])).then_inc(s["logits_added"], 1)
                dve.wait_ge(s["logits_added"], 2 * g + 2)
                dve.reduce_max(gate_max[:], logits[:], AX.X).then_inc(s["gate_maxed"], 1)
                dve.wait_ge(s["gate_maxed"], g + 1)
                dve.tensor_sub(logits[:], logits[:], gate_max[:].unsqueeze(2).broadcast_to([P, TPG, EXPERTS])).then_inc(s["gate_centred"], 1)

            def gate_choice(g):
                dve.wait_ge(s["gate_centred"], g + 1)
                dve.tensor_scalar(cand[:], logits[:], 0.0, float(EXPERTS), ALU.is_lt, ALU.mult).then_inc(s["cand_a"], 1)
                dve.wait_ge(s["cand_a"], g + 1)
                dve.tensor_add(cand[:], cand[:], sb["expert_ids"][:].unsqueeze(1).broadcast_to([P, TPG, EXPERTS])).then_inc(s["cand_b"], 1)
                dve.wait_ge(s["gate_exped"], g + 1)
                dve.reduce_sum(gate_sum[:], gate_exp[:], AX.X).then_inc(s["gate_summed"], 1)
                dve.wait_ge(s["cand_b"], g + 1)
                dve.tensor_reduce(sb["route"][:, bass.ds(TPG * g, TPG)], cand[:], axis=AX.X, op=ALU.min)
                dve.wait_ge(s["gate_summed"], g + 1)
                dve.reciprocal(xf[:, :, D:XROW], gate_sum[:].unsqueeze(2).broadcast_to([P, TPG, XROW - D])).then_inc(s["gate_p"], 1)

            def unrouted(g):
                dve.wait_ge(s["gate_p"], g + 1)
                for t in range(TPG):
                    dve.scalar_tensor_tensor(out=resid[:, t, :], in0=xf[:, t, 0:D], scalar=xf[:, t, D:D + 1],
                                             in1=resid[:, t, :], op0=ALU.mult, op1=ALU.add).then_inc(s["outd_ready"], 1)

            def position_scores(g):
                dve.wait_ge(s["bd_mm"], g + 1)
                wait(dve, s["bd_stored"], 16 * g)
                for par in range(2):
                    ins = dve.tensor_add(bd[:, par, :, :, :].rearrange("p t n r -> p t (n r)"),
                                         bd_ps[:, par, 0:GTOK].rearrange("p (t m) -> p t m", t=TPG),
                                         sb["bd_const"][:, par, :, :].rearrange("p n r -> p (n r)").unsqueeze(1)
                                         .broadcast_to([P, TPG, PAIRS * IMAGES]))
                ins.then_inc(s["bd_ready"], 1)

            def scores_max(g):
                dve.wait_ge(s["ac_mm"], g + 1)
                dve.wait_ge(s["bd_shifted"], 16 * QUADS * g + 16 * QUADS)
                dve.tensor_add(scores5, ac_ps[:, :, 0:GTOK], scores5).then_inc(s["sum_ready"], 1)
                dve.wait_ge(s["sum_ready"], g + 1)
                dve.reduce_max(row_max[:], scores[:], AX.X).then_inc(s["max_ready"], 1)

            def scores_sum(g):
                dve.wait_ge(s["exped"], g + 1)
                dve.reduce_sum(row_sum[:], scores[:], AX.X).then_inc(s["rowsum_ready"], 1)
                dve.wait_ge(s["rowsum_ready"], g + 1)
                dve.reciprocal(row_inv[:], row_sum[:]).then_inc(s["inv_ready"], 1)

            def turn_probs(g):
                dve.wait_ge(s["probs_ready"], g + 1)
                wait(dve, s["pv_mm"], DC * g)
                for q in range(QUADS):
                    rows = slice(q * IMAGES, (q + 1) * IMAGES)
                    dve.transpose(probsT[rows, :, rows], scores[rows, :, :]).then_inc(s["probsT_ready"], 1)

            def attention_lo(g):
                for c in range(DC):
                    dve.wait_ge(s["attn_his"], DC * g + c + 1)
                    dve.scalar_tensor_tensor(out=attnT_lo[:, c, :], in0=attn_bank(c),
                                             scalar=sb["qkv_b"][:, 2 * DC + c:2 * DC + c + 1],
                                             in1=attnT_hi[:, c, :].bitcast(F32), op0=ALU.add, op1=ALU.subtract
                                             ).then_inc(s["attn_los"], 1)

            def residual(g, tiles):
                for t in tiles:
                    dve.wait_ge(s["out_mm"], TPG * g + t + 1)
                    if t == 0:
                        dve.wait_ge(s["resid_ready"], TPG * g + TPG)
                    dve.tensor_add(resid[:, t, :], wide_ps[:, t % 2, :], resid[:, t, :]).then_inc(s["h2_ready"], 1)
                    dve.wait_ge(s["h2_ready"], TPG * g + t + 1)
                    dve.bn_stats(stats2[:, t, :], resid[:, t, :]).then_inc(s["stats2_ready"], 1)
                if tiles[-1] == TPG - 1:
                    hold_until(dve, [(s["stats2_ready"], 2 * TPG * g + TPG)], dve_passed)
                    for t in range(TPG):
                        dve.bn_aggr(mv2[:, t, :], stats2[:, t, :]).then_inc(s["stats2_ready"], 1)

            def step(i, first, last):
                if not last:
                    for t in range(TPG):
                        patches_lo(i + 1, t)
                position_scores(i)
                if not first:
                    xf_lo(i - 1)
                    gate_logits(i - 1)
                    gate_choice(i - 1)
                scores_max(i)
                if not first:
                    unrouted(i - 1)
                scores_sum(i)
                turn_probs(i)
                if not last:
                    tokens(i + 1, 0)
                    tokens(i + 1, 1)
                attention_lo(i)
                if not last:
                    tokens(i + 1, 2)
                residual(i, (0, 1))
                if not last:
                    activations_lo(i + 1)
                residual(i, (2,))

            for t in range(TPG):
                patches_lo(0, t)
            for t in range(TPG):
                tokens(0, t)
            activations_lo(0)
            step(0, True, False)
            with dve.Fori(1, GROUPS - 1) as i:
                step(i, False, False)
            step(GROUPS - 1, False, True)
            xf_lo(GROUPS - 1)
            gate_logits(GROUPS - 1)
            gate_choice(GROUPS - 1)
            unrouted(GROUPS - 1)

        @block.gpsimd
        def _(pool):
            def coefficients(g):
                for part, t in enumerate((slice(0, 2), slice(2, 3))):
                    done, n = 10 * g + 5 * part, t.stop - t.start
                    hold_until(pool, [(s["stats_ready"], 2 * TPG * g + 2 * t.stop)], pool_passed)
                    pool.tensor_scalar(work[:, 0, t], mv[:, t, 1], EPS, None, ALU.add).then_inc(s["coef_work"], 1)
                    pool.tensor_scalar(work[:, 1, t], mv[:, t, 1], 1.0 + EPS, EPS * EPS, ALU.mult, ALU.add).then_inc(s["coef_work"], 1)
                    pool.tensor_scalar(minus_mean[:, t], mv[:, t, 0], -1.0, None, ALU.mult).then_inc(s["coef_work"], 1)
                    pool.wait_ge(s["coef_work"], done + 3)
                    pool.tensor_tensor(scale[:, :, t], work[:, :, t], sb["half"][:, t].unsqueeze(1).broadcast_to([P, 2, n]),
                                       ALU.pow).then_inc(s["coef_work"], 1)
                    pool.wait_ge(s["coef_work"], done + 4)
                    pool.tensor_tensor(shift[:, :, t], scale[:, :, t], minus_mean[:, t].unsqueeze(1).broadcast_to([P, 2, n]),
                                       ALU.mult).then_inc(s["coef_ready"], 1)
                    pool.tensor_scalar(scale_sum[:, t], scale[:, 0, t], 1.0, None, ALU.add).then_inc(s["coef_work"], 1)

            def coefficients2(g):
                hold_until(pool, [(s["stats2_ready"], 2 * TPG * g + 2 * TPG)], pool_passed)
                pool.tensor_scalar(work2[:, 0, :], mv2[:, :, 1], EPS, None, ALU.add).then_inc(s["coef2_work"], 1)
                pool.tensor_scalar(work2[:, 1, :], mv2[:, :, 0], -1.0, None, ALU.mult).then_inc(s["coef2_work"], 1)
                pool.wait_ge(s["coef2_work"], 3 * g + 2)
                pool.tensor_tensor(coef2[:, 0, :], work2[:, 0, :], sb["half"][:], ALU.pow).then_inc(s["coef2_work"], 1)
                pool.wait_ge(s["coef2_work"], 3 * g + 3)
                pool.tensor_tensor(coef2[:, 1, :], work2[:, 1, :], coef2[:, 0, :], ALU.mult).then_inc(s["coef2_ready"], 1)

            def residual(g):
                hold_until(pool, [(s["coef_work"], 10 * g + 10), (s["outd_stored"], 32 * g)], pool_passed)
                for t in range(TPG):
                    pool.tensor_scalar(resid[:, t, :], h[:, t, :], scale_sum[:, t:t + 1], shift[:, 0, t:t + 1],
                                       ALU.mult, ALU.add).then_inc(s["resid_ready"], 1)

            def centre(g):
                pool.wait_ge(s["max_ready"], g + 1)
                pool.tensor_sub(scores[:], scores[:], row_max[:].unsqueeze(2).broadcast_to([P, BLOCKS, IMAGES])).then_inc(s["centred"], 1)

            def probabilities(g):
                pool.wait_ge(s["inv_ready"], g + 1)
                pool.tensor_mul(scores[:], scores[:], row_inv[:].unsqueeze(2).broadcast_to([P, BLOCKS, IMAGES])).then_inc(s["probs_ready"], 1)

            def step(i, first, last):
                if not first:
                    coefficients2(i - 1)
                centre(i)
                probabilities(i)
                residual(i)
                if not last:
                    coefficients(i + 1)

            coefficients(0)
            step(0, True, False)
            with pool.Fori(1, GROUPS - 1) as i:
                step(i, False, False)
            step(GROUPS - 1, False, True)
            coefficients2(GROUPS - 1)

        @block.sync
        def _(sp):
            shift_in = io["shift"].rearrange("(k p r) -> p k r", k=BLOCKS, r=PADDED)[:, :, 1:PADDED]

            def load_patches(g, t):
                if not isinstance(g, int) or g > 0:
                    hold_until(sp, [(s["x_los"], TPG * g - TPG + t + 1)], sp_passed)
                sp.dma_start(x_raw[:, t, :], io["patches"][bass.ds(TPG * g + t, 1), :, :].rearrange("a p n -> p (a n)")
                             ).then_inc(x_loaded[t], 16)

            def store_normed(g):
                hold_until(sp, [(s["gate_p"], g + 1)], sp_passed)
                sp.dma_start(io["rows"][bass.ds(GTOK * g, GTOK), 0:XROW].rearrange("(t p) n -> p t n", p=P),
                             xf[:]).then_inc(s["xf_stored"], 16)

            def store_unrouted(g):
                hold_until(sp, [(s["outd_ready"], TPG * g + TPG)], sp_passed)
                sp.dma_start(io["out"][bass.ds(GTOK * g, GTOK), :].rearrange("(t p) n -> p t n", p=P),
                             resid[:]).then_inc(s["outd_stored"], 16)
                sp.dma_start(io["rows"][bass.ds(GTOK * g, GTOK), XROW:ROW].rearrange("(t p) n -> p t n", p=P),
                             resid[:]).then_inc(s["outd_stored"], 16)

            def shift(g):
                hold_until(sp, [(s["bd_ready"], g + 1)], sp_passed)
                sp.dma_start(shift_in, bd[:].rearrange("p a t n r -> p (a t n) r")).then_inc(s["bd_stored"], 16)
                hold_until(sp, [(s["bd_stored"], 16 * g + 16)], sp_passed)
                for q in range(QUADS):
                    src = io["shift"].rearrange("(k q m) -> k q m", k=BLOCKS, q=QUADS)[:, q, IMAGES:]
                    sp.dma_start(scores[q * IMAGES:(q + 1) * IMAGES, :, :],
                                 src.rearrange("k (i j) -> i k j", j=IMAGES)).then_inc(s["bd_shifted"], 16)

            def step(i, first, load):
                if load:
                    for t in range(TPG):
                        load_patches(i + 2, t)
                shift(i)
                if not first:
                    store_normed(i - 1)
                    store_unrouted(i - 1)

            for g in range(2):
                for t in range(TPG):
                    load_patches(g, t)
            step(0, True, True)
            with sp.Fori(1, GROUPS - 2) as i:
                step(i, False, True)
            step(GROUPS - 2, False, False)
            step(GROUPS - 1, False, False)
            store_normed(GROUPS - 1)
            store_unrouted(GROUPS - 1)
            sp.wait_ge(s["xf_stored"], 16 * GROUPS)
            sp.wait_ge(s["outd_stored"], 32 * GROUPS)


def place(nc, io, sb):
    ctx = ExitStack()
    with ctx:
        def buf(name, shape, dt=F32):
            return ctx.enter_context(nc.sbuf_tensor(name, shape, dt))

        def sem(name):
            return ctx.enter_context(nc.semaphore(name))

        chosen = buf("chosen", [P, EXPERTS, TILES])
        resets = buf("resets", [P, EXPERTS, TILES])
        counts = buf("counts", [P, EXPERTS, TILES])
        totals = buf("totals", [P, EXPERTS])
        before = buf("before", [P, EXPERTS])
        earlier = buf("earlier", [P, P])
        slot_ids_f = buf("slot_ids_f", [P, SLOT_TILES])
        lane_ids_f = buf("lane_ids_f", [P, P])
        slot_ids = buf("slot_ids", [P, SLOT_TILES], BF16)
        lane_ids = buf("lane_ids", [P, P], BF16)
        tile_no = buf("tile_no", [P, TILES])
        lane_no = buf("lane_no", [P, 1])
        pos = buf("pos", [P, TILES])
        pos_i = buf("pos_i", [P, TILES], I32)
        hi_i = buf("hi_i", [P, TILES], I32)
        lane_i = buf("lane_i", [P, TILES], I32)
        over = buf("over", [P, TILES])
        slot_tile = buf("slot_tile", [P, TILES])
        slot_lane = buf("slot_lane", [P, TILES])
        RING = 4
        lane_hot = buf("lane_hot", [P, RING, P], BF16)
        slot_hot = buf("slot_hot", [P, RING, 2, SLOT_TILES], BF16)
        empty = buf("empty", [P, SLOT_TILES])
        index_f = buf("index_f", [P, SLOT_TILES])
        base_ps = ctx.enter_context(nc.psum_tensor("base_ps", [P, D], F32))
        table_ps = ctx.enter_context(nc.psum_tensor("table_ps", [P, D], F32))
        consts_in, chain, total_ready, base_mm, hot, table_mm = (
            sem(n) for n in ("consts_in", "chain", "total_ready", "base_mm", "hot", "table_mm"))
        block = ctx.enter_context(nc.Block())

        @block.sync
        def _(sp):
            for dst, src in ((earlier, "earlier"), (slot_ids_f, "slot_ids"), (lane_ids_f, "lane_ids"),
                             (tile_no, "tile_no"), (lane_no, "lane_no")):
                sp.dma_start(dst[:], io[src]).then_inc(consts_in, 16)

        @block.tensor
        def _(pe):
            pe.wait_ge(total_ready, 1)
            pe.wait_ge(consts_in, 80)
            pe.matmul(base_ps[:, 0:EXPERTS], earlier[:], totals[:], start=True, stop=True).then_inc(base_mm, 1)

            def add(tile, ring, first, last):
                pe.wait_ge(hot, tile + 1)
                pe.matmul(table_ps[:, 0:2 * SLOT_TILES], lane_hot[:, ring, :],
                          slot_hot[:, ring, :, :].rearrange("p a n -> p (a n)"), start=first, stop=last
                          ).then_inc(table_mm, 1)

            for r in range(RING):
                add(r, r, r == 0, False)
            with pe.Fori(1, TILES // RING - 1) as i:
                for r in range(RING):
                    add(RING * i + r, r, False, False)
            for r in range(RING):
                add(TILES - RING + r, r, False, r == RING - 1)

        @block.vector
        def _(dve):
            done = [0]

            def link(ins):
                done[0] += 1
                ins.then_inc(chain, 1)
                dve.wait_ge(chain, done[0])

            link(dve.tensor_tensor(chosen[:], sb["route"][:].unsqueeze(1).broadcast_to([P, EXPERTS, TILES]),
                                   sb["expert_ids"][:].unsqueeze(2).broadcast_to([P, EXPERTS, TILES]), ALU.is_equal))
            link(dve.memset(resets[:], 1.0))
            link(dve.memset(resets[:, :, 0:1], 0.0))
            link(dve.tensor_tensor_scan(counts[:].rearrange("p e t -> p (e t)"), resets[:].rearrange("p e t -> p (e t)"),
                                        chosen[:].rearrange("p e t -> p (e t)"), 0.0, ALU.mult, ALU.add))
            dve.tensor_copy(totals[:].unsqueeze(2), counts[:, :, TILES - 1:TILES]).then_inc(total_ready, 1)
            dve.wait_ge(base_mm, 1)
            link(dve.tensor_copy(before[:], base_ps[:, 0:EXPERTS]))
            link(dve.tensor_add(counts[:], counts[:], before[:].unsqueeze(2).broadcast_to([P, EXPERTS, TILES])))
            link(dve.tensor_mul(counts[:], counts[:], chosen[:]))
            link(dve.reduce_sum(pos[:], counts[:].rearrange("p e t -> p t e"), AX.X))
            link(dve.tensor_scalar(pos[:], pos[:], -1.0, None, ALU.add))
            link(dve.tensor_copy(pos_i[:], pos[:]))
            link(dve.tensor_scalar(hi_i[:], pos_i[:], 7, None, ALU.arith_shift_right))
            link(dve.tensor_scalar(lane_i[:], pos_i[:], P - 1, None, ALU.bitwise_and))
            link(dve.tensor_copy(slot_tile[:], hi_i[:]))
            link(dve.tensor_copy(slot_lane[:], lane_i[:]))
            link(dve.scalar_tensor_tensor(out=slot_tile[:], in0=sb["route"][:], scalar=float(TPE), in1=slot_tile[:],
                                          op0=ALU.mult, op1=ALU.add))
            link(dve.tensor_scalar(over[:], pos[:], float(CAPACITY), 4096.0, ALU.is_ge, ALU.mult))
            link(dve.tensor_add(slot_tile[:], slot_tile[:], over[:]))
            dve.wait_ge(consts_in, 80)
            link(dve.tensor_copy(slot_ids[:], slot_ids_f[:]))
            link(dve.tensor_copy(lane_ids[:], lane_ids_f[:]))

            def one_hot(tile, ring, first):
                if not first:
                    dve.wait_ge(table_mm, tile - RING + 1)
                col = bass.ds(tile, 1)
                dve.tensor_scalar(lane_hot[:, ring, :], lane_ids[:], slot_lane[:, col], None, ALU.is_equal)
                dve.tensor_scalar(slot_hot[:, ring, 0, :], slot_ids[:], slot_tile[:, col], tile_no[:, col],
                                  ALU.is_equal, ALU.mult)
                dve.tensor_scalar(slot_hot[:, ring, 1, :], slot_ids[:], slot_tile[:, col], lane_no[:],
                                  ALU.is_equal, ALU.mult).then_inc(hot, 1)

            for r in range(RING):
                one_hot(r, r, True)
            with dve.Fori(1, TILES // RING) as i:
                for r in range(RING):
                    one_hot(RING * i + r, r, False)
            dve.wait_ge(table_mm, TILES)
            link(dve.tensor_scalar(empty[:], table_ps[:, 0:SLOT_TILES], 0.0, float(DUMP + P), ALU.is_equal, ALU.mult))
            link(dve.tensor_scalar(index_f[:], table_ps[:, 0:SLOT_TILES], float(P), float(-P), ALU.mult, ALU.add))
            link(dve.tensor_add(index_f[:], index_f[:], table_ps[:, SLOT_TILES:2 * SLOT_TILES]))
            link(dve.tensor_add(index_f[:], index_f[:], empty[:]))
            link(dve.tensor_scalar(empty[:], table_ps[:, 0:SLOT_TILES], 0.0, lane_no[:], ALU.is_equal, ALU.mult))
            link(dve.tensor_add(index_f[:], index_f[:], empty[:]))
            link(dve.tensor_copy(sb["index"][:], index_f[:]))


def experts(nc, io, sb):
    ctx = ExitStack()
    with ctx:
        def buf(name, shape, dt=F32):
            return ctx.enter_context(nc.sbuf_tensor(name, shape, dt))

        def sem(name):
            return ctx.enter_context(nc.semaphore(name))

        RING = TPE
        AHEAD = RING // 2
        PAIR = 2 * TPE
        STEPS = EXPERTS // 2
        w_raw = buf("w_raw", [P, 2, DC, D])
        w_hi = buf("ew_hi", [P, 2, DC, D], F32R)
        w_lo = buf("ew_lo", [P, 2, DC, D], F32R)
        bias = buf("ebias", [P, 2, D])
        rows = buf("rows_sb", [P, RING, ROW])
        now = buf("now", [P, RING], I32)
        xT_hi = buf("xT_hi", [P, 2, DC * P], F32R)
        xT_lo = buf("xT_lo", [P, 2, DC * P], F32R)
        turn = ctx.enter_context(nc.psum_tensor("turn", [P, 2, D], F32))
        prod = ctx.enter_context(nc.psum_tensor("prod", [P, 2, D], F32))
        w_in = [sem(f"w_in{r}") for r in range(2)]
        sp_passed = sem("sp_passed2")
        gathered = [sem(f"gathered{r}") for r in range(RING)]
        scattered = [sem(f"scattered{r}") for r in range(RING)]
        index_now, passed, w_his, w_los, xT_mm, xT_his, xT_los, y_mm, y_biased, y_gap, result_ready = (
            sem(n) for n in "index_now pool_passed2 ew_his ew_los xT_mm xT_his xT_los y_mm y_biased y_gap result_ready".split())
        block = ctx.enter_context(nc.Block())
        ident = sb["ident"]

        @block.sync
        def _(sp):
            def load(i, half):
                if not isinstance(i, int) or i > 0:
                    hold_until(sp, [(w_los, DC * (2 * i + half - 1))], sp_passed)
                sp.dma_start(w_raw[:, half, :, :], io["expert_wT"][bass.ds(2 * i + half, 1), :, :, :]
                             .rearrange("a p c n -> p (a c) n")).then_inc(w_in[half], 16)
                if not isinstance(i, int) or i > 0:
                    hold_until(sp, [(y_biased, PAIR * i - PAIR + TPE * (half + 1))], sp_passed)
                sp.dma_start(bias[:, half, :], io["expert_b"][bass.ds(2 * i + half, 1), :].broadcast_to([P, D])
                             ).then_inc(w_in[half], 16)

            load(0, 0)
            load(0, 1)
            with sp.Fori(1, STEPS) as i:
                load(i, 0)
                load(i, 1)

        @block.scalar
        def _(act):
            def split(i, half, c):
                if c == 0:
                    act.wait_ge(w_in[half], 32 * i + 32)
                    wait(act, y_mm, PAIR * i - PAIR + TPE * (half + 1))
                act.activation(w_hi[:, half, c, :], w_raw[:, half, c, :], ACT.Copy).then_inc(w_his, 1)

            def rows_hi(i, k):
                act.wait_ge(xT_mm, PAIR * i + k + 1)
                act.activation(xT_hi[:, k % 2, :], turn[:, k % 2, :], ACT.Copy).then_inc(xT_his, 1)

            def step(i, last):
                for k in range(PAIR):
                    rows_hi(i, k)
                    if 2 <= k < 2 + DC:
                        split(i, 1, k - 2)
                    elif TPE + 2 <= k < TPE + 2 + DC and not last:
                        split(i + 1, 0, k - TPE - 2)

            for c in range(DC):
                split(0, 0, c)
            step(0, False)
            with act.Fori(1, STEPS - 1) as i:
                step(i, False)
            step(STEPS - 1, True)

        @block.vector
        def _(dve):
            def split(i, half, c):
                dve.wait_ge(w_his, DC * (2 * i + half) + c + 1)
                dve.tensor_sub(w_lo[:, half, c, :], w_raw[:, half, c, :], w_hi[:, half, c, :].bitcast(F32)).then_inc(w_los, 1)

            def rows_lo(i, k):
                dve.wait_ge(xT_his, PAIR * i + k + 1)
                dve.tensor_sub(xT_lo[:, k % 2, :], turn[:, k % 2, :], xT_hi[:, k % 2, :].bitcast(F32)).then_inc(xT_los, 1)

            def finish(i, k):
                n, row = PAIR * i + k, rows[:, k % RING, :]
                dve.wait_ge(y_mm, n + 1)
                gap = prod[:, k % 2, :]
                dve.tensor_sub(row[:, 0:D], bias[:, k // TPE, :], row[:, 0:D]).then_inc(y_gap, 1)
                dve.wait_ge(y_gap, n + 1)
                dve.tensor_add(row[:, 0:D], gap, row[:, 0:D]).then_inc(y_biased, 1)
                dve.wait_ge(y_biased, n + 1)
                dve.scalar_tensor_tensor(out=row[:, XROW:ROW], in0=row[:, 0:D], scalar=row[:, D:D + 1],
                                         in1=row[:, XROW:ROW], op0=ALU.mult, op1=ALU.add).then_inc(result_ready, 1)

            def step(i, last):
                for k in range(PAIR):
                    if k + 1 < PAIR:
                        rows_lo(i, k + 1)
                    elif not last:
                        rows_lo(i + 1, 0)
                    finish(i, k)
                    if 2 <= k < 2 + DC:
                        split(i, 1, k - 2)
                    elif TPE + 2 <= k < TPE + 2 + DC and not last:
                        split(i + 1, 0, k - TPE - 2)

            for c in range(DC):
                split(0, 0, c)
            rows_lo(0, 0)
            step(0, False)
            with dve.Fori(1, STEPS - 1) as i:
                step(i, False)
            step(STEPS - 1, True)

        @block.tensor
        def _(pe):
            def turn_rows(i, k):
                pe.wait_ge(gathered[k % RING], 16 * (2 * i + k // RING) + 16)
                wait(pe, xT_los, PAIR * i + k - 1)
                for c in range(DC):
                    last = pe.transpose(turn[:, k % 2, c * P:(c + 1) * P], rows[:, k % RING, c * P:(c + 1) * P], ident[:])
                last.then_inc(xT_mm, 1)

            def multiply(i, k):
                half = k // TPE
                if k % TPE == 0:
                    pe.wait_ge(w_los, DC * (2 * i + half) + DC)
                pe.wait_ge(xT_los, PAIR * i + k + 1)
                wait(pe, y_biased, PAIR * i + k - 1)
                for c in range(DC):
                    hi, lo = (x[:, k % 2, c * P:(c + 1) * P] for x in (xT_hi, xT_lo))
                    pe.matmul(prod[:, k % 2, :], hi, w_hi[:, half, c, :], start=c == 0, stop=False)
                    pe.matmul(prod[:, k % 2, :], hi, w_lo[:, half, c, :], start=False, stop=False)
                    last = pe.matmul(prod[:, k % 2, :], lo, w_hi[:, half, c, :], start=False, stop=c == DC - 1)
                last.then_inc(y_mm, 1)

            def step(i, last):
                for k in range(PAIR):
                    if k + 1 < PAIR:
                        turn_rows(i, k + 1)
                    elif not last:
                        turn_rows(i + 1, 0)
                    multiply(i, k)

            turn_rows(0, 0)
            step(0, False)
            with pe.Fori(1, STEPS - 1) as i:
                step(i, False)
            step(STEPS - 1, True)

        @block.gpsimd
        def _(pool):
            def gather(i, k):
                slot = k % RING
                hold_until(pool, [(scattered[slot], 16 * (2 * i + k // RING))], passed)
                pool.tensor_copy(now[:, slot:slot + 1], sb["index"][:, bass.ds(PAIR * i + k, 1)]).then_inc(index_now, 1)
                hold_until(pool, [(index_now, PAIR * i + k + 1)], passed)
                pool.indirect_dma_start(rows[:, slot, :], None, io["rows"],
                                        bass.IndirectOffsetOnAxis(ap=now[:, slot:slot + 1], axis=0)).then_inc(gathered[slot], 16)

            def scatter(i, k):
                slot = k % RING
                hold_until(pool, [(result_ready, PAIR * i + k + 1)], passed)
                pool.indirect_dma_start(io["out"], bass.IndirectOffsetOnAxis(ap=now[:, slot:slot + 1], axis=0),
                                        rows[:, slot, XROW:ROW], None, bounds_check=TOKENS - 1, oob_is_err=False
                                        ).then_inc(scattered[slot], 16)

            def step(i, last):
                for k in range(PAIR):
                    if k + AHEAD < PAIR or not last:
                        gather(i, k + AHEAD)
                    scatter(i, k)

            for k in range(AHEAD):
                gather(0, k)
            step(0, False)
            with pool.Fori(1, STEPS - 1) as i:
                step(i, False)
            step(STEPS - 1, True)
            for slot in range(RING):
                pool.wait_ge(scattered[slot], 16 * 2 * STEPS)


def build(nc, io):
    with ExitStack() as whole:
        sb = {}

        def hold(ctx, name, shape, dt=F32):
            sb[name] = ctx.enter_context(nc.sbuf_tensor(f"{name}_sb", shape, dt))

        hold(whole, "ident", [P, P])
        hold(whole, "expert_ids", [P, EXPERTS])
        hold(whole, "route", [P, TILES])
        hold(whole, "index", [P, SLOT_TILES], I32)
        with ExitStack() as first:
            for name, cols in (("tok", D * KC), ("qkv", 3 * D * DC), ("out", D * DC)):
                chunks = KC if name == "tok" else DC
                hold(first, f"{name}_hi", [P, chunks, cols // chunks], F32R)
                hold(first, f"{name}_lo", [P, chunks, cols // chunks], F32R)
            hold(first, "rk", [P, PAIRS, IMAGES])
            hold(first, "bd_const", [P, 2, PAIRS, IMAGES])
            hold(first, "qkv_b", [P, 3 * DC])
            hold(first, "tok_b", [P, D])
            hold(first, "gate_w", [P, DC, 2, EXPERTS], F32R)
            hold(first, "gate_b", [P, EXPERTS])
            hold(first, "half", [P, TPG])
            hold(first, "probsT", [P, BLOCKS, P])
            prepare(nc, io, sb)
            tower(nc, io, sb)
        place(nc, io, sb)
        experts(nc, io, sb)


def constants():
    f32 = np.float32
    lane = np.arange(P)
    image, quad = lane % IMAGES, lane // IMAGES
    order = image * QUADS + quad
    place_in = np.arange(IMAGES - 1, -1, -1, dtype=f32)
    inv = (1.0 / np.power(f32(10000.0), np.arange(0, D, 2, dtype=f32) / f32(D))).astype(f32)
    angle = place_in[:, None] * inv[None, :]
    sinusoid = np.concatenate([np.sin(angle), np.cos(angle)], axis=-1).astype(f32)
    spread = lambda row, dt: np.ascontiguousarray(np.broadcast_to(row, (P, len(row)))).astype(dt)
    return {
        "ident": np.eye(P, dtype=f32),
        "sinusoid": np.ascontiguousarray(sinusoid.T.reshape(DC, P, IMAGES).transpose(1, 0, 2)),
        "expert_ids": spread(np.arange(EXPERTS), f32),
        "earlier": (order[:, None] < order[None, :]).astype(f32),
        "slot_ids": spread(np.arange(SLOT_TILES), f32),
        "lane_ids": spread(lane, f32),
        "tile_no": spread(np.arange(1, TILES + 1), f32),
        "lane_no": lane.astype(f32)[:, None],
    }


def kernel(**inputs):
    import concourse.bacc as bacc
    from concourse.bass_utils import run_bass_kernel_spmd

    a = {k: np.asarray(v) for k, v in inputs.items()}
    n = SIDE // PATCH
    x = a["x"].reshape(IMAGES, CHANNELS, n, PATCH, n, PATCH).transpose(2, 4, 1, 3, 5, 0)
    x = x.reshape(QUADS, TILES, KC, P, IMAGES).transpose(1, 3, 2, 0, 4).reshape(TILES, P, KC * P)

    def chunked(w):
        out, inn = w.shape
        return np.ascontiguousarray(w.T.reshape(inn // P, P, out).transpose(1, 0, 2))

    def spread(row):
        return np.ascontiguousarray(np.broadcast_to(row, (P, row.size)))

    def columns(row):
        return np.ascontiguousarray(row.reshape(-1, P).T)

    arrays = {
        "patches": np.ascontiguousarray(x),
        "tok_wT": chunked(a["L0_tok_w"]),
        "tok_b": spread(a["L0_tok_b"]),
        "qkv_wT": chunked(a["L0_attn_Wqkv"]),
        "wr_wT": chunked(a["L0_attn_Wr"]),
        "out_wT": chunked(a["L0_attn_Wo"]),
        "gamma": columns(a["L0_attn_ln_gamma"]),
        "beta": columns(a["L0_attn_ln_beta"]),
        "r_w_bias": columns(a["L0_attn_r_w_bias"]),
        "r_r_bias": columns(a["L0_attn_r_r_bias"]),
        "gate_wT": chunked(a["L0_ffn_switch_w"]),
        "gate_b": spread(a["L0_ffn_switch_b"]),
        "expert_wT": np.ascontiguousarray(a["L0_ffn_expert_w"].transpose(0, 2, 1).reshape(EXPERTS, DC, P, D).transpose(0, 2, 1, 3)),
        "expert_b": a["L0_ffn_expert_b"],
        **constants(),
    }
    nc = bacc.Bacc("TRN2", target_bir_lowering=False, num_devices=1)
    io = {k: nc.dram_tensor(f"in_{k}", v.shape, mybir.dt.from_np(v.dtype), kind="ExternalInput").ap() for k, v in arrays.items()}
    io["out"] = nc.dram_tensor("out_rows", (TOKENS, D), F32, kind="ExternalOutput").ap()
    io["rows"] = nc.dram_tensor("token_rows", (TOKENS + P, ROW), F32, kind="Internal").ap()
    io["shift"] = nc.dram_tensor("shift_scratch", (BLOCKS * BLOCK_STRIDE,), F32, kind="Internal").ap()
    build(nc, io)
    done = run_bass_kernel_spmd(nc, [{f"in_{k}": v for k, v in arrays.items()}], core_ids=[0])
    out = np.asarray(done.results[0]["out_rows"])
    return out.reshape(TILES, QUADS, IMAGES, D).transpose(2, 1, 0, 3).reshape(IMAGES, POSITIONS, D)
```

```python
from contextlib import ExitStack

import numpy as np

import concourse.bass as bass
from concourse import mybir

P = 128
IMAGES, CHANNELS, SIDE, PATCH = 32, 3, 384, 16
POSITIONS = (SIDE // PATCH) ** 2
QUADS = P // IMAGES
TILES = POSITIONS // QUADS
TPG = 3
GROUPS = TILES // TPG
GTOK = TPG * P
D = 512
DC = D // P
KC = CHANNELS * PATCH * PATCH // P
HEADS, DH = 8, 64
PAIRS = HEADS // 2
BLOCKS = 2 * TPG * PAIRS
EXPERTS = 16
TOKENS = IMAGES * POSITIONS
CAPACITY = int(1.2 * TOKENS / EXPERTS)
TPE = -(-CAPACITY // P)
SLOT_TILES = EXPERTS * TPE
ROW_SLOTS = TPE
XROW = D + 4
ROW = XROW + D
EPS = 1e-5
PADDED = IMAGES + 1
SHIFT_ROW = PADDED * BLOCKS

F32, F32R, I32 = mybir.dt.float32, mybir.dt.float32r, mybir.dt.int32
ALU, ACT, AX = mybir.AluOpType, mybir.ActivationFunctionType, mybir.AxisListType


def wait(eng, sem, value):
    if not isinstance(value, int) or value > 0:
        eng.wait_ge(sem, value)


def hold_until(eng, waits, passed):
    for sem, value in waits:
        if not isinstance(value, int) or value > 0:
            eng.wait_ge(sem, value)
            eng.sem_inc(passed, 1)


def prepare(nc, io, sb):
    ctx = ExitStack()
    with ctx:
        def buf(name, shape, dt=F32):
            return ctx.enter_context(nc.sbuf_tensor(name, shape, dt))

        def sem(name):
            return ctx.enter_context(nc.semaphore(name))

        tok_raw = buf("tok_raw", [P, KC, D])
        qkv_raw = buf("qkv_raw", [P, DC, 3 * D])
        out_raw = buf("out_raw", [P, DC, D])
        wr_raw = buf("wr_raw", [P, DC, D])
        gate_raw = buf("gate_raw", [P, DC, EXPERTS])
        sinusoid = buf("sinusoid", [P, DC, IMAGES])
        gamma = buf("gamma", [P, DC])
        beta = buf("beta", [P, DC])
        w_bias = buf("w_bias", [P, PAIRS])
        r_bias = buf("r_bias", [P, PAIRS])
        bias_gap = buf("bias_gap", [P, PAIRS])
        gap_cols = buf("gap_cols", [P, PAIRS, P])
        zeros = buf("zeros", [P, SHIFT_ROW])
        proj_ps = ctx.enter_context(nc.psum_tensor("proj_ps", [P, 2, D], F32))
        gap_ps = ctx.enter_context(nc.psum_tensor("gap_ps", [P, 2, D], F32))
        tok_in, out_in, small_in, wr_in = (sem(f"{n}_in") for n in ("tok", "out", "small", "wr"))
        qkv_in = [sem(f"qkv_in{c}") for c in range(DC)]
        zeros_set, zeros_out, his, los = (sem(n) for n in ("zeros_set", "zeros_out", "his", "los"))
        beta_summed, projected, rk_ready, gap_ready, gap_mm, prep_done, zeroed = (
            sem(n) for n in ("beta_summed", "projected", "rk_ready", "gap_ready", "gap_mm", "prep_done", "zeroed"))
        block = ctx.enter_context(nc.Block())

        @block.sync
        def _(sp):
            for dst, src in ((gamma, "gamma"), (beta, "beta"), (w_bias, "r_w_bias"), (r_bias, "r_r_bias"),
                             (sinusoid, "sinusoid"), (sb["ident"], "ident"), (sb["tok_b"], "tok_b"),
                             (gate_raw, "gate_wT"), (sb["gate_b"], "gate_b"), (sb["expert_ids"], "expert_ids")):
                sp.dma_start(dst[:], io[src]).then_inc(small_in, 16)
            sp.dma_start(wr_raw[:], io["wr_wT"]).then_inc(wr_in, 16)
            for c in range(DC):
                sp.dma_start(qkv_raw[:, c, :], io["qkv_wT"][:, c, :]).then_inc(qkv_in[c], 16)
            sp.dma_start(tok_raw[:], io["tok_wT"]).then_inc(tok_in, 16)
            sp.dma_start(out_raw[:], io["out_wT"]).then_inc(out_in, 16)
            sp.wait_ge(zeros_set, 1)
            sp.dma_start(io["shift"].rearrange("(p n) -> p n", p=P),
                         zeros[:]).then_inc(zeros_out, 16)
            for t in range(TPG):
                sp.dma_start(sb["x_raw"][:, t, :], io["patches"][t, :, :]).then_inc(sb["x_loaded"][t], 16)
            sp.wait_ge(zeros_out, 16)

        @block.scalar
        def _(act):
            act.wait_ge(small_in, 160)
            for c in range(DC):
                act.wait_ge(qkv_in[c], 16)
                act.activation(sb["qkv_hi"][:, c, :], qkv_raw[:, c, :], ACT.Copy, scale=gamma[:, c:c + 1]).then_inc(his, 1)
            act.wait_ge(tok_in, 16)
            for c in range(KC):
                act.activation(sb["tok_hi"][:, c, :], tok_raw[:, c, :], ACT.Copy).then_inc(his, 1)
            act.wait_ge(out_in, 16)
            for c in range(DC):
                act.activation(sb["out_hi"][:, c, :], out_raw[:, c, :], ACT.Copy).then_inc(his, 1)

        @block.vector
        def _(dve):
            dve.wait_ge(small_in, 160)
            dve.tensor_sub(bias_gap[:], r_bias[:], w_bias[:]).then_inc(prep_done, 1)
            dve.tensor_copy(sb["gate_w"][:, :, 0, :], gate_raw[:]).then_inc(prep_done, 1)
            dve.wait_ge(prep_done, 2)
            dve.tensor_sub(sb["gate_w"][:, :, 1, :], gate_raw[:], sb["gate_w"][:, :, 0, :].bitcast(F32)).then_inc(prep_done, 1)
            dve.tensor_copy(gap_cols[:], bias_gap[:].unsqueeze(2).broadcast_to([P, PAIRS, P])).then_inc(gap_ready, 1)
            dve.wait_ge(projected, 1)
            dve.wait_ge(zeroed, 4)
            for par in range(2):
                rows = slice(par * DH, (par + 1) * DH)
                dve.tensor_copy(sb["rk"][rows, :, par, :], proj_ps[rows, 1, 0:DC * IMAGES].rearrange("p (c r) -> p c r", c=DC)
                                ).then_inc(rk_ready, 1)
            for c in range(DC):
                dve.wait_ge(his, c + 1)
                dve.scalar_tensor_tensor(out=sb["qkv_lo"][:, c, :], in0=qkv_raw[:, c, :], scalar=gamma[:, c:c + 1],
                                         in1=sb["qkv_hi"][:, c, :].bitcast(F32), op0=ALU.mult, op1=ALU.subtract).then_inc(los, 1)
            for c in range(KC):
                dve.wait_ge(his, DC + c + 1)
                dve.tensor_sub(sb["tok_lo"][:, c, :], tok_raw[:, c, :], sb["tok_hi"][:, c, :].bitcast(F32)).then_inc(los, 1)
            dve.wait_ge(gap_mm, 1)
            for par in range(2):
                dve.tensor_copy(sb["bd_const"][:, :, par, :], gap_ps[:, par, 0:PAIRS * IMAGES].rearrange("p (c r) -> p c r", c=PAIRS)
                                ).then_inc(prep_done, 1)
            for c in range(DC):
                dve.wait_ge(his, KC + DC + c + 1)
                dve.tensor_sub(sb["out_lo"][:, c, :], out_raw[:, c, :], sb["out_hi"][:, c, :].bitcast(F32)).then_inc(los, 1)
            dve.wait_ge(projected, 2)
            dve.reduce_sum(sb["qkv_b"][:], proj_ps[:, 0, 0:3 * DC * DC].rearrange("p (e c) -> p e c", c=DC), AX.X).then_inc(beta_summed, 1)
            dve.wait_ge(beta_summed, 1)
            dve.tensor_add(sb["qkv_b"][:, 0:DC], sb["qkv_b"][:, 0:DC], w_bias[:]).then_inc(prep_done, 1)

        @block.gpsimd
        def _(pool):
            pool.memset(zeros[:], 0.0).then_inc(zeros_set, 1)
            pool.memset(sb["half"][:], -0.5).then_inc(zeroed, 1)
            pool.memset(sb["rk"][:], 0.0).then_inc(zeroed, 1)
            pool.memset(sb["kT"][:], 0.0).then_inc(zeroed, 1)
            pool.memset(sb["probsT"][:], 0.0).then_inc(zeroed, 1)

        @block.tensor
        def _(pe):
            def multiply(out, weights, x, first, last):
                for q in range(QUADS):
                    cols = slice(q * IMAGES, (q + 1) * IMAGES)
                    ins = pe.matmul(out[cols], weights[:, cols], x, start=first, stop=last)
                return ins

            pe.wait_ge(small_in, 160)
            pe.wait_ge(wr_in, 16)
            for e in range(DC):
                for c in range(DC):
                    last = multiply(proj_ps[:, 1, e * IMAGES:(e + 1) * IMAGES], wr_raw[:, c, e * P:(e + 1) * P],
                                    sinusoid[:, c, :], c == 0, c == DC - 1)
            last.then_inc(projected, 1)
            pe.wait_ge(gap_ready, 1)
            pe.wait_ge(rk_ready, 2)
            for par in range(2):
                rows = slice(par * DH, (par + 1) * DH)
                for n in range(PAIRS):
                    last = multiply(gap_ps[:, par, n * IMAGES:(n + 1) * IMAGES], gap_cols[rows, n, :],
                                    sb["rk"][rows, n, par, :], True, True)
            last.then_inc(gap_mm, 1)
            for c in range(DC):
                pe.wait_ge(qkv_in[c], 16)
                for e in range(3 * DC):
                    last = multiply(proj_ps[:, 0, e * DC + c:e * DC + c + 1], qkv_raw[:, c, e * P:(e + 1) * P],
                                    beta[:, c:c + 1], True, True)
            last.then_inc(projected, 1)


def tower(nc, io, sb):
    ctx = ExitStack()
    with ctx:
        def buf(name, shape, dt=F32):
            return ctx.enter_context(nc.sbuf_tensor(name, shape, dt))

        def sem(name):
            return ctx.enter_context(nc.semaphore(name))

        x_raw = sb["x_raw"]
        x_hi = buf("x_hi", [P, TPG, KC * P], F32R)
        x_lo = buf("x_lo", [P, TPG, KC * P], F32R)
        h = buf("h", [P, TPG, D])
        u = buf("u", [P, TPG, D])
        resid = sb["resid"]
        xf = sb["xf"]
        wT_hi = buf("wT_hi", [P, DC, GTOK], F32R)
        wT_lo = buf("wT_lo", [P, DC, GTOK], F32R)
        qT = buf("qT", [P, PAIRS, GTOK])
        kT = sb["kT"]
        v = u
        bd = buf("bd", [P, IMAGES, BLOCKS])
        scores = buf("scores", [P, BLOCKS, IMAGES])
        row_max = buf("row_max", [P, BLOCKS])
        row_sum = buf("row_sum", [P, BLOCKS])
        row_inv = buf("row_inv", [P, BLOCKS])
        probsT = sb["probsT"]
        attnT_hi = buf("attnT_hi", [P, DC, GTOK], F32R)
        attnT_lo = buf("attnT_lo", [P, DC, GTOK], F32R)
        stats = buf("stats", [P, TPG, 6])
        mv = buf("mv", [P, TPG, 2])
        stats2 = buf("stats2", [P, TPG, 6])
        mv2 = buf("mv2", [P, TPG, 2])
        work = buf("work", [P, 2, TPG])
        minus_mean = buf("minus_mean", [P, TPG])
        scale = buf("scale", [P, 2, TPG])
        shift = buf("shift", [P, 2, TPG])
        scale_sum = buf("scale_sum", [P, TPG])
        coef2 = buf("coef2", [P, 2, TPG])
        work2 = buf("work2", [P, 2, TPG])
        halves = buf("halves", [P, TPG * 2 * EXPERTS])
        logits = buf("logits", [P, TPG, EXPERTS])
        gate_exp = buf("gate_exp", [P, TPG, EXPERTS])
        cand = buf("cand", [P, TPG, EXPERTS])
        gate_max = buf("gate_max", [P, TPG])
        gate_sum = buf("gate_sum", [P, TPG])
        wide_ps = ctx.enter_context(nc.psum_tensor("wide_ps", [P, 2, D], F32))
        turn_ps = ctx.enter_context(nc.psum_tensor("turn_ps", [P, 2, D], F32))
        ac_ps = ctx.enter_context(nc.psum_tensor("ac_ps", [P, 2, D], F32))
        bd_ps = ctx.enter_context(nc.psum_tensor("bd_ps", [P, 2, D], F32))

        x_loaded = sb["x_loaded"]
        names = """x_his x_los tok_mm h_ready stats_ready coef_work coef_ready u_ready resid_ready uT_mm w_his w_los
            qk_mm qk_ready bd_mm bd_ready bd_stored bd_shifted v_mm v_ready ac_mm sum_ready max_ready centred exped
            rowsum_ready inv_ready probs_ready probsT_ready pv_mm attn_his attn_los out_mm h2_ready stats2_ready
            coef2_work coef2_ready xf_ready xfT_mm xfT_ready xfT_los gate_mm logits_added logits_read gate_maxed gate_centred
            gate_exped gate_summed gate_p cand_a cand_b outd_ready""".split()
        s = {n: sem(n) for n in names}
        for name in ("xf_stored", "h2_stored", "outd_stored"):
            s[name] = sb[name]
        pe_passed, dve_passed, pool_passed, sp_passed = (sem(f"{n}_passed") for n in ("pe", "dve", "pool", "sp"))
        block = ctx.enter_context(nc.Block())
        ident = sb["ident"]

        def u_bank(c):
            return (turn_ps if c < 2 else ac_ps)[:, c % 2, 0:GTOK]

        def attn_bank(c):
            return (bd_ps if c < 2 else turn_ps)[:, c % 2, 0:GTOK]

        def xf_bank(c):
            return (bd_ps if c < 2 else ac_ps)[:, c % 2, 0:GTOK]

        @block.tensor
        def _(pe):
            def three(out, a_hi, a_lo, b_hi, b_lo, first, last):
                pe.matmul(out, a_hi, b_hi, start=first, stop=False)
                pe.matmul(out, a_hi, b_lo, start=False, stop=False)
                return pe.matmul(out, a_lo, b_hi, start=False, stop=last)

            def tokenize(g, first, tiles):
                for t in tiles:
                    pe.wait_ge(s["x_los"], TPG * g + t + 1)
                    if t == 2:
                        pe.wait_ge(s["h_ready"], TPG * g + 1)
                    elif not first:
                        pe.wait_ge(s["v_ready"], TPG * g + t - 1)
                    for c in range(KC):
                        cols = slice(c * P, (c + 1) * P)
                        last = three(wide_ps[:, (t + 1) % 2, :], x_hi[:, t, cols], x_lo[:, t, cols],
                                     sb["tok_hi"][:, c, :], sb["tok_lo"][:, c, :], c == 0, c == KC - 1)
                    last.then_inc(s["tok_mm"], 1)

            def turn_u(g, first):
                for c in range(DC):
                    if c == 0:
                        pe.wait_ge(s["u_ready"], TPG * g + TPG)
                    if c < 2 and not first:
                        pe.wait_ge(s["attn_los"], DC * (g - 1) + c + 3)
                    elif not first:
                        pe.wait_ge(s["sum_ready"], g)
                    for t in range(TPG):
                        last = pe.transpose(u_bank(c)[:, t * P:(t + 1) * P], u[:, t, c * P:(c + 1) * P], ident[:])
                    last.then_inc(s["uT_mm"], 1)

            def query_key(g, e):
                if e == 0:
                    pe.wait_ge(s["w_los"], DC * g + DC)
                if e >= 2:
                    pe.wait_ge(s["qk_ready"], 2 * DC * g + e - 1)
                for c in range(DC):
                    cols = slice(e * P, (e + 1) * P)
                    last = three(turn_ps[:, e % 2, 0:GTOK], sb["qkv_hi"][:, c, cols], sb["qkv_lo"][:, c, cols],
                                 wT_hi[:, c, :], wT_lo[:, c, :], c == 0, c == DC - 1)
                last.then_inc(s["qk_mm"], 1)

            def turn_xf(g, last_group):
                for c in range(DC):
                    if c == 0:
                        pe.wait_ge(s["xf_ready"], TPG * g + TPG)
                    if last_group and c < 2:
                        pe.wait_ge(s["attn_los"], DC * g + c + 1)
                    elif last_group:
                        pe.wait_ge(s["sum_ready"], g + 1)
                    elif c < 2:
                        pe.wait_ge(s["bd_ready"], g + 2)
                    else:
                        pe.wait_ge(s["w_los"], DC * (g + 1) + c + 1)
                    for t in range(TPG):
                        last = pe.transpose(xf_bank(c)[:, t * P:(t + 1) * P], xf[:, t, c * P:(c + 1) * P], ident[:])
                    last.then_inc(s["xfT_mm"], 1)

            def gate(g):
                pe.wait_ge(s["xfT_los"], DC * g + DC)
                pe.wait_ge(s["h2_ready"], TPG * g + TPG)
                for c in range(DC):
                    for half in (attnT_hi, attnT_lo):
                        last = pe.matmul(wide_ps[0:2 * EXPERTS, 1, 0:GTOK], sb["gate_w"][:, c, :, :].rearrange("p a e -> p (a e)"),
                                         half[:, c, :], start=c == 0 and half is attnT_hi, stop=c == DC - 1 and half is attnT_lo)
                last.then_inc(s["gate_mm"], 1)

            def position_scores(g, bank):
                if bank == 0:
                    hold_until(pe, [(s["qk_ready"], 2 * DC * g + DC),
                                    (s["attn_los"], DC * g)], pe_passed)
                for t in range(TPG):
                    for n in (2 * bank, 2 * bank + 1):
                        at = (t * 2 + n % 2) * 2 * IMAGES
                        for q in range(QUADS):
                            toks = slice(t * P + q * IMAGES, t * P + (q + 1) * IMAGES)
                            last = pe.matmul(bd_ps[q * IMAGES:(q + 1) * IMAGES, bank, at:at + 2 * IMAGES], qT[:, n, toks],
                                             sb["rk"][:, n, :, :].rearrange("p a r -> p (a r)"), start=True, stop=True)
                last.then_inc(s["bd_mm"], 1)

            def values(g, tiles):
                for t in tiles:
                    if t == 0:
                        wait(pe, s["h2_ready"], TPG * g)
                    elif t == 1:
                        wait(pe, s["logits_read"], g)
                    else:
                        pe.wait_ge(s["v_ready"], TPG * g + 1)
                    for c in range(DC):
                        cols = slice(t * P, (t + 1) * P)
                        last = three(wide_ps[:, t % 2, :], wT_hi[:, c, cols], wT_lo[:, c, cols],
                                     sb["qkv_hi"][:, c, 2 * D:], sb["qkv_lo"][:, c, 2 * D:], c == 0, c == DC - 1)
                    last.then_inc(s["v_mm"], 1)

            def content_scores(g, bank):
                if bank == 0:
                    hold_until(pe, [(s["qk_ready"], 2 * DC * g + 2 * DC),
                                    (s["xfT_los"], DC * g)], pe_passed)
                for t in range(TPG):
                    for n in (2 * bank, 2 * bank + 1):
                        at = (t * 2 + n % 2) * 2 * IMAGES
                        for q in range(QUADS):
                            toks = slice(t * P + q * IMAGES, t * P + (q + 1) * IMAGES)
                            last = pe.matmul(ac_ps[q * IMAGES:(q + 1) * IMAGES, bank, at:at + 2 * IMAGES]
                                             .rearrange("p (a j) -> p a j", a=2), qT[:, n, toks], kT[:, n, :, toks],
                                             start=True, stop=True)
                last.then_inc(s["ac_mm"], 1)

            def attend(g, first):
                pe.wait_ge(s["v_ready"], TPG * g + TPG)
                pe.wait_ge(s["probsT_ready"], QUADS * g + QUADS)
                for c in range(DC):
                    if c >= 2:
                        pe.wait_ge(s["qk_ready"], 2 * DC * g + c + 5)
                    elif first:
                        pe.wait_ge(s["bd_ready"], g + 1)
                    else:
                        pe.wait_ge(s["xfT_los"], DC * (g - 1) + c + 1)
                    for par in range(2):
                        head = 2 * c + par
                        for t in range(TPG):
                            blk = ((c // 2 * TPG + t) * 2 + c % 2) * 2 + par
                            last = pe.matmul(attn_bank(c)[par * DH:(par + 1) * DH, t * P:(t + 1) * P],
                                             v[:, t, head * DH:(head + 1) * DH], probsT[:, blk, :], start=True, stop=True)
                    last.then_inc(s["pv_mm"], 1)

            def project(g, last_group, tiles):
                if tiles[0] == 0:
                    pe.wait_ge(s["attn_los"], DC * g + DC)
                for t in tiles:
                    if t == 2:
                        pe.wait_ge(s["h2_ready"], TPG * g + 1)
                    elif last_group:
                        pe.wait_ge(s["v_ready"], TPG * g + TPG)
                    else:
                        pe.wait_ge(s["h_ready"], TPG * g + TPG + t + 2)
                    for c in range(DC):
                        cols = slice(t * P, (t + 1) * P)
                        last = three(wide_ps[:, t % 2, :], attnT_hi[:, c, cols], attnT_lo[:, c, cols],
                                     sb["out_hi"][:, c, :], sb["out_lo"][:, c, :], c == 0, c == DC - 1)
                    last.then_inc(s["out_mm"], 1)

            def step(i, first, last):
                for e in range(DC + 1):
                    query_key(i, e)
                position_scores(i, 0)
                query_key(i, DC + 1)
                position_scores(i, 1)
                query_key(i, DC + 2)
                query_key(i, DC + 3)
                if not first:
                    turn_xf(i - 1, False)
                values(i, (0,))
                content_scores(i, 0)
                if not first:
                    gate(i - 1)
                content_scores(i, 1)
                values(i, (1, 2))
                if not last:
                    tokenize(i + 1, False, (0, 1))
                attend(i, first)
                if not last:
                    tokenize(i + 1, False, (2,))
                project(i, last, (0, 1))
                if not last:
                    turn_u(i + 1, False)
                project(i, last, (2,))

            tokenize(0, True, (0, 1, 2))
            turn_u(0, True)
            step(0, True, False)
            with pe.Fori(1, GROUPS - 1) as i:
                step(i, False, False)
            step(GROUPS - 1, False, True)
            turn_xf(GROUPS - 1, True)
            gate(GROUPS - 1)

        @block.scalar
        def _(act):
            def patches_hi(g, t):
                act.wait_ge(x_loaded[t], 16 * g + 16)
                wait(act, s["tok_mm"], TPG * g - TPG + t + 1)
                act.activation(x_hi[:, t, :], x_raw[:, t, :], ACT.Copy).then_inc(s["x_his"], 1)

            def scale_u(g):
                for t in range(TPG):
                    if t != 1:
                        act.wait_ge(s["coef_ready"], 2 * g + (1 if t == 0 else 2))
                    act.activation(u[:, t, :], h[:, t, :], ACT.Identity, bias=shift[:, 1, t:t + 1],
                                   scale=scale[:, 1, t:t + 1]).then_inc(s["u_ready"], 1)

            def activations_hi(g):
                for c in range(DC):
                    act.wait_ge(s["uT_mm"], DC * g + c + 1)
                    act.activation(wT_hi[:, c, :], u_bank(c), ACT.Copy).then_inc(s["w_his"], 1)

            def query_key(g, e):
                act.wait_ge(s["qk_mm"], 2 * DC * g + e + 1)
                if e < DC:
                    last = act.activation(qT[:, e, :], turn_ps[:, e % 2, 0:GTOK], ACT.Identity, bias=sb["qkv_b"][:, e:e + 1])
                else:
                    for par in range(2):
                        rows = slice(par * DH, (par + 1) * DH)
                        last = act.activation(kT[rows, e - DC, par, :], turn_ps[rows, e % 2, 0:GTOK], ACT.Identity,
                                              bias=sb["qkv_b"][rows, e:e + 1])
                last.then_inc(s["qk_ready"], 1)

            def normalise(g, t):
                if t == 0:
                    act.wait_ge(s["coef2_ready"], g + 1)
                    wait(act, s["xf_stored"], 16 * g)
                    wait(act, s["outd_ready"], TPG * g)
                act.activation(xf[:, t, 0:D], resid[:, t, :], ACT.Identity, bias=coef2[:, 1, t:t + 1],
                               scale=coef2[:, 0, t:t + 1]).then_inc(s["xf_ready"], 1)

            def xf_turned(g):
                for c in range(DC):
                    act.wait_ge(s["xfT_mm"], DC * g + c + 1)
                    act.activation(attnT_hi[:, c, :], xf_bank(c), ACT.Copy).then_inc(s["xfT_ready"], 1)

            def gate_exponentials(g):
                act.wait_ge(s["gate_centred"], g + 1)
                act.activation(gate_exp[:], logits[:], ACT.Exp).then_inc(s["gate_exped"], 1)

            def values(g, tiles):
                for t in tiles:
                    act.wait_ge(s["v_mm"], TPG * g + t + 1)
                    act.activation(v[:, t, :], wide_ps[:, t % 2, :], ACT.Copy).then_inc(s["v_ready"], 1)

            def exponentials(g):
                act.wait_ge(s["centred"], g + 1)
                act.activation(scores[:], scores[:], ACT.Exp, scale=DH ** -0.5).then_inc(s["exped"], 1)

            def attention_hi(g, c):
                act.wait_ge(s["pv_mm"], DC * g + c + 1)
                act.activation(attnT_hi[:, c, :], attn_bank(c), ACT.Identity,
                               bias=sb["qkv_b"][:, 2 * DC + c:2 * DC + c + 1]).then_inc(s["attn_his"], 1)

            def step(i, first, last):
                for e in range(DC):
                    query_key(i, e)
                    if not first and e < TPG:
                        normalise(i - 1, e)
                for e in range(DC, 2 * DC):
                    if not last and e < DC + TPG:
                        patches_hi(i + 1, e - DC)
                    query_key(i, e)
                if not first:
                    xf_turned(i - 1)
                values(i, (0,))
                if not first:
                    gate_exponentials(i - 1)
                values(i, (1,))
                exponentials(i)
                values(i, (2,))
                for c in range(DC):
                    attention_hi(i, c)
                if not last:
                    scale_u(i + 1)
                    activations_hi(i + 1)

            for t in range(TPG):
                patches_hi(0, t)
            scale_u(0)
            activations_hi(0)
            step(0, True, False)
            with act.Fori(1, GROUPS - 1) as i:
                step(i, False, False)
            step(GROUPS - 1, False, True)
            for t in range(TPG):
                normalise(GROUPS - 1, t)
            xf_turned(GROUPS - 1)
            gate_exponentials(GROUPS - 1)

        @block.vector
        def _(dve):
            def patches_lo(g, t):
                dve.wait_ge(s["x_his"], TPG * g + t + 1)
                dve.tensor_sub(x_lo[:, t, :], x_raw[:, t, :], x_hi[:, t, :].bitcast(F32)).then_inc(s["x_los"], 1)

            def tokens(g, t):
                dve.wait_ge(s["tok_mm"], TPG * g + t + 1)
                if t == 0:
                    wait(dve, s["u_ready"], TPG * g)
                    wait(dve, s["resid_ready"], TPG * g)
                dve.tensor_add(h[:, t, :], wide_ps[:, (t + 1) % 2, :], sb["tok_b"][:]).then_inc(s["h_ready"], 1)
                dve.wait_ge(s["h_ready"], TPG * g + t + 1)
                dve.bn_stats(stats[:, t, :], h[:, t, :]).then_inc(s["stats_ready"], 1)
                if t >= 1:
                    hold_until(dve, [(s["stats_ready"], 2 * TPG * g + (2 if t == 1 else 5))], dve_passed)
                    for k in ((0, 1) if t == 1 else (2,)):
                        dve.bn_aggr(mv[:, k, :], stats[:, k, :]).then_inc(s["stats_ready"], 1)

            def activations_lo(g):
                for c in range(DC):
                    dve.wait_ge(s["w_his"], DC * g + c + 1)
                    dve.tensor_sub(wT_lo[:, c, :], u_bank(c), wT_hi[:, c, :].bitcast(F32)).then_inc(s["w_los"], 1)

            def xf_lo(g):
                for c in range(DC):
                    dve.wait_ge(s["xfT_ready"], DC * g + c + 1)
                    dve.tensor_sub(attnT_lo[:, c, :], xf_bank(c), attnT_hi[:, c, :].bitcast(F32)).then_inc(s["xfT_los"], 1)

            def gate_logits(g):
                dve.wait_ge(s["gate_mm"], g + 1)
                for q in range(QUADS):
                    rows = slice(q * IMAGES, (q + 1) * IMAGES)
                    ins = dve.transpose(halves[rows, :].rearrange("p (t b) -> p t b", t=TPG),
                                        wide_ps[0:2 * EXPERTS, 1, 0:GTOK].rearrange("p (t b) -> p t b", t=TPG)[:, :, rows])
                ins.then_inc(s["logits_read"], 1)
                dve.wait_ge(s["logits_read"], g + 1)
                sums = halves[:].rearrange("p (t a e) -> p t a e", t=TPG, a=2)
                dve.tensor_add(logits[:], sums[:, :, 0, :], sums[:, :, 1, :]).then_inc(s["logits_added"], 1)
                dve.wait_ge(s["logits_added"], 2 * g + 1)
                dve.tensor_add(logits[:], logits[:],
                               sb["gate_b"][:].unsqueeze(1).broadcast_to([P, TPG, EXPERTS])).then_inc(s["logits_added"], 1)
                dve.wait_ge(s["logits_added"], 2 * g + 2)
                dve.reduce_max(gate_max[:], logits[:], AX.X).then_inc(s["gate_maxed"], 1)
                dve.wait_ge(s["gate_maxed"], g + 1)
                dve.tensor_sub(logits[:], logits[:], gate_max[:].unsqueeze(2).broadcast_to([P, TPG, EXPERTS])).then_inc(s["gate_centred"], 1)

            def gate_choice(g):
                dve.wait_ge(s["gate_centred"], g + 1)
                dve.tensor_scalar(cand[:], logits[:], 0.0, float(EXPERTS), ALU.is_lt, ALU.mult).then_inc(s["cand_a"], 1)
                dve.wait_ge(s["cand_a"], g + 1)
                dve.tensor_add(cand[:], cand[:], sb["expert_ids"][:].unsqueeze(1).broadcast_to([P, TPG, EXPERTS])).then_inc(s["cand_b"], 1)
                dve.wait_ge(s["gate_exped"], g + 1)
                dve.reduce_sum(gate_sum[:], gate_exp[:], AX.X).then_inc(s["gate_summed"], 1)
                dve.wait_ge(s["cand_b"], g + 1)
                dve.tensor_reduce(sb["route"][:, bass.ds(TPG * g, TPG)], cand[:], axis=AX.X, op=ALU.min)
                dve.wait_ge(s["gate_summed"], g + 1)
                dve.reciprocal(xf[:, :, D:XROW], gate_sum[:].unsqueeze(2).broadcast_to([P, TPG, XROW - D])).then_inc(s["gate_p"], 1)

            def unrouted(g):
                dve.wait_ge(s["gate_p"], g + 1)
                dve.wait_ge(s["h2_stored"], 16 * g + 16)
                for t in range(TPG):
                    dve.scalar_tensor_tensor(out=resid[:, t, :], in0=xf[:, t, 0:D], scalar=xf[:, t, D:D + 1],
                                             in1=resid[:, t, :], op0=ALU.mult, op1=ALU.add).then_inc(s["outd_ready"], 1)

            def position_scores(g):
                wait(dve, s["sum_ready"], g)
                for bank in range(2):
                    dve.wait_ge(s["bd_mm"], 2 * g + bank + 1)
                    ins = dve.tensor_add(bd[:].rearrange("p r (b t h) -> p b t h r", b=2, t=TPG)[:, bank],
                                         bd_ps[:, bank, 0:GTOK].rearrange("p (t h r) -> p t h r", t=TPG, h=PAIRS),
                                         sb["bd_const"][:, 2 * bank:2 * bank + 2, :, :].rearrange("p n a r -> p (n a) r")
                                         .unsqueeze(1).broadcast_to([P, TPG, PAIRS, IMAGES]))
                ins.then_inc(s["bd_ready"], 1)

            def scores_max(g):
                dve.wait_ge(s["ac_mm"], 2 * g + 2)
                dve.wait_ge(s["bd_shifted"], 16 * QUADS * g + 16 * QUADS)
                wait(dve, s["probsT_ready"], QUADS * g)
                dve.tensor_add(scores[:].rearrange("p (a k) j -> p a k j", a=2),
                               ac_ps[:, :, 0:GTOK].rearrange("p a (k j) -> p a k j", j=IMAGES),
                               bd[:].rearrange("p j (a k) -> p a k j", a=2)).then_inc(s["sum_ready"], 1)
                dve.wait_ge(s["sum_ready"], g + 1)
                dve.reduce_max(row_max[:], scores[:], AX.X).then_inc(s["max_ready"], 1)

            def probabilities(g):
                dve.wait_ge(s["exped"], g + 1)
                dve.reduce_sum(row_sum[:], scores[:], AX.X).then_inc(s["rowsum_ready"], 1)
                dve.wait_ge(s["rowsum_ready"], g + 1)
                dve.reciprocal(row_inv[:], row_sum[:]).then_inc(s["inv_ready"], 1)
                dve.wait_ge(s["inv_ready"], g + 1)
                dve.tensor_mul(scores[:], scores[:], row_inv[:].unsqueeze(2).broadcast_to([P, BLOCKS, IMAGES])).then_inc(s["probs_ready"], 1)

            def turn_probs(g):
                dve.wait_ge(s["probs_ready"], g + 1)
                wait(dve, s["pv_mm"], DC * g)
                for q in range(QUADS):
                    rows = slice(q * IMAGES, (q + 1) * IMAGES)
                    dve.transpose(probsT[rows, :, rows], scores[rows, :, :]).then_inc(s["probsT_ready"], 1)

            def attention_lo(g):
                for c in range(DC):
                    dve.wait_ge(s["attn_his"], DC * g + c + 1)
                    dve.scalar_tensor_tensor(out=attnT_lo[:, c, :], in0=attn_bank(c),
                                             scalar=sb["qkv_b"][:, 2 * DC + c:2 * DC + c + 1],
                                             in1=attnT_hi[:, c, :].bitcast(F32), op0=ALU.add, op1=ALU.subtract
                                             ).then_inc(s["attn_los"], 1)

            def residual(g, tiles):
                for t in tiles:
                    dve.wait_ge(s["out_mm"], TPG * g + t + 1)
                    if t == 0:
                        dve.wait_ge(s["resid_ready"], TPG * g + TPG)
                    dve.tensor_add(resid[:, t, :], wide_ps[:, t % 2, :], resid[:, t, :]).then_inc(s["h2_ready"], 1)
                    dve.wait_ge(s["h2_ready"], TPG * g + t + 1)
                    dve.bn_stats(stats2[:, t, :], resid[:, t, :]).then_inc(s["stats2_ready"], 1)
                if tiles[-1] == TPG - 1:
                    hold_until(dve, [(s["stats2_ready"], 2 * TPG * g + TPG)], dve_passed)
                    for t in range(TPG):
                        dve.bn_aggr(mv2[:, t, :], stats2[:, t, :]).then_inc(s["stats2_ready"], 1)

            def step(i, first, last):
                if not last:
                    for t in range(TPG):
                        patches_lo(i + 1, t)
                position_scores(i)
                if not first:
                    xf_lo(i - 1)
                    gate_logits(i - 1)
                    gate_choice(i - 1)
                scores_max(i)
                if not first:
                    unrouted(i - 1)
                probabilities(i)
                turn_probs(i)
                if not last:
                    tokens(i + 1, 0)
                    tokens(i + 1, 1)
                attention_lo(i)
                if not last:
                    tokens(i + 1, 2)
                residual(i, (0, 1))
                if not last:
                    activations_lo(i + 1)
                residual(i, (2,))

            for t in range(TPG):
                patches_lo(0, t)
            for t in range(TPG):
                tokens(0, t)
            activations_lo(0)
            step(0, True, False)
            with dve.Fori(1, GROUPS - 1) as i:
                step(i, False, False)
            step(GROUPS - 1, False, True)
            xf_lo(GROUPS - 1)
            gate_logits(GROUPS - 1)
            gate_choice(GROUPS - 1)
            unrouted(GROUPS - 1)

        @block.gpsimd
        def _(pool):
            def coefficients(g):
                for part, t in enumerate((slice(0, 2), slice(2, 3))):
                    done, n = 10 * g + 5 * part, t.stop - t.start
                    hold_until(pool, [(s["stats_ready"], 2 * TPG * g + 2 * t.stop)], pool_passed)
                    pool.tensor_scalar(work[:, 0, t], mv[:, t, 1], EPS, None, ALU.add).then_inc(s["coef_work"], 1)
                    pool.tensor_scalar(work[:, 1, t], mv[:, t, 1], 1.0 + EPS, EPS * EPS, ALU.mult, ALU.add).then_inc(s["coef_work"], 1)
                    pool.tensor_scalar(minus_mean[:, t], mv[:, t, 0], -1.0, None, ALU.mult).then_inc(s["coef_work"], 1)
                    pool.wait_ge(s["coef_work"], done + 3)
                    pool.tensor_tensor(scale[:, :, t], work[:, :, t], sb["half"][:, t].unsqueeze(1).broadcast_to([P, 2, n]),
                                       ALU.pow).then_inc(s["coef_work"], 1)
                    pool.wait_ge(s["coef_work"], done + 4)
                    pool.tensor_tensor(shift[:, :, t], scale[:, :, t], minus_mean[:, t].unsqueeze(1).broadcast_to([P, 2, n]),
                                       ALU.mult).then_inc(s["coef_ready"], 1)
                    pool.tensor_scalar(scale_sum[:, t], scale[:, 0, t], 1.0, None, ALU.add).then_inc(s["coef_work"], 1)

            def coefficients2(g):
                hold_until(pool, [(s["stats2_ready"], 2 * TPG * g + 2 * TPG)], pool_passed)
                pool.tensor_scalar(work2[:, 0, :], mv2[:, :, 1], EPS, None, ALU.add).then_inc(s["coef2_work"], 1)
                pool.tensor_scalar(work2[:, 1, :], mv2[:, :, 0], -1.0, None, ALU.mult).then_inc(s["coef2_work"], 1)
                pool.wait_ge(s["coef2_work"], 3 * g + 2)
                pool.tensor_tensor(coef2[:, 0, :], work2[:, 0, :], sb["half"][:], ALU.pow).then_inc(s["coef2_work"], 1)
                pool.wait_ge(s["coef2_work"], 3 * g + 3)
                pool.tensor_tensor(coef2[:, 1, :], work2[:, 1, :], coef2[:, 0, :], ALU.mult).then_inc(s["coef2_ready"], 1)

            def residual(g):
                hold_until(pool, [(s["coef_work"], 10 * g + 10), (s["outd_stored"], 16 * g)], pool_passed)
                for t in range(TPG):
                    pool.tensor_scalar(resid[:, t, :], h[:, t, :], scale_sum[:, t:t + 1], shift[:, 0, t:t + 1],
                                       ALU.mult, ALU.add).then_inc(s["resid_ready"], 1)

            def centre(g):
                pool.wait_ge(s["max_ready"], g + 1)
                pool.tensor_sub(scores[:], scores[:], row_max[:].unsqueeze(2).broadcast_to([P, BLOCKS, IMAGES])).then_inc(s["centred"], 1)

            def step(i, first, last):
                if not first:
                    coefficients2(i - 1)
                centre(i)
                residual(i)
                if not last:
                    coefficients(i + 1)

            coefficients(0)
            step(0, True, False)
            with pool.Fori(1, GROUPS - 1) as i:
                step(i, False, False)
            step(GROUPS - 1, False, True)
            coefficients2(GROUPS - 1)

        @block.sync
        def _(sp):
            shift_in = io["shift"].rearrange("(p n) -> p n", p=P)[:, BLOCKS:SHIFT_ROW]
            shift_out = io["shift"].rearrange("(q n) -> q n", q=QUADS)[:, IMAGES * BLOCKS:]

            def load_patches(g, t):
                if not isinstance(g, int) or g > 0:
                    hold_until(sp, [(s["x_los"], TPG * g - TPG + t + 1)], sp_passed)
                sp.dma_start(x_raw[:, t, :], io["patches"][bass.ds(TPG * g + t, 1), :, :].rearrange("a p n -> p (a n)")
                             ).then_inc(x_loaded[t], 16)

            def store_normed(g):
                hold_until(sp, [(s["gate_p"], g + 1)], sp_passed)
                sp.dma_start(io["rows"][bass.ds(GTOK * g, GTOK), 0:XROW].rearrange("(t p) n -> p t n", p=P),
                             xf[:]).then_inc(s["xf_stored"], 16)

            def store_unrouted(g):
                hold_until(sp, [(s["outd_ready"], TPG * g + TPG)], sp_passed)
                sp.dma_start(io["out"][bass.ds(GTOK * g, GTOK), :].rearrange("(t p) n -> p t n", p=P),
                             resid[:]).then_inc(s["outd_stored"], 16)

            def store_h2(g):
                hold_until(sp, [(s["stats2_ready"], 2 * TPG * g + TPG)], sp_passed)
                sp.dma_start(io["rows"][bass.ds(GTOK * g, GTOK), XROW:ROW].rearrange("(t p) n -> p t n", p=P),
                             resid[:]).then_inc(s["h2_stored"], 16)

            def shift(g):
                hold_until(sp, [(s["bd_ready"], g + 1)], sp_passed)
                sp.dma_start(shift_in, bd[:].rearrange("p r k -> p (r k)")).then_inc(s["bd_stored"], 16)
                hold_until(sp, [(s["bd_stored"], 16 * g + 16)], sp_passed)
                for q in range(QUADS):
                    sp.dma_start(bd[q * IMAGES:(q + 1) * IMAGES, :, :].rearrange("p j k -> p (j k)"),
                                 shift_out[q].rearrange("(i n) -> i n", i=IMAGES)).then_inc(s["bd_shifted"], 16)

            def step(i, first, load):
                if not first:
                    store_h2(i - 1)
                shift(i)
                if load:
                    for t in range(TPG):
                        load_patches(i + 2, t)
                if not first:
                    store_normed(i - 1)
                    store_unrouted(i - 1)

            for t in range(TPG):
                load_patches(1, t)
            step(0, True, True)
            with sp.Fori(1, GROUPS - 2) as i:
                step(i, False, True)
            step(GROUPS - 2, False, False)
            step(GROUPS - 1, False, False)
            store_h2(GROUPS - 1)
            store_normed(GROUPS - 1)
            store_unrouted(GROUPS - 1)


def place(nc, io, sb):
    ctx = ExitStack()
    with ctx:
        def buf(name, shape, dt=F32):
            return ctx.enter_context(nc.sbuf_tensor(name, shape, dt))

        def sem(name):
            return ctx.enter_context(nc.semaphore(name))

        chosen = buf("chosen", [P, EXPERTS, TILES])
        resets = buf("resets", [P, EXPERTS, TILES])
        counts = buf("counts", [P, EXPERTS, TILES])
        totals = buf("totals", [P, EXPERTS])
        before = buf("before", [P, EXPERTS])
        earlier = buf("earlier", [P, P])
        slot_ids = buf("slot_ids", [P, SLOT_TILES])
        lane_ids = buf("lane_ids", [P, P])
        row_no = buf("row_no", [P, TILES])
        pos = buf("pos", [P, TILES])
        pos_i = buf("pos_i", [P, TILES], I32)
        hi_i = buf("hi_i", [P, TILES], I32)
        lane_i = buf("lane_i", [P, TILES], I32)
        over = buf("over", [P, TILES])
        minus_lane = buf("minus_lane", [P, TILES])
        one = buf("one", [P, 1])
        slot_tile = buf("slot_tile", [P, TILES])
        slot_lane = buf("slot_lane", [P, TILES])
        RING = 16
        lane_gap = buf("lane_gap", [P, RING, P])
        lane_hot = buf("lane_hot", [P, RING, P])
        slot_hot = buf("slot_hot", [P, RING, SLOT_TILES])
        empty = buf("empty", [P, SLOT_TILES])
        index_f = buf("index_f", [P, SLOT_TILES])
        base_ps = ctx.enter_context(nc.psum_tensor("base_ps", [P, D], F32))
        table_ps = ctx.enter_context(nc.psum_tensor("table_ps", [P, D], F32))
        consts_in, chain, total_ready, base_mm, table_mm, resets_set, one_set, rows_set, keys_ready = (
            sem(n) for n in "consts_in chain total_ready base_mm table_mm resets_set one_set rows_set keys_ready".split())
        hot_by_dve, hot_by_act, gap_squared = (
            sem(n) for n in "hot_by_dve hot_by_act gap_squared".split())
        w_raw, w_hi, w_lo = sb["w_raw"], sb["w_hi"], sb["w_lo"]
        block = ctx.enter_context(nc.Block())

        @block.sync
        def _(sp):
            for dst, src in ((earlier, "earlier"), (slot_ids, "slot_ids"), (lane_ids, "lane_ids"),
                             (row_no, "row_no")):
                sp.dma_start(dst[:], io[src]).then_inc(consts_in, 16)
            for half in range(2):
                sp.dma_start(w_raw[:, half, :, :], io["expert_wT"][half, :, :, :]).then_inc(sb["w_in"][half], 16)
                sp.dma_start(sb["bias"][:, half, :], io["expert_b"][half:half + 1, :].broadcast_to([P, D])).then_inc(sb["w_in"][half], 16)
            sp.wait_ge(sb["xf_stored"], 16 * GROUPS)
            sp.wait_ge(sb["h2_stored"], 16 * GROUPS)
            sp.wait_ge(sb["outd_stored"], 16 * GROUPS)

        @block.scalar
        def _(act):
            for half in range(2):
                act.wait_ge(sb["w_in"][half], 32)
                for c in range(DC):
                    act.activation(w_hi[:, half, c, :], w_raw[:, half, c, :], ACT.Copy).then_inc(sb["w_his"], 1)

            def lane_hot_odd(i, r):
                if not isinstance(i, int):
                    act.wait_ge(table_mm, RING * (i - 1) + r + 1)
                act.activation(lane_gap[:, r, :], lane_ids[:], ACT.Square, bias=minus_lane[:, bass.ds(RING * i + r, 1)]
                               ).then_inc(gap_squared, 1)
                act.wait_ge(gap_squared, RING // 2 * i + r // 2 + 1)
                act.activation(lane_hot[:, r, :], lane_gap[:, r, :], ACT.Relu, bias=one[:], scale=-1.0).then_inc(hot_by_act, 1)

            act.wait_ge(keys_ready, 1)
            act.wait_ge(one_set, 1)
            act.wait_ge(consts_in, 64)
            for r in range(1, RING, 2):
                lane_hot_odd(0, r)
            with act.Fori(1, TILES // RING) as i:
                for r in range(1, RING, 2):
                    lane_hot_odd(i, r)

        @block.gpsimd
        def _(pool):
            pool.memset(resets[:], 1.0).then_inc(resets_set, 1)
            pool.wait_ge(resets_set, 1)
            pool.memset(resets[:, :, 0:1], 0.0).then_inc(resets_set, 1)
            pool.memset(one[:], 1.0).then_inc(one_set, 1)
            pool.memset(sb["gathered_rows"][:], 0.0).then_inc(rows_set, 1)
            for half in range(2):
                for c in range(DC):
                    pool.wait_ge(sb["w_his"], DC * half + c + 1)
                    pool.tensor_sub(w_lo[:, half, c, :], w_raw[:, half, c, :], w_hi[:, half, c, :].bitcast(F32)).then_inc(sb["w_los"], 1)

        @block.tensor
        def _(pe):
            pe.wait_ge(total_ready, 1)
            pe.wait_ge(consts_in, 64)
            pe.matmul(base_ps[:, 0:EXPERTS], earlier[:], totals[:], start=True, stop=True).then_inc(base_mm, 1)

            def add(i, r, first, last):
                pe.wait_ge(hot_by_dve, RING * i + r + 1)
                if r % 2:
                    pe.wait_ge(hot_by_act, RING // 2 * i + r // 2 + 1)
                pe.matmul(table_ps[:, 0:SLOT_TILES], lane_hot[:, r, :], slot_hot[:, r, :], start=first, stop=last
                          ).then_inc(table_mm, 1)

            for r in range(RING):
                add(0, r, r == 0, False)
            with pe.Fori(1, TILES // RING - 1) as i:
                for r in range(RING):
                    add(i, r, False, False)
            for r in range(RING):
                add(TILES // RING - 1, r, False, r == RING - 1)

        @block.vector
        def _(dve):
            done = [0]

            def link(ins):
                done[0] += 1
                ins.then_inc(chain, 1)
                dve.wait_ge(chain, done[0])

            link(dve.tensor_tensor(chosen[:], sb["route"][:].unsqueeze(1).broadcast_to([P, EXPERTS, TILES]),
                                   sb["expert_ids"][:].unsqueeze(2).broadcast_to([P, EXPERTS, TILES]), ALU.is_equal))
            dve.wait_ge(resets_set, 2)
            link(dve.tensor_tensor_scan(counts[:].rearrange("p e t -> p (e t)"), resets[:].rearrange("p e t -> p (e t)"),
                                        chosen[:].rearrange("p e t -> p (e t)"), 0.0, ALU.mult, ALU.add))
            dve.tensor_copy(totals[:].unsqueeze(2), counts[:, :, TILES - 1:TILES]).then_inc(total_ready, 1)
            dve.wait_ge(base_mm, 1)
            link(dve.tensor_copy(before[:], base_ps[:, 0:EXPERTS]))
            link(dve.tensor_add(counts[:], counts[:], before[:].unsqueeze(2).broadcast_to([P, EXPERTS, TILES])))
            link(dve.tensor_mul(counts[:], counts[:], chosen[:]))
            link(dve.reduce_sum(pos[:], counts[:].rearrange("p e t -> p t e"), AX.X))
            link(dve.tensor_scalar(pos[:], pos[:], -1.0, None, ALU.add))
            link(dve.tensor_copy(pos_i[:], pos[:]))
            link(dve.tensor_scalar(hi_i[:], pos_i[:], 7, None, ALU.arith_shift_right))
            link(dve.tensor_scalar(lane_i[:], pos_i[:], P - 1, None, ALU.bitwise_and))
            link(dve.tensor_copy(slot_tile[:], hi_i[:]))
            link(dve.tensor_copy(slot_lane[:], lane_i[:]))
            link(dve.scalar_tensor_tensor(out=slot_tile[:], in0=sb["route"][:], scalar=float(TPE), in1=slot_tile[:],
                                          op0=ALU.mult, op1=ALU.add))
            link(dve.tensor_scalar(over[:], pos[:], float(CAPACITY), 4096.0, ALU.is_ge, ALU.mult))
            link(dve.tensor_add(slot_tile[:], slot_tile[:], over[:]))
            dve.tensor_scalar(minus_lane[:], slot_lane[:], -1.0, None, ALU.mult).then_inc(keys_ready, 1)
            dve.wait_ge(consts_in, 64)

            def one_hot(i, r):
                if not isinstance(i, int):
                    dve.wait_ge(table_mm, RING * (i - 1) + r + 1)
                col = bass.ds(RING * i + r, 1)
                if r % 2 == 0:
                    dve.tensor_scalar(lane_hot[:, r, :], lane_ids[:], slot_lane[:, col], None, ALU.is_equal)
                dve.tensor_scalar(slot_hot[:, r, :], slot_ids[:], slot_tile[:, col], row_no[:, col],
                                  ALU.is_equal, ALU.mult).then_inc(hot_by_dve, 1)

            for r in range(RING):
                one_hot(0, r)
            with dve.Fori(1, TILES // RING) as i:
                for r in range(RING):
                    one_hot(i, r)
            dve.wait_ge(table_mm, TILES)
            link(dve.tensor_scalar(empty[:], table_ps[:, 0:SLOT_TILES], 0.0, float(TOKENS + 1), ALU.is_equal, ALU.mult))
            link(dve.scalar_tensor_tensor(out=index_f[:], in0=table_ps[:, 0:SLOT_TILES], scalar=-1.0, in1=empty[:],
                                          op0=ALU.add, op1=ALU.add))
            link(dve.tensor_copy(sb["index"][:], index_f[:]))


def experts(nc, io, sb):
    ctx = ExitStack()
    with ctx:
        def buf(name, shape, dt=F32):
            return ctx.enter_context(nc.sbuf_tensor(name, shape, dt))

        def sem(name):
            return ctx.enter_context(nc.semaphore(name))

        RING = ROW_SLOTS
        AHEAD = RING // 2
        PAIR = 2 * TPE
        STEPS = EXPERTS // 2
        w_raw, w_hi, w_lo, bias = sb["w_raw"], sb["w_hi"], sb["w_lo"], sb["bias"]
        rows = sb["gathered_rows"]
        now = buf("now", [P, RING], I32)
        biased = buf("biased", [P, 2, D])
        xT_hi = buf("xT_hi", [P, 2, DC * P], F32R)
        xT_lo = buf("xT_lo", [P, 2, DC * P], F32R)
        turn = ctx.enter_context(nc.psum_tensor("turn", [P, 2, D], F32))
        prod = ctx.enter_context(nc.psum_tensor("prod", [P, 2, D], F32))
        w_in, w_his, w_los = sb["w_in"], sb["w_his"], sb["w_los"]
        sp_passed = sem("sp_passed2")
        gathered = [sem(f"gathered{r}") for r in range(RING)]
        scattered = [sem(f"scattered{r}") for r in range(RING)]
        index_now, passed, xT_mm, xT_his, xT_los, y_mm, y_biased, result_ready = (
            sem(n) for n in "index_now pool_passed2 xT_mm xT_his xT_los y_mm y_biased result_ready".split())
        block = ctx.enter_context(nc.Block())
        ident = sb["ident"]

        @block.sync
        def _(sp):
            def load(i, half):
                hold_until(sp, [(w_los, DC * (2 * i + half - 1))], sp_passed)
                sp.dma_start(w_raw[:, half, :, :], io["expert_wT"][bass.ds(2 * i + half, 1), :, :, :]
                             .rearrange("a p c n -> p (a c) n")).then_inc(w_in[half], 16)
                hold_until(sp, [(y_biased, PAIR * i - PAIR + TPE * (half + 1))], sp_passed)
                sp.dma_start(bias[:, half, :], io["expert_b"][bass.ds(2 * i + half, 1), :].broadcast_to([P, D])
                             ).then_inc(w_in[half], 16)

            with sp.Fori(1, STEPS) as i:
                load(i, 0)
                load(i, 1)

        @block.scalar
        def _(act):
            def split(i, half, c):
                if c == 0:
                    act.wait_ge(w_in[half], 32 * i + 32)
                    wait(act, y_mm, PAIR * i - PAIR + TPE * (half + 1))
                act.activation(w_hi[:, half, c, :], w_raw[:, half, c, :], ACT.Copy).then_inc(w_his, 1)

            def rows_hi(i, k):
                act.wait_ge(xT_mm, PAIR * i + k + 1)
                act.activation(xT_hi[:, k % 2, :], turn[:, k % 2, :], ACT.Copy).then_inc(xT_his, 1)

            def step(i, first, last):
                for k in range(PAIR):
                    rows_hi(i, k)
                    if 2 <= k < 2 + DC and not first:
                        split(i, 1, k - 2)
                    elif TPE + 2 <= k < TPE + 2 + DC and not last:
                        split(i + 1, 0, k - TPE - 2)

            step(0, True, False)
            with act.Fori(1, STEPS - 1) as i:
                step(i, False, False)
            step(STEPS - 1, False, True)

        @block.vector
        def _(dve):
            def split(i, half, c):
                dve.wait_ge(w_his, DC * (2 * i + half) + c + 1)
                dve.tensor_sub(w_lo[:, half, c, :], w_raw[:, half, c, :], w_hi[:, half, c, :].bitcast(F32)).then_inc(w_los, 1)

            def rows_lo(i, k):
                dve.wait_ge(xT_his, PAIR * i + k + 1)
                dve.tensor_sub(xT_lo[:, k % 2, :], turn[:, k % 2, :], xT_hi[:, k % 2, :].bitcast(F32)).then_inc(xT_los, 1)

            def finish(i, k):
                n, row = PAIR * i + k, rows[:, k % RING, :]
                dve.wait_ge(y_mm, n + 1)
                dve.tensor_add(biased[:, k % 2, :], prod[:, k % 2, :], bias[:, k // TPE, :]).then_inc(y_biased, 1)
                dve.wait_ge(y_biased, n + 1)
                dve.scalar_tensor_tensor(out=row[:, XROW:ROW], in0=biased[:, k % 2, :], scalar=row[:, D:D + 1],
                                         in1=row[:, XROW:ROW], op0=ALU.mult, op1=ALU.add).then_inc(result_ready, 1)

            def step(i, first, last):
                for k in range(PAIR):
                    if k + 1 < PAIR:
                        rows_lo(i, k + 1)
                    elif not last:
                        rows_lo(i + 1, 0)
                    finish(i, k)
                    if 2 <= k < 2 + DC and not first:
                        split(i, 1, k - 2)
                    elif TPE + 2 <= k < TPE + 2 + DC and not last:
                        split(i + 1, 0, k - TPE - 2)

            rows_lo(0, 0)
            step(0, True, False)
            with dve.Fori(1, STEPS - 1) as i:
                step(i, False, False)
            step(STEPS - 1, False, True)

        @block.tensor
        def _(pe):
            def turn_rows(i, k):
                pe.wait_ge(gathered[k % RING], 16 * (2 * i + k // RING) + 16)
                wait(pe, xT_los, PAIR * i + k - 1)
                for c in range(DC):
                    last = pe.transpose(turn[:, k % 2, c * P:(c + 1) * P], rows[:, k % RING, c * P:(c + 1) * P], ident[:])
                last.then_inc(xT_mm, 1)

            def multiply(i, k):
                half = k // TPE
                if k % TPE == 0:
                    pe.wait_ge(w_los, DC * (2 * i + half) + DC)
                pe.wait_ge(xT_los, PAIR * i + k + 1)
                wait(pe, y_biased, PAIR * i + k - 1)
                for c in range(DC):
                    hi, lo = (x[:, k % 2, c * P:(c + 1) * P] for x in (xT_hi, xT_lo))
                    pe.matmul(prod[:, k % 2, :], hi, w_hi[:, half, c, :], start=c == 0, stop=False)
                    pe.matmul(prod[:, k % 2, :], hi, w_lo[:, half, c, :], start=False, stop=False)
                    last = pe.matmul(prod[:, k % 2, :], lo, w_hi[:, half, c, :], start=False, stop=c == DC - 1)
                last.then_inc(y_mm, 1)

            def step(i, last):
                for k in range(PAIR):
                    if k + 1 < PAIR:
                        turn_rows(i, k + 1)
                    elif not last:
                        turn_rows(i + 1, 0)
                    multiply(i, k)

            turn_rows(0, 0)
            step(0, False)
            with pe.Fori(1, STEPS - 1) as i:
                step(i, False)
            step(STEPS - 1, True)

        @block.gpsimd
        def _(pool):
            def gather(i, k):
                slot = k % RING
                hold_until(pool, [(scattered[slot], 16 * (2 * i + k // RING))], passed)
                pool.tensor_copy(now[:, slot:slot + 1], sb["index"][:, bass.ds(PAIR * i + k, 1)]).then_inc(index_now, 1)
                hold_until(pool, [(index_now, PAIR * i + k + 1)], passed)
                pool.indirect_dma_start(rows[:, slot, :], None, io["rows"],
                                        bass.IndirectOffsetOnAxis(ap=now[:, slot:slot + 1], axis=0),
                                        bounds_check=TOKENS - 1, oob_is_err=False).then_inc(gathered[slot], 16)

            def scatter(i, k):
                slot = k % RING
                hold_until(pool, [(result_ready, PAIR * i + k + 1)], passed)
                pool.indirect_dma_start(io["out"], bass.IndirectOffsetOnAxis(ap=now[:, slot:slot + 1], axis=0),
                                        rows[:, slot, XROW:ROW], None, bounds_check=TOKENS - 1, oob_is_err=False
                                        ).then_inc(scattered[slot], 16)

            def step(i, last):
                for k in range(PAIR):
                    if k + AHEAD < PAIR or not last:
                        gather(i, k + AHEAD)
                    scatter(i, k)

            for k in range(AHEAD):
                gather(0, k)
            step(0, False)
            with pool.Fori(1, STEPS - 1) as i:
                step(i, False)
            step(STEPS - 1, True)
            for slot in range(RING):
                pool.wait_ge(scattered[slot], 16 * 2 * STEPS)


def build(nc, io):
    with ExitStack() as whole:
        sb = {}

        def hold(ctx, name, shape, dt=F32):
            sb[name] = ctx.enter_context(nc.sbuf_tensor(f"{name}_sb", shape, dt))

        hold(whole, "ident", [P, P])
        hold(whole, "expert_ids", [P, EXPERTS])
        hold(whole, "route", [P, TILES])
        hold(whole, "index", [P, SLOT_TILES], I32)
        hold(whole, "resid", [P, TPG, D])
        hold(whole, "xf", [P, TPG, XROW])
        for name in ("xf_stored", "h2_stored", "outd_stored"):
            sb[name] = whole.enter_context(nc.semaphore(name))
        with ExitStack() as first:
            for name, cols in (("tok", D * KC), ("qkv", 3 * D * DC), ("out", D * DC)):
                chunks = KC if name == "tok" else DC
                hold(first, f"{name}_hi", [P, chunks, cols // chunks], F32R)
                hold(first, f"{name}_lo", [P, chunks, cols // chunks], F32R)
            hold(first, "rk", [P, PAIRS, 2, IMAGES])
            hold(first, "bd_const", [P, PAIRS, 2, IMAGES])
            hold(first, "kT", [P, PAIRS, 2, GTOK])
            hold(first, "qkv_b", [P, 3 * DC])
            hold(first, "tok_b", [P, D])
            hold(first, "gate_w", [P, DC, 2, EXPERTS], F32R)
            hold(first, "gate_b", [P, EXPERTS])
            hold(first, "half", [P, TPG])
            hold(first, "probsT", [P, BLOCKS, P])
            hold(first, "x_raw", [P, TPG, KC * P])
            sb["x_loaded"] = [first.enter_context(nc.semaphore(f"x_loaded{t}")) for t in range(TPG)]
            prepare(nc, io, sb)
            tower(nc, io, sb)
        for name, dt in (("w_raw", F32), ("w_hi", F32R), ("w_lo", F32R)):
            hold(whole, name, [P, 2, DC, D], dt)
        hold(whole, "bias", [P, 2, D])
        hold(whole, "gathered_rows", [P, ROW_SLOTS, ROW])
        sb["w_in"] = [whole.enter_context(nc.semaphore(f"w_in{half}")) for half in range(2)]
        sb["w_his"], sb["w_los"] = (whole.enter_context(nc.semaphore(name)) for name in ("expert_his", "expert_los"))
        place(nc, io, sb)
        experts(nc, io, sb)


def constants():
    f32 = np.float32
    lane = np.arange(P)
    image, quad = lane % IMAGES, lane // IMAGES
    order = image * QUADS + quad
    place_in = np.arange(IMAGES - 1, -1, -1, dtype=f32)
    inv = (1.0 / np.power(f32(10000.0), np.arange(0, D, 2, dtype=f32) / f32(D))).astype(f32)
    angle = place_in[:, None] * inv[None, :]
    sinusoid = np.concatenate([np.sin(angle), np.cos(angle)], axis=-1).astype(f32)
    spread = lambda row, dt: np.ascontiguousarray(np.broadcast_to(row, (P, len(row)))).astype(dt)
    return {
        "ident": np.eye(P, dtype=f32),
        "sinusoid": np.ascontiguousarray(sinusoid.T.reshape(DC, P, IMAGES).transpose(1, 0, 2)),
        "expert_ids": spread(np.arange(EXPERTS), f32),
        "earlier": (order[:, None] < order[None, :]).astype(f32),
        "slot_ids": spread(np.arange(SLOT_TILES), f32),
        "lane_ids": spread(lane, f32),
        "row_no": (np.arange(TILES)[None, :] * P + lane[:, None] + 1).astype(f32),
    }


def kernel(**inputs):
    import concourse.bacc as bacc
    from concourse.bass_utils import run_bass_kernel_spmd

    a = {k: np.asarray(v) for k, v in inputs.items()}
    n = SIDE // PATCH
    x = a["x"].reshape(IMAGES, CHANNELS, n, PATCH, n, PATCH).transpose(2, 4, 1, 3, 5, 0)
    x = x.reshape(QUADS, TILES, KC, P, IMAGES).transpose(1, 3, 2, 0, 4).reshape(TILES, P, KC * P)

    def chunked(w):
        out, inn = w.shape
        return np.ascontiguousarray(w.T.reshape(inn // P, P, out).transpose(1, 0, 2))

    def spread(row):
        return np.ascontiguousarray(np.broadcast_to(row, (P, row.size)))

    def columns(row):
        return np.ascontiguousarray(row.reshape(-1, P).T)

    arrays = {
        "patches": np.ascontiguousarray(x),
        "tok_wT": chunked(a["L0_tok_w"]),
        "tok_b": spread(a["L0_tok_b"]),
        "qkv_wT": chunked(a["L0_attn_Wqkv"]),
        "wr_wT": chunked(a["L0_attn_Wr"]),
        "out_wT": chunked(a["L0_attn_Wo"]),
        "gamma": columns(a["L0_attn_ln_gamma"]),
        "beta": columns(a["L0_attn_ln_beta"]),
        "r_w_bias": columns(a["L0_attn_r_w_bias"]),
        "r_r_bias": columns(a["L0_attn_r_r_bias"]),
        "gate_wT": chunked(a["L0_ffn_switch_w"]),
        "gate_b": spread(a["L0_ffn_switch_b"]),
        "expert_wT": np.ascontiguousarray(a["L0_ffn_expert_w"].transpose(0, 2, 1).reshape(EXPERTS, DC, P, D).transpose(0, 2, 1, 3)),
        "expert_b": a["L0_ffn_expert_b"],
        **constants(),
    }
    nc = bacc.Bacc("TRN2", target_bir_lowering=False, num_devices=1)
    io = {k: nc.dram_tensor(f"in_{k}", v.shape, mybir.dt.from_np(v.dtype), kind="ExternalInput").ap() for k, v in arrays.items()}
    io["out"] = nc.dram_tensor("out_rows", (TOKENS, D), F32, kind="ExternalOutput").ap()
    io["rows"] = nc.dram_tensor("token_rows", (TOKENS, ROW), F32, kind="Internal").ap()
    io["shift"] = nc.dram_tensor("shift_scratch", (P * SHIFT_ROW,), F32, kind="Internal").ap()
    build(nc, io)
    done = run_bass_kernel_spmd(nc, [{f"in_{k}": v for k, v in arrays.items()}], core_ids=[0])
    out = np.asarray(done.results[0]["out_rows"])
    return out.reshape(TILES, QUADS, IMAGES, D).transpose(2, 1, 0, 3).reshape(IMAGES, POSITIONS, D)
```
